# Optimizing a Trainium2 kernel written in Bass

```python
import numpy as np
import jax
import jax.numpy as jnp

def _softmax(x, axis=-1):
    return jax.nn.softmax(x, axis=axis)

def _gelu(x):
    return jax.nn.gelu(x, approximate=True)

def _silu(x):
    return jax.nn.silu(x)

def _sigmoid(x):
    return jax.nn.sigmoid(x)

def _layernorm(x, axis=-1, eps=1e-05):
    m = jnp.mean(x, axis=axis, keepdims=True)
    v = jnp.var(x, axis=axis, keepdims=True)
    return (x - m) / jnp.sqrt(v + eps)

def _scatter_add(tgt, idx, src, axis=0):
    return tgt.at[idx].add(src)

def _segment_sum(src, seg, n):
    return jax.ops.segment_sum(src, seg, n)
kernel_name = 'mk_adj_ffn_d4_adj_r2_fe7a71'

def setup_inputs(seed: int=0):
    np.random.seed(seed)
    _w = jnp.asarray

    def _rec_inputs():
        import jax
        import jax.numpy as jnp
        _gk = jax.random.key(seed)
        x = 0.0002279 + 0.9999 * jax.random.normal(jax.random.fold_in(_gk, 1), (2048, 128), jnp.float32)
        _a = jax.random.bernoulli(jax.random.fold_in(_gk, 2), 0.0078125, (2048, 2048))
        _a = jnp.logical_or(_a, jnp.swapaxes(_a, -1, -2))
        _a = jnp.logical_or(_a, jnp.eye(2048, dtype=bool))
        adj = _a.astype(jnp.int32)
        return (x, adj)
    x, adj = _rec_inputs()

    def _L0_gnn_setup():
        import jax, jax.numpy as jnp
        import numpy as np
        IN_FEATURES = 128
        OUT_FEATURES = 128
        HEADS = 4
        F_HEAD = OUT_FEATURES // HEADS
        N = 2048
        key = jax.random.key(seed)
        k_adj, k_in, k_w, k_phi = jax.random.split(key, 4)
        adj = jax.random.randint(k_adj, (N, N), 0, 2, dtype=jnp.int32)
        x = jax.random.normal(k_in, (N, IN_FEATURES), dtype=jnp.float32)
        lim_w = float(np.sqrt(6.0 / (IN_FEATURES + F_HEAD)))
        weights = jax.random.uniform(k_w, (HEADS, IN_FEATURES, F_HEAD), jnp.float32, -lim_w, lim_w)
        biases = jnp.zeros((HEADS, F_HEAD), jnp.float32)
        lim_p = float(np.sqrt(6.0 / (2 * F_HEAD + 1)))
        phis = jax.random.uniform(k_phi, (HEADS, 2 * F_HEAD, 1), jnp.float32, -lim_p, lim_p)
        return {'adj': adj, 'input': x, 'weights': weights, 'biases': biases, 'phis': phis}
    _L0_gnn_all = _L0_gnn_setup()
    _L0_gnn_in = {k: v for k, v in _L0_gnn_all.items() if k in ('weights', 'biases', 'phis')}
    del _L0_gnn_all

    def _L0_ffn_setup():
        import jax, jax.numpy as jnp
        import numpy as np
        B, T, IN_DIM = (64, 128, 128)
        HID, OUT_DIM = (256, 128)
        N_LAYERS, N_EXPERTS, N_SHARED = (2, 16, 1)
        key = jax.random.key(seed)
        ks = jax.random.split(key, 10)
        s = 0.02
        x = jax.random.normal(ks[0], (B, T, IN_DIM), dtype=jnp.float32)
        route_id = jax.random.randint(ks[1], (B,), 0, N_EXPERTS)
        Wi = jax.random.normal(ks[2], (HID, IN_DIM), dtype=jnp.float32) * s
        bi = jnp.zeros((HID,), dtype=jnp.float32)
        Wr = jax.random.normal(ks[3], (N_LAYERS, N_EXPERTS, HID, HID), dtype=jnp.float32) * s
        br = jax.random.normal(ks[4], (N_LAYERS, N_EXPERTS, HID), dtype=jnp.float32) * s
        Ws = jax.random.normal(ks[5], (N_LAYERS, N_SHARED, HID, HID), dtype=jnp.float32) * s
        bs = jax.random.normal(ks[6], (N_LAYERS, N_SHARED, HID), dtype=jnp.float32) * s
        Wo = jax.random.normal(ks[7], (OUT_DIM, HID), dtype=jnp.float32) * s
        bo = jnp.zeros((OUT_DIM,), dtype=jnp.float32)
        return {'x': x, 'route_id': route_id, 'Wi': Wi, 'bi': bi, 'Wr': Wr, 'br': br, 'Ws': Ws, 'bs': bs, 'Wo': Wo, 'bo': bo}
    _L0_ffn_all = _L0_ffn_setup()
    _L0_ffn_in = {k: v for k, v in _L0_ffn_all.items() if k in ('route_id', 'Wi', 'bi', 'Wr', 'br', 'Ws', 'bs', 'Wo', 'bo')}
    del _L0_ffn_all

    def _L1_gnn_setup():
        import jax, jax.numpy as jnp
        import numpy as np
        NEG = -9000000000000000.0
        key = jax.random.key(seed)
        k1, k2, k3, k4 = jax.random.split(key, 4)
        N, F_IN, F_OUT = (4096, 128, 128)
        h = jax.random.normal(k1, (N, F_IN), dtype=jnp.float32)
        adj = jax.random.randint(k2, (N, N), 0, 2, dtype=jnp.int32)
        W = jax.random.normal(k3, (F_IN, F_OUT), dtype=jnp.float32) * (1.0 / np.sqrt(F_IN))
        a = jax.random.normal(k4, (2 * F_OUT,), dtype=jnp.float32) * (1.0 / np.sqrt(2 * F_OUT))
        return {'h': h, 'adj': adj, 'W': W, 'a': a}
    _L1_gnn_all = _L1_gnn_setup()
    _L1_gnn_in = {k: v for k, v in _L1_gnn_all.items() if k in ('W', 'a')}
    del _L1_gnn_all

    def _L1_ffn_setup():
        import jax, jax.numpy as jnp
        import numpy as np
        B, S, D, E, H, K = (4, 2048, 128, 8, 256, 2)
        key = jax.random.key(seed)
        ks = jax.random.split(key, 6)
        x = jax.random.normal(ks[0], (B, S, D), jnp.float32)
        Wg = jax.random.normal(ks[1], (D, E), jnp.float32) * 0.02
        bg = jnp.zeros((E,), jnp.float32)
        W1 = jax.random.normal(ks[2], (E, D, H), jnp.float32) * 0.02
        b1 = jnp.zeros((E, H), jnp.float32)
        W2 = jax.random.normal(ks[3], (E, H, D), jnp.float32) * 0.02
        b2 = jnp.zeros((E, D), jnp.float32)
        return {'x': x, 'Wg': Wg, 'bg': bg, 'W1': W1, 'b1': b1, 'W2': W2, 'b2': b2}
    _L1_ffn_all = _L1_ffn_setup()
    _L1_ffn_in = {k: v for k, v in _L1_ffn_all.items() if k in ('Wg', 'bg', 'W1', 'b1', 'W2', 'b2')}
    del _L1_ffn_all

    def _L2_gnn_setup():
        import jax, jax.numpy as jnp
        import numpy as np
        N, IN_DIM, OUT_DIM = (4096, 128, 128)
        key = jax.random.key(seed)
        k1, k2, k3, k4 = jax.random.split(key, 4)
        x = jax.random.normal(k1, (N, IN_DIM), dtype=jnp.float32)
        adj = jax.random.randint(k2, (N, N), 0, 2, dtype=jnp.int32)
        W = jax.random.normal(k3, (OUT_DIM, IN_DIM), dtype=jnp.float32) / np.sqrt(IN_DIM)
        a = jax.random.normal(k4, (2 * OUT_DIM,), dtype=jnp.float32) / np.sqrt(2 * OUT_DIM)
        return {'x': x, 'adj': adj, 'W': W, 'a': a}
    _L2_gnn_all = _L2_gnn_setup()
    _L2_gnn_in = {k: v for k, v in _L2_gnn_all.items() if k in ('W', 'a')}
    del _L2_gnn_all

    def _L2_ffn_setup():
        import jax, jax.numpy as jnp
        import numpy as np
        D_IN, D_HID, D_OUT = (128, 256, 128)
        N_EXPERTS, TOP_K = (64, 2)
        B, S = (8, 2048)
        key = jax.random.key(seed)
        ks = jax.random.split(key, 8)
        scale_in = 1.0 / np.sqrt(D_IN)
        scale_hid = 1.0 / np.sqrt(D_HID)
        return {'x': jax.random.normal(ks[0], (B, S, D_IN), dtype=jnp.float32), 'Wr': jax.random.uniform(ks[1], (D_IN, N_EXPERTS), jnp.float32, -scale_in, scale_in), 'br': jax.random.uniform(ks[2], (N_EXPERTS,), jnp.float32, -scale_in, scale_in), 'W1': jax.random.uniform(ks[3], (N_EXPERTS, D_IN, D_HID), jnp.float32, -scale_in, scale_in), 'b1': jax.random.uniform(ks[4], (N_EXPERTS, D_HID), jnp.float32, -scale_in, scale_in), 'W2': jax.random.uniform(ks[5], (N_EXPERTS, D_HID, D_OUT), jnp.float32, -scale_hid, scale_hid), 'b2': jax.random.uniform(ks[6], (N_EXPERTS, D_OUT), jnp.float32, -scale_hid, scale_hid)}
    _L2_ffn_all = _L2_ffn_setup()
    _L2_ffn_in = {k: v for k, v in _L2_ffn_all.items() if k in ('Wr', 'br', 'W1', 'b1', 'W2', 'b2')}
    del _L2_ffn_all

    def _L3_gnn_setup():
        import jax, jax.numpy as jnp
        import numpy as np
        N = 4096
        D_IN = 128
        D_OUT = 128
        NEG_INF = -9000000000000000.0
        key = jax.random.key(seed)
        k1, k2, k3, k4 = jax.random.split(key, 4)
        node_features = jax.random.normal(k1, (N, D_IN), dtype=jnp.float32)
        adjacency_matrix = jax.random.randint(k2, (N, N), 0, 2, dtype=jnp.int32)
        W = jax.random.normal(k3, (D_OUT, D_IN), dtype=jnp.float32) / np.sqrt(D_IN)
        b_W = jnp.zeros((D_OUT,), dtype=jnp.float32)
        a_vec = jax.random.normal(k4, (2 * D_OUT,), dtype=jnp.float32) / np.sqrt(2 * D_OUT)
        b_a = jnp.zeros((1,), dtype=jnp.float32)
        return {'node_features': node_features, 'adjacency_matrix': adjacency_matrix, 'W': W, 'b_W': b_W, 'a_vec': a_vec, 'b_a': b_a}
    _L3_gnn_all = _L3_gnn_setup()
    _L3_gnn_in = {k: v for k, v in _L3_gnn_all.items() if k in ('W', 'b_W', 'a_vec', 'b_a')}
    del _L3_gnn_all

    def _L3_ffn_setup():
        import jax, jax.numpy as jnp
        import numpy as np
        NUM_EXPERTS = 8
        TOP_K = 2
        B, S, D = (8, 4096, 128)

        def _moe(tokens, router_w, w1, b1, w2, b2):
            N = tokens.shape[0]
            E = router_w.shape[0]
            logits = tokens.astype(jnp.float32) @ router_w.astype(jnp.float32).T
            probs = jax.nn.softmax(logits, axis=-1)
            rw, re = jax.lax.top_k(probs, TOP_K)
            if TOP_K > 1:
                rw = rw / jnp.maximum(rw.sum(-1, keepdims=True), 1e-12)
            rw = rw.astype(tokens.dtype)
            combine = jnp.zeros((N, E), tokens.dtype).at[jnp.arange(N)[:, None], re].set(rw)
            out = tokens
            for e in range(E):
                h = jax.nn.gelu(tokens @ w1[e] + b1[e], approximate=False)
                y = h @ w2[e] + b2[e]
                out = out + combine[:, e:e + 1] * y
            return out
        key = jax.random.key(seed)
        ks = jax.random.split(key, 4)
        scale = 1.0 / np.sqrt(D).astype(np.float32)
        return {'input_embeddings': jax.random.normal(ks[0], (B, S, D), jnp.float32), 'router_w': jax.random.normal(ks[1], (NUM_EXPERTS, D), jnp.float32) * scale, 'w1': jax.random.normal(ks[2], (NUM_EXPERTS, D, D), jnp.float32) * scale, 'b1': jnp.zeros((NUM_EXPERTS, D), jnp.float32), 'w2': jax.random.normal(ks[3], (NUM_EXPERTS, D, D), jnp.float32) * scale, 'b2': jnp.zeros((NUM_EXPERTS, D), jnp.float32)}
    _L3_ffn_all = _L3_ffn_setup()
    _L3_ffn_in = {k: v for k, v in _L3_ffn_all.items() if k in ('router_w', 'w1', 'b1', 'w2', 'b2')}
    del _L3_ffn_all
    return {'x': x, 'adj': adj, 'L0_gnn_weights': _L0_gnn_in['weights'], 'L0_gnn_biases': _L0_gnn_in['biases'], 'L0_gnn_phis': _L0_gnn_in['phis'], 'L0_ffn_route_id': _L0_ffn_in['route_id'], 'L0_ffn_Wi': _L0_ffn_in['Wi'], 'L0_ffn_bi': _L0_ffn_in['bi'], 'L0_ffn_Wr': _L0_ffn_in['Wr'], 'L0_ffn_br': _L0_ffn_in['br'], 'L0_ffn_Ws': _L0_ffn_in['Ws'], 'L0_ffn_bs': _L0_ffn_in['bs'], 'L0_ffn_Wo': _L0_ffn_in['Wo'], 'L0_ffn_bo': _L0_ffn_in['bo'], 'L1_gnn_W': _L1_gnn_in['W'], 'L1_gnn_a': _L1_gnn_in['a'], 'L1_ffn_Wg': _L1_ffn_in['Wg'], 'L1_ffn_bg': _L1_ffn_in['bg'], 'L1_ffn_W1': _L1_ffn_in['W1'], 'L1_ffn_b1': _L1_ffn_in['b1'], 'L1_ffn_W2': _L1_ffn_in['W2'], 'L1_ffn_b2': _L1_ffn_in['b2'], 'L2_gnn_W': _L2_gnn_in['W'], 'L2_gnn_a': _L2_gnn_in['a'], 'L2_ffn_Wr': _L2_ffn_in['Wr'], 'L2_ffn_br': _L2_ffn_in['br'], 'L2_ffn_W1': _L2_ffn_in['W1'], 'L2_ffn_b1': _L2_ffn_in['b1'], 'L2_ffn_W2': _L2_ffn_in['W2'], 'L2_ffn_b2': _L2_ffn_in['b2'], 'L3_gnn_W': _L3_gnn_in['W'], 'L3_gnn_b_W': _L3_gnn_in['b_W'], 'L3_gnn_a_vec': _L3_gnn_in['a_vec'], 'L3_gnn_b_a': _L3_gnn_in['b_a'], 'L3_ffn_router_w': _L3_ffn_in['router_w'], 'L3_ffn_w1': _L3_ffn_in['w1'], 'L3_ffn_b1': _L3_ffn_in['b1'], 'L3_ffn_w2': _L3_ffn_in['w2'], 'L3_ffn_b2': _L3_ffn_in['b2']}

def reference(x, adj, L0_gnn_weights, L0_gnn_biases, L0_gnn_phis, L0_ffn_route_id, L0_ffn_Wi, L0_ffn_bi, L0_ffn_Wr, L0_ffn_br, L0_ffn_Ws, L0_ffn_bs, L0_ffn_Wo, L0_ffn_bo, L1_gnn_W, L1_gnn_a, L1_ffn_Wg, L1_ffn_bg, L1_ffn_W1, L1_ffn_b1, L1_ffn_W2, L1_ffn_b2, L2_gnn_W, L2_gnn_a, L2_ffn_Wr, L2_ffn_br, L2_ffn_W1, L2_ffn_b1, L2_ffn_W2, L2_ffn_b2, L3_gnn_W, L3_gnn_b_W, L3_gnn_a_vec, L3_gnn_b_a, L3_ffn_router_w, L3_ffn_w1, L3_ffn_b1, L3_ffn_w2, L3_ffn_b2):
    import jax
    import jax.numpy as jnp

    def _L0_gnn_ref(adj, input, weights, biases, phis):
        import jax, jax.numpy as jnp
        import numpy as np
        IN_FEATURES = 128
        OUT_FEATURES = 128
        HEADS = 4
        F_HEAD = OUT_FEATURES // HEADS
        N = 2048
        x_prime = jnp.einsum('nd,hdf->hnf', input, weights) + biases[:, None, :]
        phi_src = phis[:, :F_HEAD, 0]
        phi_dst = phis[:, F_HEAD:, 0]
        s_src = jnp.einsum('hnf,hf->hn', x_prime, phi_src)
        s_dst = jnp.einsum('hnf,hf->hn', x_prime, phi_dst)
        S = s_src[:, :, None] + s_dst[:, None, :]
        S = jax.nn.leaky_relu(S, negative_slope=0.2)
        mask = adj.astype(jnp.float32) + jnp.eye(N, dtype=jnp.float32) > 0
        S_masked = jnp.where(mask[None, :, :], S, jnp.float32(-1000000000.0))
        attention = jax.nn.softmax(S_masked, axis=-1)
        h = jnp.einsum('hij,hjf->hif', attention, x_prime)
        h_concat = jnp.transpose(h, (1, 0, 2)).reshape(N, HEADS * F_HEAD)
        return h_concat

    def _L0_ffn_ref(x, route_id, Wi, bi, Wr, br, Ws, bs, Wo, bo):
        import jax, jax.numpy as jnp
        import numpy as np
        B, T, IN_DIM = (64, 128, 128)
        HID, OUT_DIM = (256, 128)
        N_LAYERS, N_EXPERTS, N_SHARED = (2, 16, 1)
        flat = x.reshape(-1, x.shape[-1])
        n_tok = flat.shape[0]
        route = jnp.repeat(route_id, n_tok // route_id.shape[0])
        h = jax.nn.relu(flat @ Wi.T + bi)
        n_layers, n_experts = (Wr.shape[0], Wr.shape[1])
        for l in range(n_layers):
            shared = (jnp.einsum('nd,shd->snh', h, Ws[l]) + bs[l][:, None, :]).mean(axis=0)
            routed = jnp.zeros_like(h)
            for e in range(n_experts):
                ye = h @ Wr[l, e].T + br[l, e]
                routed = routed + jnp.where((route == e)[:, None], ye, 0.0)
            h = jax.nn.relu(shared + routed + h)
        out = h @ Wo.T + bo
        return out.reshape(*x.shape[:-1], out.shape[-1])

    def _L1_gnn_ref(h, adj, W, a):
        import jax, jax.numpy as jnp
        import numpy as np
        NEG = -9000000000000000.0
        Wh = h @ W
        F_OUT = Wh.shape[1]
        a1, a2 = (a[:F_OUT], a[F_OUT:])
        s1 = Wh @ a1
        s2 = Wh @ a2
        e = jax.nn.leaky_relu(s1[:, None] + s2[None, :], negative_slope=0.2)
        e = jnp.where(adj > 0, e, NEG)
        attention = jax.nn.softmax(e, axis=-1)
        return attention @ Wh

    def _L1_ffn_ref(x, Wg, bg, W1, b1, W2, b2):
        import jax, jax.numpy as jnp
        import numpy as np
        B, S, D, E, H, K = (4, 2048, 128, 8, 256, 2)
        Bv, Sv, Dv = x.shape
        gate_scores = x @ Wg + bg
        _, idx = jax.lax.top_k(gate_scores, K)
        mask = jax.nn.one_hot(idx, E, dtype=x.dtype).sum(axis=-2)
        xf = x.reshape(-1, Dv)
        mf = mask.reshape(-1, E)
        h = jax.nn.gelu(jnp.einsum('td,edh->teh', xf, W1) + b1[None], approximate=False)
        y = jnp.einsum('teh,ehd->ted', h, W2) + b2[None]
        out = jnp.einsum('ted,te->td', y, mf)
        return out.reshape(Bv, Sv, Dv)

    def _L2_gnn_ref(x, adj, W, a):
        import jax, jax.numpy as jnp
        import numpy as np
        N, IN_DIM, OUT_DIM = (4096, 128, 128)
        h = jnp.einsum('ni,oi->no', x, W)
        out_dim = W.shape[0]
        a1, a2 = (a[:out_dim], a[out_dim:])
        e_i = h @ a1
        e_j = h @ a2
        e = e_i[:, None] + e_j[None, :]
        e = jnp.where(adj == 0, -jnp.inf, e)
        attn_weights = jax.nn.softmax(e, axis=1)
        h_new = attn_weights @ h
        return h_new

    def _L2_ffn_ref(x, Wr, br, W1, b1, W2, b2):
        import jax, jax.numpy as jnp
        import numpy as np
        D_IN, D_HID, D_OUT = (128, 256, 128)
        N_EXPERTS, TOP_K = (64, 2)
        B, S = (8, 2048)
        Bx, Sx, D = x.shape
        xf = x.reshape(-1, D)
        T = xf.shape[0]
        E = Wr.shape[1]
        logits = xf @ Wr + br
        topk_logits, topk_idx = jax.lax.top_k(logits, TOP_K)
        gates = jax.nn.softmax(topk_logits, axis=1)
        combine = jnp.zeros((T, E), xf.dtype).at[jnp.arange(T)[:, None], topk_idx].add(gates)
        out = jnp.zeros((T, W2.shape[-1]), xf.dtype)
        for e in range(E):
            h = jax.nn.relu(xf @ W1[e] + b1[e])
            y = h @ W2[e] + b2[e]
            out = out + combine[:, e:e + 1] * y
        return out.reshape(Bx, Sx, -1)

    def _L3_gnn_ref(node_features, adjacency_matrix, W, b_W, a_vec, b_a):
        import jax, jax.numpy as jnp
        import numpy as np
        N = 4096
        D_IN = 128
        D_OUT = 128
        NEG_INF = -9000000000000000.0
        h = node_features @ W.T + b_W
        a1, a2 = (a_vec[:D_OUT], a_vec[D_OUT:])
        e = (h @ a1)[:, None] + (h @ a2)[None, :] + b_a[0]
        e = jnp.where(e > 0, e, 0.2 * e)
        scores = jnp.where(adjacency_matrix > 0, e, jnp.float32(NEG_INF))
        attention = jax.nn.softmax(scores, axis=1)
        h_prime = attention @ h
        return h_prime

    def _L3_ffn_ref(input_embeddings, router_w, w1, b1, w2, b2):
        import jax, jax.numpy as jnp
        import numpy as np
        NUM_EXPERTS = 8
        TOP_K = 2
        B, S, D = (8, 4096, 128)

        def _moe(tokens, router_w, w1, b1, w2, b2):
            N = tokens.shape[0]
            E = router_w.shape[0]
            logits = tokens.astype(jnp.float32) @ router_w.astype(jnp.float32).T
            probs = jax.nn.softmax(logits, axis=-1)
            rw, re = jax.lax.top_k(probs, TOP_K)
            if TOP_K > 1:
                rw = rw / jnp.maximum(rw.sum(-1, keepdims=True), 1e-12)
            rw = rw.astype(tokens.dtype)
            combine = jnp.zeros((N, E), tokens.dtype).at[jnp.arange(N)[:, None], re].set(rw)
            out = tokens
            for e in range(E):
                h = jax.nn.gelu(tokens @ w1[e] + b1[e], approximate=False)
                y = h @ w2[e] + b2[e]
                out = out + combine[:, e:e + 1] * y
            return out
        b, s, d = input_embeddings.shape
        tokens = input_embeddings.reshape(b * s, d)
        return _moe(tokens, router_w, w1, b1, w2, b2).reshape(b, s, d)
    x = x + _L0_gnn_ref(adj, _layernorm(x, axis=-1), L0_gnn_weights, L0_gnn_biases, L0_gnn_phis)
    x = x + _L0_ffn_ref(_layernorm(x, axis=-1)[None], L0_ffn_route_id, L0_ffn_Wi, L0_ffn_bi, L0_ffn_Wr, L0_ffn_br, L0_ffn_Ws, L0_ffn_bs, L0_ffn_Wo, L0_ffn_bo)[0]
    x = x + _L1_gnn_ref(_layernorm(x, axis=-1), adj, L1_gnn_W, L1_gnn_a)
    x = x + _L1_ffn_ref(_layernorm(x, axis=-1)[None], L1_ffn_Wg, L1_ffn_bg, L1_ffn_W1, L1_ffn_b1, L1_ffn_W2, L1_ffn_b2)[0]
    x = x + _L2_gnn_ref(_layernorm(x, axis=-1), adj, L2_gnn_W, L2_gnn_a)
    x = x + _L2_ffn_ref(_layernorm(x, axis=-1)[None], L2_ffn_Wr, L2_ffn_br, L2_ffn_W1, L2_ffn_b1, L2_ffn_W2, L2_ffn_b2)[0]
    x = x + _L3_gnn_ref(_layernorm(x, axis=-1), adj, L3_gnn_W, L3_gnn_b_W, L3_gnn_a_vec, L3_gnn_b_a)
    x = x + _L3_ffn_ref(_layernorm(x, axis=-1)[None], L3_ffn_router_w, L3_ffn_w1, L3_ffn_b1, L3_ffn_w2, L3_ffn_b2)[0]
    return x

_drawn_inputs = setup_inputs


def setup_inputs(seed=0):
    import zlib

    import numpy as np

    out = dict(_drawn_inputs(seed))
    spreads = {'L0_gnn_biases': (0.0, 0.1),
     'L0_ffn_bi': (0.0, 0.1),
     'L0_ffn_bo': (0.0, 0.1),
     'L1_ffn_bg': (0.0, 0.1),
     'L1_ffn_b1': (0.0, 0.1),
     'L1_ffn_b2': (0.0, 0.1),
     'L3_gnn_b_W': (0.0, 0.1),
     'L3_ffn_b1': (0.0, 0.434),
     'L3_ffn_b2': (0.0, 0.301)}
    factors = {'L0_ffn_br': 2.887, 'L2_ffn_b1': 3.425}
    for name, (base, spread) in spreads.items():
        noise = np.random.default_rng([zlib.crc32(name.encode()), seed]).standard_normal(out[name].shape)
        drawn = base * np.exp(spread * noise) if base else spread * noise
        out[name] = jnp.asarray(drawn.astype(out[name].dtype))
    for name, factor in factors.items():
        out[name] = (out[name] * factor).astype(out[name].dtype)
    return out
```

```python
from contextlib import ExitStack

import concourse.bass as bass
from concourse import mybir

ALU = mybir.AluOpType
ACT = mybir.ActivationFunctionType
F32 = mybir.dt.float32
BF16 = mybir.dt.bfloat16
I32 = mybir.dt.int32
U32 = mybir.dt.uint32
AX_X = mybir.AxisListType.X
RMAX = bass.bass_isa.ReduceOp.max

P = 128
N = 2048
D = 128
T = N // P
CH = 512
NC = N // CH
TPC = CH // P
EPS = 1e-5
SLOPE = 0.2
REST = 1.0 - SLOPE
HEADROOM = 40.0

HEADS = 4
FH = D // HEADS
VW = 2 * (FH + 1)
PARTS = 3
HB = N // 2
TH = HB // P

HID = 256
KH = HID // P
LAYERS = 2
E0 = 16
GROUPS = 64
GT = N // GROUPS
GPC = CH // GT


PHASES = ["g0", "f0", "g1", "f1", "g2", "f2", "g3", "f3"]
EXPERTS = {"f1": (8, 2), "f2": (64, 2), "f3": (8, 1)}


def stage_counts():
    counts = {}
    for stage, n in dict(stats=T, veps=1, rstd=1, xn=T, xnt_ps=T, xnt=NC).items():
        counts[stage] = {p: n for p in PHASES}
    for stage, n in dict(max=1, gmax=1).items():
        counts[stage] = {p: n for p in ("g0", "g1", "g2", "g3")}
    for stage, n in dict(wa_ps=1, wa=2, ab_ps=1, wx=2, shift=1, uv=3, xv=2, q_used=T, acct=NC, out_ps=T).items():
        counts[stage] = {p: n for p in ("g1", "g2", "g3")}
    for stage, n in dict(abc_ps=NC, gbc=NC, negc=1, rel=T, q=T).items():
        counts[stage] = {p: n for p in ("g1", "g3")}
    for stage, n in dict(lg_ps=1, top=T, cmb=1, cmbt_ps=T, cmbt=NC, bias_ps=T, acc=1, iota=1).items():
        counts[stage] = {p: n for p in EXPERTS}
    for stage, n in dict(gap=1, gap_exp=1).items():
        counts[stage] = {p: n for p in ("f2", "f3")}
    for stage, n in dict(w0=24, w1=24, y_ps=NC, y=NC).items():
        counts[stage] = {p: n * e for p, (e, _) in EXPERTS.items()}
    for stage in ("h_ps", "ht"):
        counts[stage] = {p: NC * e * k for p, (e, k) in EXPERTS.items()}
    return counts


COUNTS = stage_counts()


def build(nc, dram, out):
    ctx = ExitStack()
    with ctx:
        sems = {}

        def S(name):
            stage = name.split(".")[-1]
            if "." in name and name.split(".")[0] in COUNTS.get(stage, {}):
                name = stage
            if name not in sems:
                sems[name] = ctx.enter_context(nc.semaphore(name.replace(".", "_")))
            return sems[name]

        def sb(name, shape, dt=F32):
            return ctx.enter_context(nc.sbuf_tensor(name, shape, dt))

        def at(name, value):
            phase, stage = name.split(".") if "." in name else (name, "")
            base = sum(n for p, n in COUNTS.get(stage, {}).items() if PHASES.index(p) < PHASES.index(phase))
            return S(name), base + value

        def wait(eng, sem, value):
            if not isinstance(value, int) or value > 0:
                eng.wait_ge(*at(sem, value))

        X = sb("x_residual", [P, T, D])
        XN = sb("x_normed", [P, T, D])
        XNT = sb("x_normed_t", [P, N])
        MASK = sb("mask_t", [P, T, N], BF16)
        DIAG = sb("mask_diagonal", [P, T, P], BF16)
        IDENT = sb("identity", [P, P])
        IDB = sb("identity_bf16", [P, P], BF16)
        STATS = sb("ln_stats", [P, T, 6])
        MV = sb("ln_mean_var", [P, T, 2])
        RSTD = sb("ln_rstd", [P, T])
        VEPS = sb("ln_var_eps", [P, T])
        MHALF = sb("minus_half", [P, T])
        SMALL = sb("small", [P, 64])
        MAXES = sb("maxes", [P, 8])
        GMAX = sb("global_maxes", [P, 8])
        AB = sb("scores_ab", [P, T, 8])
        AU = sb("scores_u", [P, T, 8])
        AV = sb("scores_v", [P, T, 8])
        WA = sb("wa", [P, 8])
        WA1B = sb("wa1_broadcast", [P, 4, P])
        RDEN = sb("rden", [P, T])

        w0cat = sb("w0_cat", [P, D])
        w0t = sb("w0_t", [FH, HEADS, P])
        phi0 = sb("phi0", [FH, HEADS, 2])
        bias0 = sb("bias0", [P, D])
        bias0t = sb("bias0_t", [FH, HEADS])
        bias0tb = sb("bias0_t_broadcast", [FH, HEADS, P])
        gw = {}
        for g in (1, 2, 3):
            gw[g] = dict(
                io=sb(f"g{g}_w_in_out", [P, D]), oi=sb(f"g{g}_w_out_in", [P, D]),
                last=sb(f"g{g}_w_last_row", [P, D]), a=sb(f"g{g}_a", [P, 2]),
                wx=sb(f"g{g}_projection", [P, D + 1]))
        b3row = sb("g3_b_row", [P, D])
        b3col = sb("g3_b_col", [P, 1])
        b3cb = sb("g3_b_col_broadcast", [P, P])
        ba3 = sb("g3_b_a", [P, 1])

        ARENA_WORDS = 25088
        arena = sb("arena", [P, ARENA_WORDS])
        top = [0]

        def region(words, at=None):
            a = top[0] if at is None else at
            assert a + words <= ARENA_WORDS, (a, words)
            if at is None:
                top[0] = a + words
            return arena[:, a:a + words]

        PS = ctx.enter_context(nc.psum_tensor("ps", [P, 8, CH], F32))

        ABC = region(HEADS * N).rearrange("p (h n) -> p h n", h=HEADS)
        VH = region(T * HEADS * PARTS * VW // 2).bitcast(BF16).rearrange(
            "p (t h s w) -> p t h s w", t=T, h=HEADS, s=PARTS)
        vf_at = top[0]
        VF = region(T * HEADS * VW).rearrange("p (t h w) -> p t h w", t=T, h=HEADS)
        M1R = 4
        M1 = region(M1R * HB // 2, at=vf_at).bitcast(BF16).rearrange("p (r n) -> p r n", r=M1R)
        hx_at = top[0]
        RM = region(T * HEADS * (FH + 1)).rearrange("p (t h w) -> p t h w", t=T, h=HEADS)
        HX = region(T * D, at=hx_at).rearrange("p (t d) -> p t d", t=T)
        t1_at = top[0]
        T1 = region(2 * TH * PARTS * VW).rearrange("p (b t s w) -> p b t s w", b=2, t=TH, s=PARTS)
        RS = region(TH * VW).rearrange("p (t w) -> p t w", t=TH)
        RD = region(TH * (FH + 1)).rearrange("p (t w) -> p t w", t=TH)
        RE = region(TH * (FH + 1)).rearrange("p (t w) -> p t w", t=TH)
        ADJ = region(2 * N, at=t1_at).bitcast(I32).rearrange("p (b n) -> p b n", b=2)

        top[0] = 0
        GBC = region(N)
        REL = region(2 * N).rearrange("p (b n) -> p b n", b=2)
        QT = region(2 * N).rearrange("p (b n) -> p b n", b=2)
        XV = region(T * D).rearrange("p (t d) -> p t d", t=T)
        XS = region(T * PARTS * D // 2).bitcast(BF16).rearrange("p (t s d) -> p t s d", t=T, s=PARTS)
        ACCT = region(N)

        top[0] = 0
        WR = region(E0 * KH * HID).rearrange("p (e k o) -> p e k o", e=E0, k=KH)
        WST = region(4 * KH * HID).rearrange("p (b k o) -> p b k o", b=4, k=KH)
        WS = region(LAYERS * KH * HID).rearrange("p (l k o) -> p l k o", l=LAYERS, k=KH)
        HT0 = region(KH * N).rearrange("p (k n) -> p k n", k=KH)
        WI = region(HID)
        WO = region(KH * D).rearrange("p (k o) -> p k o", k=KH)
        BRS = region(LAYERS * HID).rearrange("p (l o) -> p l o", l=LAYERS)
        ONEH = region(N)
        HSUM = region(2 * CH).rearrange("p (b n) -> p b n", b=2)
        BI = region(KH)
        BO = region(D)
        ROUTE = region(GROUPS).bitcast(I32)
        ROUTEF = region(GROUPS)
        IOTAF = region(1)
        IOTAI = region(1).bitcast(I32)

        def moe_arena(E, H):
            top[0] = 0
            k = H // P
            return dict(
                k=k,
                w1=region(2 * H).rearrange("p (b h) -> p b h", b=2),
                w2=region(2 * k * D).rearrange("p (b k d) -> p b k d", b=2, k=k),
                b1=region(2 * k).rearrange("p (b k) -> p b k", b=2),
                ht=region(2 * k * CH).rearrange("p (b k n) -> p b k n", b=2, k=k),
                wg=region(E), bg=region(E), b2=region(D),
                lg=region(T * E).rearrange("p (t e) -> p t e", t=T),
                cmb=region(T * E).rearrange("p (t e) -> p t e", t=T),
                oh=region(T * E).rearrange("p (t e) -> p t e", t=T),
                iota=region(E), iotai=region(E).bitcast(I32),
                top8=region(T * 8).rearrange("p (t e) -> p t e", t=T),
                idx=region(T * 8).bitcast(U32).rearrange("p (t e) -> p t e", t=T),
                idxf=region(T * 8).rearrange("p (t e) -> p t e", t=T),
                gt=region(T * 2).rearrange("p (t e) -> p t e", t=T),
                gd=region(T),
                cmbt=region(N))

        MOE = {1: dict(E=8, H=256, act=ACT.Gelu, gated=False, has_bg=True, names=("Wg", "bg", "W1", "b1", "W2", "b2")),
               2: dict(E=64, H=256, act=ACT.Relu, gated=True, has_bg=True, names=("Wr", "br", "W1", "b1", "W2", "b2")),
               3: dict(E=8, H=128, act=ACT.Gelu, gated=True, has_bg=False, names=("router_w", None, "w1", "b1", "w2", "b2"))}
        for m in MOE.values():
            m.update(moe_arena(m["E"], m["H"]))

        block = ctx.enter_context(nc.Block())

        @block.sync
        def _(sp):
            def load(dst, src, sem):
                sp.dma_start(dst, src).then_inc(S(sem), 16)

            load(X[:], dram["x"].rearrange("(t p) d -> p t d", p=P), "x_in")
            load(w0cat[:], dram["w0cat"], "w_g0")
            load(w0t[:], dram["w0t"], "w_g0")
            load(phi0[:], dram["phi0"], "w_g0")
            load(bias0[:], dram["bias0"].partition_broadcast(P), "w_g0")
            load(bias0t[:], dram["bias0t"], "w_g0")
            for g in (1, 2, 3):
                load(gw[g]["io"][:], dram[f"g{g}_io"], f"w_g{g}")
                load(gw[g]["oi"][:], dram[f"g{g}_oi"], f"w_g{g}")
                load(gw[g]["last"][:], dram[f"g{g}_io"][D - 1, :].partition_broadcast(P), f"w_g{g}")
                load(gw[g]["a"][:], dram[f"g{g}_a"], f"w_g{g}")
            load(b3row[:], dram["g3_b"].partition_broadcast(P), "w_g3")
            load(b3col[:], dram["g3_bc"], "w_g3")
            load(ba3[:], dram["g3_ba"].partition_broadcast(P), "w_g3")
            for j in range(T):
                wait(sp, "mask", j - 1)
                load(ADJ[:, j % 2, :], dram["adjt"][j * P:(j + 1) * P, :], f"adj{j % 2}")

            sp.wait_ge(*at("x_done", 1))
            load(WI, dram["f0_wi"], "w_f0")
            load(BI, dram["f0_bi"], "w_f0")
            load(ROUTE[0:1, :], dram["f0_route"].rearrange("(a g) -> a g", a=1), "w_f0")
            load(ROUTEF[0:E0, :].bitcast(I32), dram["f0_route"].partition_broadcast(E0), "w_f0")
            load(WS, dram["f0_ws"].rearrange("l k p o -> p l k o"), "w_f0")
            load(BRS[0:E0, :, :], dram["f0_br"].rearrange("l e o -> e l o"), "w_f0")
            load(BRS[E0:E0 + 1, :, :], dram["f0_bs"].rearrange("l e o -> e l o"), "w_f0")
            load(WO, dram["f0_wo"].rearrange("k p o -> p k o"), "w_f0")
            load(BO, dram["f0_bo"].partition_broadcast(P), "w_f0")
            for l in range(LAYERS):
                if l:
                    sp.wait_ge(*at("f0.staged", GROUPS * l))
                load(WR, dram["f0_wr"][l].rearrange("e k p o -> p e k o"), "w_f0r")

            for m, M in MOE.items():
                n1, nb, nw1, nb1, nw2, nb2 = M["names"]
                ph = f"f{m}"
                sp.wait_ge(*at("x_done", 2 * m + 1))
                load(M["wg"], dram[f"{ph}_wg"], f"w_{ph}")
                if M["has_bg"]:
                    load(M["bg"], dram[f"{ph}_bg"].partition_broadcast(P), f"w_{ph}")
                load(M["b2"][0:M["E"], :], dram[f"{ph}_b2"], f"w_{ph}")

                def experts(q):
                    for b in range(2):
                        if not (isinstance(q, int) and q == 0):
                            sp.wait_ge(*at(f"{ph}.y_ps", NC * (2 * q + b - 1)))
                        e = 2 * q + b
                        load(M["w1"][:, b, :], dram[f"{ph}_w1"][bass.ds(e, 1)].rearrange("e p h -> p (e h)"), f"{ph}.w{b}")
                        load(M["w2"][:, b, :, :], dram[f"{ph}_w2"][bass.ds(e, 1)].rearrange("e k p d -> p (e k) d"), f"{ph}.w{b}")
                        load(M["b1"][:, b, :], dram[f"{ph}_b1"][bass.ds(e, 1)].rearrange("e p k -> p (e k)"), f"{ph}.w{b}")
                experts(0)
                with sp.Fori(1, M["E"] // 2) as q:
                    experts(q)

            sp.wait_ge(*at("x_done", len(PHASES)))
            sp.dma_start(out.rearrange("(t p) d -> p t d", p=P), X[:]).then_inc(S("stored"), 16)
            sp.wait_ge(*at("stored", 16))

        @block.gpsimd
        def _(pool):
            chain = [0]

            def link(ins):
                chain[0] += 1
                ins.then_inc(S("pool_chain"), 1)
                pool.wait_ge(*at("pool_chain", chain[0]))

            link(nc.gpsimd.memset(IDENT[:], 0.0))
            link(nc.gpsimd.affine_select(out=IDENT[:], in_=IDENT[:], compare_op=ALU.not_equal, fill=1.0,
                                         base=0, pattern=[[-1, P]], channel_multiplier=1))
            nc.gpsimd.memset(MHALF[:], -0.5).then_inc(S("ident"), 1)
            nc.gpsimd.tensor_copy(IDB[:], IDENT[:]).then_inc(S("ident"), 1)

            def rstd(ph):
                pool.wait_ge(*at(f"{ph}.veps", 1))
                if ph == "g0":
                    pool.wait_ge(*at("ident", 1))
                nc.gpsimd.tensor_tensor(RSTD[:], VEPS[:], MHALF[:], ALU.pow).then_inc(S(f"{ph}.rstd"), 1)

            def all_max(ph, n):
                pool.wait_ge(*at(f"{ph}.max", 1))
                nc.gpsimd.partition_all_reduce(GMAX[:, 0:n], MAXES[:, 0:n], P, RMAX).then_inc(S(f"{ph}.gmax"), 1)

            rstd("g0")
            all_max("g0", 8)

            for t in range(T):
                pool.wait_ge(*at("g0.mask_copied", t + 1))
                src = T1.rearrange("p b t s w -> p (b t s w)")[:, (t % TH) * 396:(t % TH + 1) * 396].rearrange(
                    "p (h s w) -> p h s w", h=HEADS, s=PARTS)
                dst = RM[:, t, :, :]
                link(nc.gpsimd.tensor_tensor(dst, src[:, :, 0, :], src[:, :, 1, :], ALU.add))
                nc.gpsimd.tensor_tensor(dst, dst, src[:, :, 2, :], ALU.add).then_inc(S("g0.rm"), 1)

            def head_out(h, ib):
                n = 2 * h + ib
                pool.wait_ge(*at("g0.copied", n + 1))
                tiles = slice(ib * TH, (ib + 1) * TH)
                pool_ops = [
                    (RS, T1[:, ib, :, 0, :], T1[:, ib, :, 1, :], ALU.add),
                    (RS, RS, T1[:, ib, :, 2, :], ALU.add),
                    (RD, RM[:, tiles, h, :], RS[:, :, FH + 1:], ALU.subtract),
                    (RD, RD, AU[:, tiles, 4 + h:5 + h].to_broadcast([P, TH, FH + 1]), ALU.mult),
                    (RE, RS[:, :, 0:FH + 1], AU[:, tiles, h:h + 1].to_broadcast([P, TH, FH + 1]), ALU.mult),
                ]
                if n:
                    pool.wait_ge(*at("g0.rec", n))
                for o, a, b, op in pool_ops:
                    link(nc.gpsimd.tensor_tensor(o, a, b, op))
                link(nc.gpsimd.tensor_tensor(RE, RE, RD, ALU.add))
                nc.gpsimd.nop().then_inc(S("g0.weighed"), 1)
                pool.wait_ge(*at("g0.rec", n + 1))
                link(nc.gpsimd.tensor_tensor(RE[:, :, 0:FH], RE[:, :, 0:FH], RDEN[:, 0:TH].rearrange("p (t a) -> p t a", a=1).to_broadcast([P, TH, FH]), ALU.mult))
                xs = X[:, tiles, h * FH:(h + 1) * FH]
                link(nc.gpsimd.tensor_tensor(xs, xs, RE[:, :, 0:FH], ALU.add))
                nc.gpsimd.nop().then_inc(S("g0.x_added"), 1)

            for h in range(HEADS):
                for ib in range(2):
                    head_out(h, ib)

            nc.gpsimd.iota(IOTAI[0:E0, :], pattern=[[0, 1]], base=0, channel_multiplier=1).then_inc(S("f0.iota"), 1)
            rstd("f0")
            for m, M in MOE.items():
                rstd(f"g{m}")
                all_max(f"g{m}", 2)
                pool.wait_ge(*at("x_done", 2 * m + 1))
                nc.gpsimd.iota(M["iotai"], pattern=[[1, M["E"]]], base=0, channel_multiplier=0).then_inc(S(f"f{m}.iota"), 1)
                rstd(f"f{m}")

        @block.tensor
        def _(pe):
            mm = nc.tensor.matmul

            def transpose_x(ph):
                if ph == "g0":
                    pe.wait_ge(*at("ident", 1))
                for t in range(T):
                    pe.wait_ge(*at(f"{ph}.xn", t + 1))
                    nc.tensor.transpose(PS[:, t // TPC, (t % TPC) * P:(t % TPC + 1) * P], XN[:, t, :], IDENT[:]).then_inc(S(f"{ph}.xnt_ps"), 1)

            pe.wait_ge(*at("w_g0", 16 * 5))
            pe.wait_ge(*at("g0.bias_t", 1))
            for h in range(HEADS):
                mm(PS[:, 7, 2 * h:2 * h + 2], w0t[:, h, :], phi0[:, h, :], start=True, stop=True)
                last = mm(PS[:, 7, 8 + 2 * h:10 + 2 * h], bias0tb[:, h, :], phi0[:, h, :], start=True, stop=True)
            last.then_inc(S("g0.wa_ps"), 1)
            transpose_x("g0")
            pe.wait_ge(*at("g0.xnt", NC))
            pe.wait_ge(*at("g0.wa", 2))
            for t in range(T):
                last = mm(PS[:, 6, t * 8:(t + 1) * 8], XNT[:, t * P:(t + 1) * P], WA[:], start=True, stop=True)
            last.then_inc(S("g0.ab_ps"), 1)
            for t in range(T):
                last = mm(PS[:, t // TPC, (t % TPC) * P:(t % TPC + 1) * P], XNT[:, t * P:(t + 1) * P], w0cat[:], start=True, stop=True)
                if t % TPC == TPC - 1:
                    last.then_inc(S("g0.hx_ps"), 1)
            for h in range(HEADS):
                for c in range(NC):
                    n = h * NC + c
                    if n < 4:
                        pe.wait_ge(*at("g0.hx", n + 1))
                    else:
                        pe.wait_ge(*at("g0.abc", n - 3))
                    mm(PS[:, n % 4, :], WA1B[:, h, :], XNT[:, c * CH:(c + 1) * CH], start=True, stop=True).then_inc(S("g0.abc_ps"), 1)

            pe.wait_ge(*at("g0.vh", 3))
            pe.wait_ge(*at("g0.abc", HEADS * NC))
            for r in range(2):
                for j in range(T):
                    if r == 0:
                        pe.wait_ge(*at("mask0", j + 1))
                    for i in range(TH):
                        if r and j == 0:
                            pe.wait_ge(*at("g0.mask_copied", i + 1))
                        t = r * TH + i
                        last = mm(PS[:, i, 0:396].rearrange("p (h s w) -> p h s w", h=HEADS, s=PARTS), MASK[:, j, t * P:(t + 1) * P],
                                  VH[:, j, :, :, FH + 1:], start=(j == 0), stop=(j == T - 1))
                        if j == T - 1:
                            last.then_inc(S("g0.mask_ps"), 1)

            def head_sums(h, first):
                for ib in range(2):
                    for j in range(T):
                        n = (2 * h + ib) * T + j
                        pe.wait_ge(*at("g0.m1", n + 1))
                        if j == 0:
                            if first:
                                pe.wait_ge(*at("g0.mask_copied", T))
                            else:
                                pe.wait_ge(*at("g0.copied", 2 * h + ib - 1))
                        for i in range(TH):
                            last = mm(PS[:, 4 * ib + i // 2, (i % 2) * 198:(i % 2 + 1) * 198], M1[:, n % M1R if isinstance(n, int) else (ib * T + j) % M1R, i * P:(i + 1) * P],
                                      VH[:, j, h, :, :] if isinstance(h, int) else VH[:, j, bass.ds(h, 1), :, :],
                                      start=(j == 0 and i % 2 == 0), stop=(j == T - 1), skip_group_check=True)
                        last.then_inc(S("g0.m1_used"), 1)
            head_sums(0, True)
            with pe.Fori(1, HEADS) as h:
                head_sums(h, False)

            transpose_x("f0")
            pe.wait_ge(*at("f0.xnt", NC))
            pe.wait_ge(*at("w_f0", 16 * 9))
            for c in range(NC):
                for o in range(KH):
                    n = c * KH + o
                    wait(pe, "f0.h", n - 3)
                    mm(PS[:, 4 + n % 4, :], WI[:, o * P:(o + 1) * P], XNT[:, c * CH:(c + 1) * CH], start=True, stop=True).then_inc(S("f0.h_ps"), 1)

            for l in range(LAYERS):
                pe.wait_ge(*at("f0.onehot", 1))
                for c in range(NC):
                    n = l * NC + c
                    pe.wait_ge(*at("f0.h", l * NC * KH + (c + 1) * KH))
                    wait(pe, "f0.sum", KH * (n - 1))
                    cols = slice(c * CH, (c + 1) * CH)
                    bank = 2 * (n % 2)
                    for o in range(KH):
                        for k in range(KH):
                            mm(PS[:, bank + o, :], WS[:, l, k, o * P:(o + 1) * P], HT0[:, k, cols], start=(k == 0), stop=False, skip_group_check=True)
                        mm(PS[:, bank + o, :], BRS[0:E0 + 1, l, o * P:(o + 1) * P], ONEH[0:E0 + 1, cols], start=False, stop=False, skip_group_check=True)
                    for g in range(GPC):
                        gi = n * GPC + g
                        pe.wait_ge(*at("f0.staged", gi + 1))
                        toks = slice(c * CH + g * GT, c * CH + (g + 1) * GT)
                        for o in range(KH):
                            for k in range(KH):
                                last = mm(PS[:, bank + o, g * GT:(g + 1) * GT], WST[:, g % 4, k, o * P:(o + 1) * P], HT0[:, k, toks],
                                          start=False, stop=(k == KH - 1), skip_group_check=True)
                        last.then_inc(S("f0.stage_used"), 1)
            pe.wait_ge(*at("f0.h", (LAYERS + 1) * NC * KH))
            for t in range(T):
                if t % TPC == 0:
                    pe.wait_ge(*at("f0.sum", LAYERS * NC * KH))
                for k in range(KH):
                    last = mm(PS[:, 4 + t // TPC, (t % TPC) * P:(t % TPC + 1) * P], HT0[:, k, t * P:(t + 1) * P], WO[:, k, :],
                              start=(k == 0), stop=(k == KH - 1), skip_group_check=True)
                last.then_inc(S("f0.out_ps"), 1)

            def attention(g):
                ph = f"g{g}"
                W = gw[g]
                pe.wait_ge(*at("x_done", 2 * g))
                pe.wait_ge(*at(f"w_{ph}", 16 * (7 if g == 3 else 4)))
                last = mm(PS[:, 7, 0:2], W["oi"][:], W["a"][:], start=True, stop=True)
                if g == 3:
                    pe.wait_ge(*at("g3.bias_b", 1))
                    last = mm(PS[:, 7, 2:4], b3cb[:], W["a"][:], start=True, stop=True)
                last.then_inc(S(f"{ph}.wa_ps"), 1)
                transpose_x(ph)
                pe.wait_ge(*at(f"{ph}.xnt", NC))
                pe.wait_ge(*at(f"{ph}.wa", 2))
                for t in range(T):
                    last = mm(PS[:, 6, 2 * t:2 * t + 2], XNT[:, t * P:(t + 1) * P], WA[:, 0:2], start=True, stop=True)
                last.then_inc(S(f"{ph}.ab_ps"), 1)
                if g != 2:
                    for c in range(NC):
                        mm(PS[:, c, :], WA1B[:, 0, :], XNT[:, c * CH:(c + 1) * CH], start=True, stop=True).then_inc(S(f"{ph}.abc_ps"), 1)
                    pe.wait_ge(*at(f"{ph}.gbc", NC))
                    pe.wait_ge(*at(f"{ph}.xv", 2))
                    for j in range(T):
                        pe.wait_ge(*at(f"{ph}.q", j + 1))
                        for c in range(NC):
                            last = mm(PS[:, c, :], XV[:, j, :], QT[:, j % 2, c * CH:(c + 1) * CH], start=(j == 0), stop=(j == T - 1))
                        last.then_inc(S(f"{ph}.q_used"), 1)
                else:
                    pe.wait_ge(*at(f"{ph}.xs", PARTS))
                    for j in range(T):
                        for s in range(PARTS):
                            for c in range(NC):
                                last = mm(PS[:, c, :], XS[:, j, s, :], MASK[:, j, c * CH:(c + 1) * CH],
                                          start=(j == 0 and s == 0), stop=(j == T - 1 and s == PARTS - 1))
                    last.then_inc(S(f"{ph}.q_used"), T)
                pe.wait_ge(*at(f"{ph}.wx", 2))
                pe.wait_ge(*at(f"{ph}.acct", NC))
                for t in range(T):
                    mm(PS[:, (4 + t // 3) % 8, (t % 3) * 129:(t % 3 + 1) * 129], ACCT[:, t * P:(t + 1) * P], W["wx"][:], start=True, stop=True).then_inc(S(f"{ph}.out_ps"), 1)

            def moe(m):
                M = MOE[m]
                ph, E, k_, H = f"f{m}", M["E"], M["k"], M["H"]
                pe.wait_ge(*at("x_done", 2 * m + 1))
                transpose_x(ph)
                pe.wait_ge(*at(f"{ph}.xnt", NC))
                pe.wait_ge(*at(f"w_{ph}", 16 * (3 if M["has_bg"] else 2)))
                for t in range(T):
                    bank, col = 4 + t * E // CH, t * E % CH
                    last = mm(PS[:, bank, col:col + E], XNT[:, t * P:(t + 1) * P], M["wg"], start=True, stop=True)
                last.then_inc(S(f"{ph}.lg_ps"), 1)
                pe.wait_ge(*at(f"{ph}.cmb", 1))
                for t in range(T):
                    nc.tensor.transpose(PS[0:E, t // TPC, (t % TPC) * P:(t % TPC + 1) * P], M["cmb"][:, t, :], IDENT[:]).then_inc(S(f"{ph}.cmbt_ps"), 1)
                pe.wait_ge(*at(f"{ph}.cmbt", NC))
                for t in range(T):
                    last = mm(PS[:, 4 + t // TPC, (t % TPC) * P:(t % TPC + 1) * P], M["cmbt"][0:E, t * P:(t + 1) * P], M["b2"][0:E, :], start=True, stop=True)
                    last.then_inc(S(f"{ph}.bias_ps"), 1)
                pe.wait_ge(*at(f"{ph}.acc", 1))

                def hidden(q, s):
                    b, c = s // NC, s % NC
                    n = q * 2 * NC + s
                    if c == 0:
                        pe.wait_ge(*at(f"{ph}.w{b}", 48 * q + 48))
                    wait(pe, f"{ph}.ht", k_ * (n - 1))
                    for k in range(k_):
                        mm(PS[:, 2 * (s % 2) + k, :], M["w1"][:, b, k * P:(k + 1) * P], XNT[:, c * CH:(c + 1) * CH], start=True, stop=True).then_inc(S(f"{ph}.h_ps"), 1)

                def outputs(q, s):
                    b, c = s // NC, s % NC
                    n = q * 2 * NC + s
                    pe.wait_ge(*at(f"{ph}.ht", k_ * (n + 1)))
                    wait(pe, f"{ph}.y", n - 1)
                    for t in range(TPC):
                        for k in range(k_):
                            last = mm(PS[:, 4 + s % 2, t * P:(t + 1) * P], M["ht"][:, s % 2, k, t * P:(t + 1) * P], M["w2"][:, b, k, :],
                                      start=(k == 0), stop=(k == k_ - 1), skip_group_check=True)
                    last.then_inc(S(f"{ph}.y_ps"), 1)

                def pair(q, end=False):
                    for s in range(2 * NC):
                        if s < 2 * NC - 1:
                            hidden(q, s + 1)
                        elif not end:
                            hidden(q + 1, 0)
                        outputs(q, s)
                hidden(0, 0)
                pair(0)
                if E // 2 > 2:
                    with pe.Fori(1, E // 2 - 1) as q:
                        pair(q)
                pair(E // 2 - 1, end=True)

            for g in (1, 2, 3):
                attention(g)
                moe(g)

        @block.scalar
        def _(act):
            A = nc.scalar.activation

            def copy_xnt(ph):
                for c in range(NC):
                    act.wait_ge(*at(f"{ph}.xnt_ps", TPC * (c + 1)))
                    nc.scalar.copy(XNT[:, c * CH:(c + 1) * CH], PS[:, c, :]).then_inc(S(f"{ph}.xnt"), 1)

            act.wait_ge(*at("g0.wa_ps", 1))
            nc.scalar.copy(WA[:].rearrange("p (s h) -> p s h", s=2), PS[:, 7, 0:8].rearrange("p (h s) -> p s h", s=2)).then_inc(S("g0.wa"), 1)
            nc.scalar.copy(SMALL[:, 0:8].rearrange("p (s h) -> p s h", s=2), PS[:, 7, 8:16].rearrange("p (h s) -> p s h", s=2)).then_inc(S("g0.consts"), 1)
            copy_xnt("g0")
            act.wait_ge(*at("g0.consts", 1))
            for h in range(HEADS):
                for c in range(NC):
                    n = h * NC + c
                    act.wait_ge(*at("g0.abc_ps", n + 1))
                    A(ABC[:, h, c * CH:(c + 1) * CH], PS[:, n % 4, :], ACT.Identity, bias=SMALL[:, h:h + 1]).then_inc(S("g0.abc"), 1)
            act.wait_ge(*at("g0.uv_in", 2))
            A(AV[:, :, 0:4], AV[:, :, 0:4], ACT.Exp).then_inc(S("g0.uv"), 1)
            A(AV[:, :, 4:8], AV[:, :, 4:8], ACT.Exp, scale=SLOPE).then_inc(S("g0.uv"), 1)
            A(AU[:, :, 0:4], AU[:, :, 0:4], ACT.Exp, scale=REST).then_inc(S("g0.uv"), 1)
            A(AU[:, :, 4:8], AU[:, :, 4:8], ACT.Exp, scale=-REST).then_inc(S("g0.uv"), 1)
            for t in range(T):
                act.wait_ge(*at("g0.mask_ps", t + 1))
                if t >= TH:
                    act.wait_ge(*at("g0.rm", t - TH + 1))
                if t == 0:
                    act.wait_ge(*at("mask0", T))
                dst = T1.rearrange("p b t s w -> p (b t s w)")[:, (t % TH) * 396:(t % TH + 1) * 396]
                nc.scalar.copy(dst, PS[:, t % TH, 0:396]).then_inc(S("g0.mask_copied"), 1)
            act.wait_ge(*at("g0.rm", T))
            for n in range(2 * HEADS):
                ib = n % 2
                act.wait_ge(*at("g0.m1_used", (n + 1) * T))
                wait(act, "g0.x_added", n - 1)
                for b in range(4):
                    last = nc.scalar.copy(T1[:, ib, 2 * b:2 * b + 2, :, :].rearrange("p t s w -> p (t s w)"), PS[:, 4 * ib + b, 0:396])
                last.then_inc(S("g0.copied"), 1)

            copy_xnt("f0")
            for c in range(NC):
                for o in range(KH):
                    n = c * KH + o
                    act.wait_ge(*at("f0.h_ps", n + 1))
                    A(HT0[:, o, c * CH:(c + 1) * CH], PS[:, 4 + n % 4, :], ACT.Relu, bias=BI[:, o:o + 1]).then_inc(S("f0.h"), 1)
            for n in range(LAYERS * NC):
                c = n % NC
                for o in range(KH):
                    act.wait_ge(*at("f0.sum", n * KH + o + 1))
                    A(HT0[:, o, c * CH:(c + 1) * CH], HSUM[:, o, :], ACT.Relu).then_inc(S("f0.h"), 1)

            def attention(g):
                ph = f"g{g}"
                act.wait_ge(*at(f"{ph}.wa_ps", 1))
                wn = 4 if g == 3 else 2
                nc.scalar.copy(WA[:, 0:wn], PS[:, 7, 0:wn]).then_inc(S(f"{ph}.wa"), 1)
                copy_xnt(ph)
                if g != 2:
                    act.wait_ge(*at(f"{ph}.shift", 1))
                    for c in range(NC):
                        act.wait_ge(*at(f"{ph}.abc_ps", c + 1))
                        A(GBC[:, c * CH:(c + 1) * CH], PS[:, c, :], ACT.Exp, bias=SMALL[:, 0:1], scale=REST).then_inc(S(f"{ph}.gbc"), 1)
                    A(AU[:, :, 0], AB[:, :, 1], ACT.Exp, bias=SMALL[:, 1:2], scale=REST).then_inc(S(f"{ph}.uv"), 1)
                    A(SMALL[:, 5:6], SMALL[:, 3:4], ACT.Exp).then_inc(S(f"{ph}.uv"), 1)
                    A(AV[:, :, 0], AB[:, :, 1], ACT.Exp, bias=SMALL[:, 2:3], scale=SLOPE).then_inc(S(f"{ph}.uv"), 1)
                    act.wait_ge(*at(f"{ph}.negc", 1))
                    act.wait_ge(*at(f"{ph}.gbc", NC))
                    for j in range(T):
                        wait(act, f"{ph}.q", j - 1)
                        A(REL[:, j % 2, :], GBC, ACT.Relu, bias=SMALL[:, 6:7], scale=AU[:, j, 0:1]).then_inc(S(f"{ph}.rel"), 1)
                else:
                    act.wait_ge(*at(f"{ph}.shift", 1))
                    A(AV[:, :, 0], AB[:, :, 1], ACT.Exp, bias=SMALL[:, 2:3], scale=1.0).then_inc(S(f"{ph}.uv"), 3)
                for c in range(NC):
                    act.wait_ge(*at(f"{ph}.q_used", T))
                    nc.scalar.copy(ACCT[:, c * CH:(c + 1) * CH], PS[:, c, :]).then_inc(S(f"{ph}.acct"), 1)

            def moe(m):
                M = MOE[m]
                ph, E, k_ = f"f{m}", M["E"], M["k"]
                copy_xnt(ph)
                if M["gated"]:
                    act.wait_ge(*at(f"{ph}.gap", 1))
                    A(M["gt"][:, :, 1], M["gt"][:, :, 1], ACT.Exp).then_inc(S(f"{ph}.gap_exp"), 1)
                for c in range(NC):
                    act.wait_ge(*at(f"{ph}.cmbt_ps", TPC * (c + 1)))
                    nc.scalar.copy(M["cmbt"][0:E, c * CH:(c + 1) * CH], PS[0:E, c, :]).then_inc(S(f"{ph}.cmbt"), 1)

                def pair(q):
                    for s in range(2 * NC):
                        b, n = s // NC, q * 2 * NC + s
                        wait(act, f"{ph}.y_ps", n - 1)
                        for k in range(k_):
                            act.wait_ge(*at(f"{ph}.h_ps", k_ * n + k + 1))
                            A(M["ht"][:, s % 2, k, :], PS[:, 2 * (s % 2) + k, :], M["act"], bias=M["b1"][:, b, k:k + 1]).then_inc(S(f"{ph}.ht"), 1)
                pair(0)
                with act.Fori(1, E // 2) as q:
                    pair(q)

            for g in (1, 2, 3):
                attention(g)
                moe(g)

        @block.vector
        def _(dve):
            V = nc.vector
            chain = [0]

            def mark(ins):
                chain[0] += 1
                ins.then_inc(S("dve_chain"), 1)
                return chain[0]

            def link(ins):
                dve.wait_ge(*at("dve_chain", mark(ins)))

            def norm(ph):
                for t in range(T):
                    last = V.bn_stats(STATS[:, t, :], X[:, t, :])
                    last.then_inc(S(f"{ph}.stats"), 1)
                for t in range(T):
                    dve.wait_ge(*at(f"{ph}.stats", t + 1))
                    last = V.bn_aggr(MV[:, t, :], STATS[:, t, :])
                link(last)
                V.tensor_scalar(VEPS[:], MV[:, :, 1], EPS, None, ALU.add).then_inc(S(f"{ph}.veps"), 1)
                dve.wait_ge(*at(f"{ph}.rstd", 1))
                for t in range(T):
                    V.tensor_scalar(XN[:, t, :], X[:, t, :], MV[:, t, 0:1], RSTD[:, t:t + 1], ALU.subtract, ALU.mult).then_inc(S(f"{ph}.xn"), 1)

            dve.wait_ge(*at("w_g0", 16 * 5))
            V.tensor_copy(bias0tb[:], bias0t[:].rearrange("p (h a) -> p h a", a=1).to_broadcast([FH, HEADS, P])).then_inc(S("g0.bias_t"), 1)
            dve.wait_ge(*at("x_in", 16))
            norm("g0")
            dve.wait_ge(*at("g0.wa", 1))
            V.tensor_copy(WA1B[:], WA[:, 0:4].rearrange("p (h a) -> p h a", a=1).to_broadcast([P, 4, P])).then_inc(S("g0.wa"), 1)
            dve.wait_ge(*at("g0.ab_ps", 1))
            dve.wait_ge(*at("g0.consts", 1))
            link(V.tensor_tensor(AB[:], PS[:, 6, 0:T * 8].rearrange("p (t c) -> p t c", t=T),
                                 SMALL[:, 0:8].rearrange("p (a c) -> p a c", a=1).to_broadcast([P, T, 8]), ALU.add))
            V.tensor_reduce(MAXES[:, 0:8], AB[:].rearrange("p t c -> p c t"), AX_X, ALU.max).then_inc(S("g0.max"), 1)
            for c in range(NC):
                dve.wait_ge(*at("g0.hx_ps", c + 1))
                V.tensor_tensor(HX[:, c * TPC:(c + 1) * TPC, :], PS[:, c, :].rearrange("p (t d) -> p t d", t=TPC),
                                bias0[:].rearrange("p (a d) -> p a d", a=1).to_broadcast([P, TPC, D]), ALU.add).then_inc(S("g0.hx"), 1)
            dve.wait_ge(*at("g0.gmax", 1))
            bmax = GMAX[:, 4:8].rearrange("p (a c) -> p a c", a=1).to_broadcast([P, T, 4])
            V.tensor_tensor(AV[:, :, 0:4], AB[:, :, 4:8], bmax, ALU.subtract)
            V.tensor_tensor(AV[:, :, 4:8], AB[:, :, 4:8], bmax, ALU.subtract)
            link(V.tensor_tensor(AU[:, :, 0:4], AB[:, :, 0:4], bmax, ALU.add))
            V.tensor_scalar(AU[:, :, 4:8], AU[:, :, 0:4], 0.0, None, ALU.max).then_inc(S("g0.uv_in"), 1)
            dve.wait_ge(*at("g0.uv_in", 1))
            V.tensor_scalar(AU[:, :, 0:4], AU[:, :, 0:4], 0.0, None, ALU.min).then_inc(S("g0.uv_in"), 1)
            link(V.tensor_scalar(AB[:, :, 4:8], AB[:, :, 4:8], -1.0, None, ALU.mult))
            dve.wait_ge(*at("g0.hx", NC))
            dve.wait_ge(*at("g0.uv", 4))
            hx4 = HX.rearrange("p t (h f) -> p t h f", h=HEADS)
            for br in range(2):
                vcol = AV[:, :, 4 * br:4 * br + 4].rearrange("p t (h a) -> p t h a", a=1)
                for t in range(T):
                    V.tensor_tensor(VF[:, t, :, br * (FH + 1):br * (FH + 1) + FH], hx4[:, t], vcol[:, t].to_broadcast([P, HEADS, FH]), ALU.mult)
                last = V.tensor_copy(VF[:, :, :, br * (FH + 1) + FH], AV[:, :, 4 * br:4 * br + 4])
            link(last)
            for s in range(PARTS):
                last = V.tensor_copy(VH[:, :, :, s, :].rearrange("p t h w -> p (t h) w"), VF.rearrange("p t h w -> p (t h) w"))
                last.then_inc(S("g0.vh"), 1)
                if s < PARTS - 1:
                    dve.wait_ge(*at("g0.vh", s + 1))
                    link(V.tensor_tensor(VF.rearrange("p t h w -> p (t h) w"), VF.rearrange("p t h w -> p (t h) w"), VH[:, :, :, s, :].rearrange("p t h w -> p (t h) w"), ALU.subtract))

            dve.wait_ge(*at("ident", 2))
            for j in range(T):
                dve.wait_ge(*at(f"adj{j % 2}", 16 * (j // 2 + 1)))
                V.tensor_scalar(MASK[:, j, :], ADJ[:, j % 2, :], 0, None, ALU.is_gt).then_inc(S("mask"), 1)
                dve.wait_ge(*at("mask", j + 1))
                own = MASK[:, j, j * P:(j + 1) * P]
                link(V.tensor_copy(DIAG[:, j, :], own))
                V.tensor_tensor(own, own, IDB[:], ALU.max).then_inc(S("mask0"), 1)
            dve.wait_ge(*at("mask0", T))
            dve.wait_ge(*at("g0.abc", HEADS * NC))
            dve.wait_ge(*at("g0.vh", PARTS))

            def recip(n):
                dve.wait_ge(*at("g0.weighed", n + 1))
                V.reciprocal(RDEN[:, 0:TH], RE[:, :, FH]).then_inc(S("g0.rec"), 1)

            for h in range(HEADS):
                for ib in range(2):
                    for j in range(T):
                        n = (2 * h + ib) * T + j
                        wait(dve, "g0.m1_used", n - M1R + 1)
                        V.scalar_tensor_tensor(M1[:, n % M1R, :], ABC[:, h, ib * HB:(ib + 1) * HB], AB[:, j, 4 + h:5 + h],
                                               MASK[:, j, ib * HB:(ib + 1) * HB], ALU.is_gt, ALU.mult).then_inc(S("g0.m1"), 1)
                    if 2 * h + ib:
                        recip(2 * h + ib - 1)
            recip(2 * HEADS - 1)
            for j in range(T):
                last = V.tensor_copy(MASK[:, j, j * P:(j + 1) * P], DIAG[:, j, :])
            link(last)
            dve.wait_ge(*at("g0.x_added", 2 * HEADS))
            V.tensor_copy(SMALL[:, 32:33], SMALL[:, 0:1]).then_inc(S("x_done"), 1)

            norm("f0")
            dve.wait_ge(*at("f0.xn", T))
            dve.wait_ge(*at("w_f0", 16 * 9))
            dve.wait_ge(*at("f0.iota", 1))
            link(V.tensor_tensor(X[:], X[:], BO.rearrange("p (a d) -> p a d", a=1).to_broadcast([P, T, D]), ALU.add))
            V.tensor_copy(IOTAF[0:E0, :], IOTAI[0:E0, :])
            link(V.tensor_copy(ROUTEF[0:E0, :], ROUTEF[0:E0, :].bitcast(I32)))
            link(V.memset(ONEH[0:32, :], 1.0))
            V.tensor_scalar(ONEH[0:E0, :].rearrange("p (g t) -> p g t", t=GT), ROUTEF[0:E0, :].rearrange("p (g a) -> p g a", a=1).to_broadcast([E0, GROUPS, GT]),
                            IOTAF[0:E0, 0:1], None, ALU.is_equal).then_inc(S("f0.onehot"), 1)
            for n in range(LAYERS * NC):
                l, c = n // NC, n % NC
                dve.wait_ge(*at("w_f0r", 16 * (l + 1)))
                for g in range(GPC):
                    gi = n * GPC + g
                    wait(dve, "f0.stage_used", gi - 3)
                    with nc.vector.register(f"r{gi}") as _r:
                        e = dve.value_load(ROUTE[0:1, c * GPC + g:c * GPC + g + 1], min_val=0, max_val=E0 - 1)
                        V.tensor_copy(WST[:, g % 4, :, :].rearrange("p k o -> p (k o)"), WR[:, bass.ds(e, 1), :, :].rearrange("p e k o -> p (e k o)")).then_inc(S("f0.staged"), 1)
                for o in range(KH):
                    dve.wait_ge(*at("f0.stage_used", (n + 1) * GPC))
                    wait(dve, "f0.h", NC * KH + (n - 1) * KH + o + 1 if n else 0)
                    V.tensor_tensor(HSUM[:, o, :], PS[:, 2 * (n % 2) + o, :], HT0[:, o, c * CH:(c + 1) * CH], ALU.add).then_inc(S("f0.sum"), 1)
            for t in range(T):
                dve.wait_ge(*at("f0.out_ps", (t // TPC + 1) * TPC))
                last = V.tensor_tensor(X[:, t, :], X[:, t, :], PS[:, 4 + t // TPC, (t % TPC) * P:(t % TPC + 1) * P], ALU.add)
            last.then_inc(S("x_done"), 1)
            dve.wait_ge(*at("x_done", 2))

            def attention(g):
                ph = f"g{g}"
                W = gw[g]
                dve.wait_ge(*at(f"w_{ph}", 16 * (7 if g == 3 else 4)))
                if g == 3:
                    V.tensor_copy(b3cb[:], b3col[:].to_broadcast([P, P])).then_inc(S("g3.bias_b"), 1)
                V.tensor_tensor(W["wx"][:, 0:D], W["io"][:], W["last"][:], ALU.subtract).then_inc(S(f"{ph}.wx"), 1)
                V.tensor_copy(W["wx"][:, D:D + 1], IDENT[:, D - 1:D]).then_inc(S(f"{ph}.wx"), 1)
                norm(ph)
                dve.wait_ge(*at(f"{ph}.wa", 1))
                V.tensor_copy(WA1B[:, 0, :], WA[:, 0:1].to_broadcast([P, P])).then_inc(S(f"{ph}.wa"), 1)
                dve.wait_ge(*at(f"{ph}.ab_ps", 1))
                link(V.tensor_copy(AB[:, :, 0:2], PS[:, 6, 0:2 * T].rearrange("p (t c) -> p t c", t=T)))
                V.tensor_reduce(MAXES[:, 0:2], AB[:, :, 0:2].rearrange("p t c -> p c t"), AX_X, ALU.max).then_inc(S(f"{ph}.max"), 1)
                dve.wait_ge(*at(f"{ph}.gmax", 1))
                if g == 2:
                    V.tensor_scalar(SMALL[:, 2:3], GMAX[:, 1:2], -1.0, None, ALU.mult).then_inc(S(f"{ph}.shift"), 1)
                else:
                    link(V.tensor_tensor(SMALL[:, 4:5], GMAX[:, 0:1], GMAX[:, 1:2], ALU.add))
                    if g == 3:
                        link(V.tensor_tensor(SMALL[:, 4:5], SMALL[:, 4:5], WA[:, 2:3], ALU.add))
                        link(V.tensor_tensor(SMALL[:, 4:5], SMALL[:, 4:5], WA[:, 3:4], ALU.add))
                        link(V.tensor_tensor(SMALL[:, 4:5], SMALL[:, 4:5], ba3[:], ALU.add))
                    V.tensor_scalar(SMALL[:, 0:1], GMAX[:, 0:1], -REST, None, ALU.mult)
                    V.tensor_scalar(SMALL[:, 2:3], GMAX[:, 1:2], -SLOPE, None, ALU.mult)
                    link(V.tensor_scalar(SMALL[:, 3:4], SMALL[:, 4:5], 0.0, -REST, ALU.max, ALU.mult))
                    link(V.tensor_scalar(SMALL[:, 3:4], SMALL[:, 3:4], HEADROOM, None, ALU.add))
                    link(V.tensor_scalar(SMALL[:, 1:2], SMALL[:, 4:5], 0.0, None, ALU.min))
                    link(V.tensor_tensor(SMALL[:, 1:2], SMALL[:, 1:2], GMAX[:, 1:2], ALU.subtract))
                    V.tensor_scalar(SMALL[:, 1:2], SMALL[:, 1:2], REST, HEADROOM, ALU.mult, ALU.add).then_inc(S(f"{ph}.shift"), 1)
                    dve.wait_ge(*at(f"{ph}.uv", 2))
                    V.tensor_scalar(SMALL[:, 6:7], SMALL[:, 5:6], -1.0, None, ALU.mult).then_inc(S(f"{ph}.negc"), 1)
                dve.wait_ge(*at(f"{ph}.uv", 3))
                v = AV[:, :, 0:1]
                V.tensor_tensor(XV[:, :, 0:D - 1], XN[:, :, 0:D - 1], v.to_broadcast([P, T, D - 1]), ALU.mult).then_inc(S(f"{ph}.xv"), 1)
                V.tensor_copy(XV[:, :, D - 1:D], v).then_inc(S(f"{ph}.xv"), 1)
                if g == 2:
                    dve.wait_ge(*at(f"{ph}.xv", 2))
                    for s in range(PARTS):
                        V.tensor_copy(XS[:, :, s, :], XV).then_inc(S(f"{ph}.xs"), 1)
                        if s < PARTS - 1:
                            dve.wait_ge(*at(f"{ph}.xs", s + 1))
                            link(V.tensor_tensor(XV, XV, XS[:, :, s, :], ALU.subtract))
                else:
                    for j in range(T):
                        dve.wait_ge(*at(f"{ph}.rel", j + 1))
                        wait(dve, f"{ph}.q_used", j - 1)
                        V.scalar_tensor_tensor(QT[:, j % 2, :], REL[:, j % 2, :], SMALL[:, 5:6], MASK[:, j, :], ALU.add, ALU.mult).then_inc(S(f"{ph}.q"), 1)
                if g == 3:
                    link(V.tensor_tensor(X[:], X[:], b3row[:].rearrange("p (a d) -> p a d", a=1).to_broadcast([P, T, D]), ALU.add))
                dve.wait_ge(*at(f"{ph}.out_ps", T))
                V.reciprocal(RDEN[:, 0:12].rearrange("p (b t) -> p b t", b=4), PS[:, 4:8, 0:387].rearrange("p b (t c) -> p b t c", c=D + 1)[:, :, :, D])
                V.reciprocal(RDEN[:, 12:15], PS[:, 0, 0:387].rearrange("p (t c) -> p t c", c=D + 1)[:, :, D])
                link(V.reciprocal(RDEN[:, 15:16], PS[:, 1, D:D + 1]))
                for t in range(T):
                    last = V.scalar_tensor_tensor(X[:, t, :], PS[:, (4 + t // 3) % 8, (t % 3) * 129:(t % 3) * 129 + D], RDEN[:, t:t + 1], X[:, t, :], ALU.mult, ALU.add)
                last.then_inc(S("x_done"), 1)
                dve.wait_ge(*at("x_done", 2 * g + 1))

            def moe(m):
                M = MOE[m]
                ph, E = f"f{m}", M["E"]
                norm(ph)
                dve.wait_ge(*at(f"{ph}.iota", 1))
                link(V.tensor_copy(M["iota"], M["iotai"]))
                dve.wait_ge(*at(f"{ph}.lg_ps", 1))
                nb = (T * E + CH - 1) // CH
                lgps = PS[:, 4:4 + nb, :].rearrange("p b n -> p (b n)")[:, 0:T * E].rearrange("p (t e) -> p t e", t=T)
                if M["has_bg"]:
                    link(V.tensor_tensor(M["lg"], lgps, M["bg"].rearrange("p (a e) -> p a e", a=1).to_broadcast([P, T, E]), ALU.add))
                else:
                    link(V.tensor_copy(M["lg"], lgps))
                for t in range(T):
                    V.max(M["top8"][:, t, :], M["lg"][:, t, :]).then_inc(S(f"{ph}.top"), 1)
                for t in range(T):
                    dve.wait_ge(*at(f"{ph}.top", t + 1))
                    last = V.max_index(M["idx"][:, t, :], M["top8"][:, t, :], M["lg"][:, t, :])
                link(last)
                link(V.tensor_copy(M["idxf"], M["idx"]))
                if M["gated"]:
                    V.tensor_tensor(M["gt"][:, :, 1], M["top8"][:, :, 1], M["top8"][:, :, 0], ALU.subtract).then_inc(S(f"{ph}.gap"), 1)
                    dve.wait_ge(*at(f"{ph}.gap_exp", 1))
                    link(V.tensor_scalar(M["gd"], M["gt"][:, :, 1], 1.0, None, ALU.add))
                    link(V.reciprocal(M["gt"][:, :, 0], M["gd"]))
                    link(V.tensor_tensor(M["gt"][:, :, 1], M["gt"][:, :, 1], M["gt"][:, :, 0], ALU.mult))
                iot = M["iota"].rearrange("p (a e) -> p a e", a=1).to_broadcast([P, T, E])
                for k, dst in ((0, M["cmb"]), (1, M["oh"])):
                    link(V.tensor_tensor(dst, iot, M["idxf"][:, :, k:k + 1].to_broadcast([P, T, E]), ALU.is_equal))
                    if M["gated"]:
                        link(V.tensor_tensor(dst, dst, M["gt"][:, :, k:k + 1].to_broadcast([P, T, E]), ALU.mult))
                V.tensor_tensor(M["cmb"], M["cmb"], M["oh"], ALU.add).then_inc(S(f"{ph}.cmb"), 1)
                if m == 3:
                    link(V.tensor_tensor(X[:], X[:], XN[:], ALU.add))
                for c in range(NC):
                    dve.wait_ge(*at(f"{ph}.bias_ps", TPC * (c + 1)))
                    xs = X[:, c * TPC:(c + 1) * TPC, :]
                    last = V.tensor_tensor(xs, xs, PS[:, 4 + c, :].rearrange("p (t d) -> p t d", t=TPC), ALU.add)
                last.then_inc(S(f"{ph}.acc"), 1)

                def pair(q):
                    for s in range(2 * NC):
                        b, c, n = s // NC, s % NC, q * 2 * NC + s
                        dve.wait_ge(*at(f"{ph}.y_ps", n + 1))
                        if isinstance(n, int) and n < NC:
                            dve.wait_ge(*at(f"{ph}.acc", 1))
                            dve.wait_ge(*at(f"{ph}.cmb", 1))
                        else:
                            dve.wait_ge(*at(f"{ph}.y", n - NC + 1))
                        for t in range(TPC):
                            tt = c * TPC + t
                            last = V.scalar_tensor_tensor(X[:, tt, :], PS[:, 4 + s % 2, t * P:(t + 1) * P], M["cmb"][:, tt, bass.ds(2 * q + b, 1)], X[:, tt, :], ALU.mult, ALU.add)
                        last.then_inc(S(f"{ph}.y"), 1)
                pair(0)
                with dve.Fori(1, E // 2) as q:
                    pair(q)
                dve.wait_ge(*at(f"{ph}.y", E * NC))
                V.tensor_copy(SMALL[:, 32:33], IDENT[:, 0:1]).then_inc(S("x_done"), 1)

            for g in (1, 2, 3):
                attention(g)
                moe(g)


def kernel(**inputs):
    import numpy as np
    import concourse.bacc as bacc
    from concourse.bass_utils import run_bass_kernel_spmd as run

    a = {k: np.asarray(v) for k, v in inputs.items()}
    lay = {
        "x": a["x"],
        "adjt": a["adj"].T,
        "w0cat": a["L0_gnn_weights"].transpose(1, 0, 2).reshape(D, D),
        "w0t": a["L0_gnn_weights"].transpose(2, 0, 1),
        "phi0": a["L0_gnn_phis"][:, :, 0].reshape(HEADS, 2, FH).transpose(2, 0, 1),
        "bias0": a["L0_gnn_biases"].reshape(D),
        "bias0t": a["L0_gnn_biases"].T,
        "g1_io": a["L1_gnn_W"], "g1_oi": a["L1_gnn_W"].T, "g1_a": a["L1_gnn_a"].reshape(2, D).T,
        "g2_io": a["L2_gnn_W"].T, "g2_oi": a["L2_gnn_W"], "g2_a": a["L2_gnn_a"].reshape(2, D).T,
        "g3_io": a["L3_gnn_W"].T, "g3_oi": a["L3_gnn_W"], "g3_a": a["L3_gnn_a_vec"].reshape(2, D).T,
        "g3_b": a["L3_gnn_b_W"], "g3_bc": a["L3_gnn_b_W"].reshape(D, 1), "g3_ba": a["L3_gnn_b_a"],
        "f0_wi": a["L0_ffn_Wi"].T, "f0_bi": a["L0_ffn_bi"].reshape(KH, P).T,
        "f0_route": a["L0_ffn_route_id"],
        "f0_ws": a["L0_ffn_Ws"][:, 0].transpose(0, 2, 1).reshape(LAYERS, KH, P, HID),
        "f0_br": a["L0_ffn_br"], "f0_bs": a["L0_ffn_bs"],
        "f0_wr": a["L0_ffn_Wr"].transpose(0, 1, 3, 2).reshape(LAYERS, E0, KH, P, HID),
        "f0_wo": a["L0_ffn_Wo"].T.reshape(KH, P, D), "f0_bo": a["L0_ffn_bo"],
    }
    for m, (wg, bg, w1, b1, w2, b2) in ((1, ("Wg", "bg", "W1", "b1", "W2", "b2")), (2, ("Wr", "br", "W1", "b1", "W2", "b2")),
                                        (3, ("router_w", None, "w1", "b1", "w2", "b2"))):
        f = lambda name: a[f"L{m}_ffn_{name}"]
        E, _, H = f(w1).shape
        lay[f"f{m}_wg"] = f(wg).T if m == 3 else f(wg)
        if bg:
            lay[f"f{m}_bg"] = f(bg)
        lay[f"f{m}_w1"] = f(w1)
        lay[f"f{m}_b1"] = f(b1).reshape(E, H // P, P).transpose(0, 2, 1)
        lay[f"f{m}_w2"] = f(w2).reshape(E, H // P, P, D)
        lay[f"f{m}_b2"] = f(b2)

    nc = bacc.Bacc("TRN2", target_bir_lowering=False, num_devices=1)
    arrays, dram = {}, {}
    for name, v in lay.items():
        v = np.ascontiguousarray(v)
        arrays[f"in_{name}"] = v
        dram[name] = nc.dram_tensor(f"in_{name}", v.shape, mybir.dt.from_np(v.dtype), kind="ExternalInput").ap()
    out = nc.dram_tensor("out_0", (N, D), F32, kind="ExternalOutput").ap()
    build(nc, dram, out)
    r = run(nc, [arrays], core_ids=[0])
    return r.results[0]["out_0"]
```

```python
from contextlib import ExitStack

import concourse.bass as bass
from concourse import mybir

ALU = mybir.AluOpType
ACT = mybir.ActivationFunctionType
F32 = mybir.dt.float32
BF16 = mybir.dt.bfloat16
I32 = mybir.dt.int32
U32 = mybir.dt.uint32
AX_X = mybir.AxisListType.X
RMAX = bass.bass_isa.ReduceOp.max

P = 128
N = 2048
D = 128
T = N // P
CH = 512
NC = N // CH
TPC = CH // P
EPS = 1e-5
SLOPE = 0.2
REST = 1.0 - SLOPE
HEADROOM = 40.0

HEADS = 4
FH = D // HEADS
VW = 2 * (FH + 1)
PARTS = 3
HB = N // 2
TH = HB // P

HID = 256
KH = HID // P
LAYERS = 2
E0 = 16
GROUPS = 64
GT = N // GROUPS
GPC = CH // GT


PHASES = ["g0", "f0", "g1", "f1", "g2", "f2", "g3", "f3"]
EXPERTS = {"f1": (8, 2), "f3": (8, 1)}


def stage_counts():
    counts = {}
    for stage, n in dict(stats=T, veps=1, rstd=1, xn=T, xnt_ps=T, xnt=NC).items():
        counts[stage] = {p: n for p in PHASES}
    for stage, n in dict(max=1, gmax=1).items():
        counts[stage] = {p: n for p in ("g0", "g1", "g2", "g3")}
    for stage, n in dict(wa_ps=1, wa=2, ab_ps=1, wx=2, shift=1, uv=3, xv=2, q_used=T, acct=NC, out_ps=T).items():
        counts[stage] = {p: n for p in ("g1", "g2", "g3")}
    for stage, n in dict(abc_ps=NC, gbc=NC, negc=1, rel=T, q=T).items():
        counts[stage] = {p: n for p in ("g1", "g3")}
    for stage, n in dict(lg_ps=1, top=T, cmb=1, cmbt_ps=T, cmbt=NC, bias_ps=T, acc=1, iota=1).items():
        counts[stage] = {p: n for p in ("f1", "f2", "f3")}
    for stage, n in dict(gap=1, gap_exp=1).items():
        counts[stage] = {p: n for p in ("f2", "f3")}
    for stage, n in dict(w0=24, w1=24, y_ps=NC, y=NC).items():
        counts[stage] = {p: n * e for p, (e, _) in EXPERTS.items()}
    for stage in ("h_ps", "ht"):
        counts[stage] = {p: NC * e * k for p, (e, k) in EXPERTS.items()}
    return counts


COUNTS = stage_counts()

E2 = 64
TOPK = 2
EXTRA = TOPK * N // P
TILES = E2 + EXTRA
RING = 8
ROUNDS = TILES // RING
W2AT = HID + KH
WROW = W2AT + KH * D
F16 = mybir.dt.float16


def build(nc, dram, out):
    ctx = ExitStack()
    with ctx:
        sems = {}

        def S(name):
            stage = name.split(".")[-1]
            if "." in name and name.split(".")[0] in COUNTS.get(stage, {}):
                name = stage
            if name not in sems:
                sems[name] = ctx.enter_context(nc.semaphore(name.replace(".", "_")))
            return sems[name]

        def sb(name, shape, dt=F32):
            return ctx.enter_context(nc.sbuf_tensor(name, shape, dt))

        def at(name, value):
            phase, stage = name.split(".") if "." in name else (name, "")
            counts = COUNTS.get(stage, {})
            base = sum(n for p, n in counts.items() if phase in counts and PHASES.index(p) < PHASES.index(phase))
            return S(name), base + value

        def wait(eng, sem, value):
            if not isinstance(value, int) or value > 0:
                eng.wait_ge(*at(sem, value))

        X = sb("x_residual", [P, T, D])
        XN = sb("x_normed", [P, T, D])
        XNT = sb("x_normed_t", [P, N])
        MASK = sb("mask_t", [P, T, N], BF16)
        DIAG = sb("mask_diagonal", [P, T, P], BF16)
        IDENT = sb("identity", [P, P])
        IDB = sb("identity_bf16", [P, P], BF16)
        STATS = sb("ln_stats", [P, T, 6])
        MV = sb("ln_mean_var", [P, T, 2])
        RSTD = sb("ln_rstd", [P, T])
        VEPS = sb("ln_var_eps", [P, T])
        MHALF = sb("minus_half", [P, T])
        SMALL = sb("small", [P, 64])
        MAXES = sb("maxes", [P, 8])
        GMAX = sb("global_maxes", [P, 8])
        AB = sb("scores_ab", [P, T, 8])
        AU = sb("scores_u", [P, T, 8])
        AV = sb("scores_v", [P, T, 8])
        WA = sb("wa", [P, 8])
        WA1B = sb("wa1_broadcast", [P, 4, P])
        RDEN = sb("rden", [P, T])

        w0cat = sb("w0_cat", [P, D])
        w0t = sb("w0_t", [FH, HEADS, P])
        phi0 = sb("phi0", [FH, HEADS, 2])
        bias0 = sb("bias0", [P, D])
        bias0t = sb("bias0_t", [FH, HEADS])
        bias0tb = sb("bias0_t_broadcast", [FH, HEADS, P])
        gw = {}
        for g in (1, 2, 3):
            gw[g] = dict(
                io=sb(f"g{g}_w_in_out", [P, D]), oi=sb(f"g{g}_w_out_in", [P, D]),
                last=sb(f"g{g}_w_last_row", [P, D]), a=sb(f"g{g}_a", [P, 2]),
                wx=sb(f"g{g}_projection", [P, D + 1]))
        b3row = sb("g3_b_row", [P, D])
        b3col = sb("g3_b_col", [P, 1])
        b3cb = sb("g3_b_col_broadcast", [P, P])
        ba3 = sb("g3_b_a", [P, 1])

        ARENA_WORDS = 25088
        arena = sb("arena", [P, ARENA_WORDS])
        top = [0]

        def region(words, at=None):
            a = top[0] if at is None else at
            assert a + words <= ARENA_WORDS, (a, words)
            if at is None:
                top[0] = a + words
            return arena[:, a:a + words]

        PS = ctx.enter_context(nc.psum_tensor("ps", [P, 8, CH], F32))

        ABC = region(HEADS * N).rearrange("p (h n) -> p h n", h=HEADS)
        VH = region(T * HEADS * PARTS * VW // 2).bitcast(BF16).rearrange(
            "p (t h s w) -> p t h s w", t=T, h=HEADS, s=PARTS)
        vf_at = top[0]
        VF = region(T * HEADS * VW).rearrange("p (t h w) -> p t h w", t=T, h=HEADS)
        M1R = 4
        M1 = region(M1R * HB // 2, at=vf_at).bitcast(BF16).rearrange("p (r n) -> p r n", r=M1R)
        hx_at = top[0]
        RM = region(T * HEADS * (FH + 1)).rearrange("p (t h w) -> p t h w", t=T, h=HEADS)
        HX = region(T * D, at=hx_at).rearrange("p (t d) -> p t d", t=T)
        t1_at = top[0]
        T1 = region(2 * TH * PARTS * VW).rearrange("p (b t s w) -> p b t s w", b=2, t=TH, s=PARTS)
        RS = region(TH * VW).rearrange("p (t w) -> p t w", t=TH)
        RD = region(TH * (FH + 1)).rearrange("p (t w) -> p t w", t=TH)
        RE = region(TH * (FH + 1)).rearrange("p (t w) -> p t w", t=TH)
        ADJ = region(2 * N, at=t1_at).bitcast(I32).rearrange("p (b n) -> p b n", b=2)

        top[0] = 0
        GBC = region(N)
        REL = region(2 * N).rearrange("p (b n) -> p b n", b=2)
        QT = region(2 * N).rearrange("p (b n) -> p b n", b=2)
        XV = region(T * D).rearrange("p (t d) -> p t d", t=T)
        XS = region(T * PARTS * D // 2).bitcast(BF16).rearrange("p (t s d) -> p t s d", t=T, s=PARTS)
        ACCT = region(N)

        top[0] = 0
        WR = region(E0 * KH * HID).rearrange("p (e k o) -> p e k o", e=E0, k=KH)
        WST = region(4 * KH * HID).rearrange("p (b k o) -> p b k o", b=4, k=KH)
        WS = region(LAYERS * KH * HID).rearrange("p (l k o) -> p l k o", l=LAYERS, k=KH)
        HT0 = region(KH * N).rearrange("p (k n) -> p k n", k=KH)
        WI = region(HID)
        WO = region(KH * D).rearrange("p (k o) -> p k o", k=KH)
        BRS = region(LAYERS * HID).rearrange("p (l o) -> p l o", l=LAYERS)
        ONEH = region(N)
        HSUM = region(2 * CH).rearrange("p (b n) -> p b n", b=2)
        BI = region(KH)
        BO = region(D)
        ROUTE = region(GROUPS).bitcast(I32)
        ROUTEF = region(GROUPS)
        IOTAF = region(1)
        IOTAI = region(1).bitcast(I32)

        def moe_arena(E, H):
            top[0] = 0
            k = H // P
            dense = dict(
                w1=region(2 * H).rearrange("p (b h) -> p b h", b=2),
                w2=region(2 * k * D).rearrange("p (b k d) -> p b k d", b=2, k=k),
                b1=region(2 * k).rearrange("p (b k) -> p b k", b=2),
                ht=region(2 * k * CH).rearrange("p (b k n) -> p b k n", b=2, k=k)) if E == 8 else {}
            return dict(
                dense, k=k,
                wg=region(E), bg=region(E), b2=region(D),
                lg=region(T * E).rearrange("p (t e) -> p t e", t=T),
                cmb=region(T * E).rearrange("p (t e) -> p t e", t=T),
                oh=region(T * E).rearrange("p (t e) -> p t e", t=T),
                iota=region(E), iotai=region(E).bitcast(I32),
                top8=region(T * 8).rearrange("p (t e) -> p t e", t=T),
                idx=region(T * 8).bitcast(U32).rearrange("p (t e) -> p t e", t=T),
                idxf=region(T * 8).rearrange("p (t e) -> p t e", t=T),
                gt=region(T * 2).rearrange("p (t e) -> p t e", t=T),
                gd=region(T),
                cmbt=region(N))

        MOE = {1: dict(E=8, H=256, act=ACT.Gelu, gated=False, has_bg=True, names=("Wg", "bg", "W1", "b1", "W2", "b2")),
               2: dict(E=64, H=256, act=ACT.Relu, gated=True, has_bg=True, names=("Wr", "br", "W1", "b1", "W2", "b2")),
               3: dict(E=8, H=128, act=ACT.Gelu, gated=True, has_bg=False, names=("router_w", None, "w1", "b1", "w2", "b2"))}
        for m in (1, 3, 2):
            MOE[m].update(moe_arena(MOE[m]["E"], MOE[m]["H"]))

        M2 = MOE[2]
        WRING = region(RING * WROW).rearrange("p (b w) -> p b w", b=RING)
        XG = region(RING * D).rearrange("p (b d) -> p b d", b=RING)
        XGT = region(2 * P).rearrange("p (b n) -> p b n", b=2)
        HTS = region(2 * KH * P).rearrange("p (b k n) -> p b k n", b=2, k=KH)
        YS = region(4 * D).rearrange("p (b d) -> p b d", b=4)
        OHB = region(T * E2 // 2).bitcast(BF16).rearrange("p (t e) -> p t e", t=T)
        CNT = region(T * E2).rearrange("p (t e) -> p t e", t=T)
        BEFORE = region((T + 1) * E2).rearrange("p (t e) -> p t e", t=T + 1)
        RANK = region(T * E2).rearrange("p (t e) -> p t e", t=T)
        SLOT = region(T * E2).rearrange("p (t e) -> p t e", t=T)
        TMP = region(EXTRA * E2)
        MORE = region(E2)
        MOREI = region(E2).bitcast(I32)
        MORECUM = region(E2)
        SHIFT = region(E2)
        EXPERT128 = region(E2)
        ONESF = region(E2)
        SLOTF = region(T * TOPK).rearrange("p (t k) -> p t k", t=T)
        SLOTI = region(T * TOPK).bitcast(I32).rearrange("p (t k) -> p t k", t=T)
        LOI = region(T * TOPK).bitcast(I32).rearrange("p (t k) -> p t k", t=T)
        HII = region(T * TOPK).bitcast(I32).rearrange("p (t k) -> p t k", t=T)
        LOF = region(T * TOPK).rearrange("p (t k) -> p t k", t=T)
        HIF = region(T * TOPK).rearrange("p (t k) -> p t k", t=T)
        EXTRAF = region(EXTRA)
        EXTRAI = region(EXTRA).bitcast(I32)
        TOKI = region(T).bitcast(I32)
        TOKF = region(T)
        COLI = region(P).bitcast(I32)
        COLF = region(P)
        OHLO = region(T * TOPK * P // 2).bitcast(F16).rearrange("p (t k n) -> p t k n", t=T, k=TOPK)
        OHHI = region(T * TOPK * TILES // 2).bitcast(F16).rearrange("p (t k n) -> p t k n", t=T, k=TOPK)
        PERM = region(TILES).bitcast(U32)
        IDXC = region(RING).bitcast(U32)
        IDXW = region(2)
        EARLIER = region(P // 2).bitcast(BF16)
        ONESB = region(P // 2).bitcast(BF16)
        xn_rows = nc.dram_tensor("x_normed_rows", (N, D), F32).ap()
        y_rows = nc.dram_tensor("y_rows", (TILES * P, D), F32).ap()

        block = ctx.enter_context(nc.Block())

        @block.sync
        def _(sp):
            def load(dst, src, sem):
                sp.dma_start(dst, src).then_inc(S(sem), 16)

            load(X[:], dram["x"].rearrange("(t p) d -> p t d", p=P), "x_in")
            load(w0cat[:], dram["w0cat"], "w_g0")
            load(w0t[:], dram["w0t"], "w_g0")
            load(phi0[:], dram["phi0"], "w_g0")
            load(bias0[:], dram["bias0"].partition_broadcast(P), "w_g0")
            load(bias0t[:], dram["bias0t"], "w_g0")
            for g in (1, 2, 3):
                load(gw[g]["io"][:], dram[f"g{g}_io"], f"w_g{g}")
                load(gw[g]["oi"][:], dram[f"g{g}_oi"], f"w_g{g}")
                load(gw[g]["last"][:], dram[f"g{g}_io"][D - 1, :].partition_broadcast(P), f"w_g{g}")
                load(gw[g]["a"][:], dram[f"g{g}_a"], f"w_g{g}")
            load(b3row[:], dram["g3_b"].partition_broadcast(P), "w_g3")
            load(b3col[:], dram["g3_bc"], "w_g3")
            load(ba3[:], dram["g3_ba"].partition_broadcast(P), "w_g3")
            for j in range(T):
                wait(sp, "mask", j - 1)
                load(ADJ[:, j % 2, :], dram["adjt"][j * P:(j + 1) * P, :], f"adj{j % 2}")

            sp.wait_ge(*at("x_done", 1))
            load(WI, dram["f0_wi"], "w_f0")
            load(BI, dram["f0_bi"], "w_f0")
            load(ROUTE[0:1, :], dram["f0_route"].rearrange("(a g) -> a g", a=1), "w_f0")
            load(ROUTEF[0:E0, :].bitcast(I32), dram["f0_route"].partition_broadcast(E0), "w_f0")
            load(WS, dram["f0_ws"].rearrange("l k p o -> p l k o"), "w_f0")
            load(BRS[0:E0, :, :], dram["f0_br"].rearrange("l e o -> e l o"), "w_f0")
            load(BRS[E0:E0 + 1, :, :], dram["f0_bs"].rearrange("l e o -> e l o"), "w_f0")
            load(WO, dram["f0_wo"].rearrange("k p o -> p k o"), "w_f0")
            load(BO, dram["f0_bo"].partition_broadcast(P), "w_f0")
            for l in range(LAYERS):
                if l:
                    sp.wait_ge(*at("f0.staged", GROUPS * l))
                load(WR, dram["f0_wr"][l].rearrange("e k p o -> p e k o"), "w_f0r")

            def sparse():
                def weights(r, extra=False):
                    for b in range(RING):
                        if extra:
                            e = sp.value_load(EXTRAI[0:1, bass.ds(r * RING + b - E2, 1)], min_val=0, max_val=E2 - 1)
                        else:
                            e = r * RING + b
                        sp.dma_start(WRING[:, b, :], dram["f2_w"][bass.ds(e, 1)].rearrange("e p w -> p (e w)")).then_inc(S(f"f2.w{b}"), 16)
                        yield

                def round_(r, extra, last=False):
                    nxt = iter(()) if last else weights(r + 1, extra)
                    for b in range(RING):
                        s = r * RING + b
                        sp.wait_ge(*at("f2.y", s + 1))
                        sp.dma_start(y_rows[bass.ds(s * P, P), :], YS[:, b % 4, :]).then_inc(S(f"f2.y_out{b % 4}"), 16)
                        next(nxt, None)

                for _ in weights(0):
                    pass
                sp.wait_ge(*at("f2.xn", T))
                load(xn_rows.rearrange("(t p) d -> p t d", p=P), XN[:], "f2.rows")
                with sp.Fori(0, E2 // RING - 1) as r:
                    round_(r, False)
                sp.wait_ge(*at("f2.extra", 1))
                with sp.Fori(E2 // RING - 1, ROUNDS - 1) as r:
                    round_(r, True)
                round_(ROUNDS - 1, True, last=True)

            for m, M in MOE.items():
                n1, nb, nw1, nb1, nw2, nb2 = M["names"]
                ph = f"f{m}"
                sp.wait_ge(*at("x_done", 2 * m + 1))
                load(M["wg"], dram[f"{ph}_wg"], f"w_{ph}")
                if M["has_bg"]:
                    load(M["bg"], dram[f"{ph}_bg"].partition_broadcast(P), f"w_{ph}")
                load(M["b2"][0:M["E"], :], dram[f"{ph}_b2"], f"w_{ph}")
                if m == 2:
                    sparse()
                    continue

                def experts(q):
                    for b in range(2):
                        if not (isinstance(q, int) and q == 0):
                            sp.wait_ge(*at(f"{ph}.y_ps", NC * (2 * q + b - 1)))
                        e = 2 * q + b
                        load(M["w1"][:, b, :], dram[f"{ph}_w1"][bass.ds(e, 1)].rearrange("e p h -> p (e h)"), f"{ph}.w{b}")
                        load(M["w2"][:, b, :, :], dram[f"{ph}_w2"][bass.ds(e, 1)].rearrange("e k p d -> p (e k) d"), f"{ph}.w{b}")
                        load(M["b1"][:, b, :], dram[f"{ph}_b1"][bass.ds(e, 1)].rearrange("e p k -> p (e k)"), f"{ph}.w{b}")
                experts(0)
                with sp.Fori(1, M["E"] // 2) as q:
                    experts(q)

            sp.wait_ge(*at("x_done", len(PHASES)))
            sp.dma_start(out.rearrange("(t p) d -> p t d", p=P), X[:]).then_inc(S("stored"), 16)
            sp.wait_ge(*at("stored", 16))

        @block.gpsimd
        def _(pool):
            chain = [0]

            def link(ins):
                chain[0] += 1
                ins.then_inc(S("pool_chain"), 1)
                pool.wait_ge(*at("pool_chain", chain[0]))

            link(nc.gpsimd.memset(IDENT[:], 0.0))
            link(nc.gpsimd.affine_select(out=IDENT[:], in_=IDENT[:], compare_op=ALU.not_equal, fill=1.0,
                                         base=0, pattern=[[-1, P]], channel_multiplier=1))
            nc.gpsimd.memset(MHALF[:], -0.5).then_inc(S("ident"), 1)
            nc.gpsimd.tensor_copy(IDB[:], IDENT[:]).then_inc(S("ident"), 1)

            def rstd(ph):
                pool.wait_ge(*at(f"{ph}.veps", 1))
                if ph == "g0":
                    pool.wait_ge(*at("ident", 1))
                nc.gpsimd.tensor_tensor(RSTD[:], VEPS[:], MHALF[:], ALU.pow).then_inc(S(f"{ph}.rstd"), 1)

            def all_max(ph, n):
                pool.wait_ge(*at(f"{ph}.max", 1))
                nc.gpsimd.partition_all_reduce(GMAX[:, 0:n], MAXES[:, 0:n], P, RMAX).then_inc(S(f"{ph}.gmax"), 1)

            rstd("g0")
            all_max("g0", 8)

            for t in range(T):
                pool.wait_ge(*at("g0.mask_copied", t + 1))
                src = T1.rearrange("p b t s w -> p (b t s w)")[:, (t % TH) * 396:(t % TH + 1) * 396].rearrange(
                    "p (h s w) -> p h s w", h=HEADS, s=PARTS)
                dst = RM[:, t, :, :]
                link(nc.gpsimd.tensor_tensor(dst, src[:, :, 0, :], src[:, :, 1, :], ALU.add))
                nc.gpsimd.tensor_tensor(dst, dst, src[:, :, 2, :], ALU.add).then_inc(S("g0.rm"), 1)

            def head_out(h, ib):
                n = 2 * h + ib
                pool.wait_ge(*at("g0.copied", n + 1))
                tiles = slice(ib * TH, (ib + 1) * TH)
                pool_ops = [
                    (RS, T1[:, ib, :, 0, :], T1[:, ib, :, 1, :], ALU.add),
                    (RS, RS, T1[:, ib, :, 2, :], ALU.add),
                    (RD, RM[:, tiles, h, :], RS[:, :, FH + 1:], ALU.subtract),
                    (RD, RD, AU[:, tiles, 4 + h:5 + h].to_broadcast([P, TH, FH + 1]), ALU.mult),
                    (RE, RS[:, :, 0:FH + 1], AU[:, tiles, h:h + 1].to_broadcast([P, TH, FH + 1]), ALU.mult),
                ]
                if n:
                    pool.wait_ge(*at("g0.rec", n))
                for o, a, b, op in pool_ops:
                    link(nc.gpsimd.tensor_tensor(o, a, b, op))
                link(nc.gpsimd.tensor_tensor(RE, RE, RD, ALU.add))
                nc.gpsimd.nop().then_inc(S("g0.weighed"), 1)
                pool.wait_ge(*at("g0.rec", n + 1))
                link(nc.gpsimd.tensor_tensor(RE[:, :, 0:FH], RE[:, :, 0:FH], RDEN[:, 0:TH].rearrange("p (t a) -> p t a", a=1).to_broadcast([P, TH, FH]), ALU.mult))
                xs = X[:, tiles, h * FH:(h + 1) * FH]
                link(nc.gpsimd.tensor_tensor(xs, xs, RE[:, :, 0:FH], ALU.add))
                nc.gpsimd.nop().then_inc(S("g0.x_added"), 1)

            for h in range(HEADS):
                for ib in range(2):
                    head_out(h, ib)

            def sparse():
                nc.gpsimd.iota(TOKI, pattern=[[P, T]], base=0, channel_multiplier=1).then_inc(S("f2.tok"), 1)
                nc.gpsimd.iota(COLI, pattern=[[1, P]], base=0, channel_multiplier=0).then_inc(S("f2.tok"), 1)
                link(nc.gpsimd.memset(ONESB, 1.0))
                nc.gpsimd.affine_select(out=EARLIER, in_=ONESB, compare_op=ALU.is_gt, fill=0.0, base=0,
                                        pattern=[[1, P]], channel_multiplier=-1).then_inc(S("f2.tok"), 1)
                pool.wait_ge(*at("f2.perm", 1))
                pool.wait_ge(*at("f2.rows", 16))

                def gather(r):
                    for b in range(RING):
                        s = r * RING + b
                        wait(pool, "f2.xg_ps", s - RING + 1)
                        nc.gpsimd.tensor_copy(IDXC[:, b:b + 1], PERM[:, s:s + 1] if isinstance(s, int) else PERM[:, bass.ds(s, 1)]).then_inc(S("f2.idx"), 1)
                        pool.wait_ge(*at("f2.idx", s + 1))
                        nc.gpsimd.tensor_tensor(IDXW[:, 0:1], IDENT[:, 0:1], IDENT[:, 1:2], ALU.add)
                        nc.gpsimd.indirect_dma_start(out=XG[:, b, :], out_offset=None, in_=xn_rows,
                                                     in_offset=bass.IndirectOffsetOnAxis(ap=IDXC[:, b:b + 1], axis=0)).then_inc(S(f"f2.xg{b}"), 16)
                gather(0)
                with pool.Fori(1, ROUNDS) as r:
                    gather(r)
                for b in range(4):
                    pool.wait_ge(*at(f"f2.y_out{b}", 16 * TILES // 4))
                pool.wait_ge(*at("f2.xg_ps", TILES))

                def fetch(r):
                    for b in range(RING):
                        n = r * RING + b
                        wait(pool, "f2.added", n - RING + 1)
                        nc.gpsimd.tensor_copy(IDXC[:, b:b + 1], (SLOTI.rearrange("p t k -> p (t k)")[:, n:n + 1] if isinstance(n, int) else SLOTI.rearrange("p t k -> p (t k)")[:, bass.ds(n, 1)]).bitcast(U32)).then_inc(S("f2.idx"), 1)
                        pool.wait_ge(*at("f2.idx", TILES + n + 1))
                        nc.gpsimd.tensor_tensor(IDXW[:, 0:1], IDENT[:, 0:1], IDENT[:, 1:2], ALU.add)
                        nc.gpsimd.indirect_dma_start(out=XG[:, b, :], out_offset=None, in_=y_rows,
                                                     in_offset=bass.IndirectOffsetOnAxis(ap=IDXC[:, b:b + 1], axis=0)).then_inc(S(f"f2.xg{b}"), 16)
                fetch(0)
                with pool.Fori(1, T * TOPK // RING) as r:
                    fetch(r)

            nc.gpsimd.iota(IOTAI[0:E0, :], pattern=[[0, 1]], base=0, channel_multiplier=1).then_inc(S("f0.iota"), 1)
            rstd("f0")
            for m, M in MOE.items():
                rstd(f"g{m}")
                all_max(f"g{m}", 2)
                pool.wait_ge(*at("x_done", 2 * m + 1))
                nc.gpsimd.iota(M["iotai"], pattern=[[1, M["E"]]], base=0, channel_multiplier=0).then_inc(S(f"f{m}.iota"), 1)
                rstd(f"f{m}")
                if m == 2:
                    sparse()

        @block.tensor
        def _(pe):
            mm = nc.tensor.matmul

            def transpose_x(ph):
                if ph == "g0":
                    pe.wait_ge(*at("ident", 1))
                for t in range(T):
                    pe.wait_ge(*at(f"{ph}.xn", t + 1))
                    nc.tensor.transpose(PS[:, t // TPC, (t % TPC) * P:(t % TPC + 1) * P], XN[:, t, :], IDENT[:]).then_inc(S(f"{ph}.xnt_ps"), 1)

            pe.wait_ge(*at("w_g0", 16 * 5))
            pe.wait_ge(*at("g0.bias_t", 1))
            for h in range(HEADS):
                mm(PS[:, 7, 2 * h:2 * h + 2], w0t[:, h, :], phi0[:, h, :], start=True, stop=True)
                last = mm(PS[:, 7, 8 + 2 * h:10 + 2 * h], bias0tb[:, h, :], phi0[:, h, :], start=True, stop=True)
            last.then_inc(S("g0.wa_ps"), 1)
            transpose_x("g0")
            pe.wait_ge(*at("g0.xnt", NC))
            pe.wait_ge(*at("g0.wa", 2))
            for t in range(T):
                last = mm(PS[:, 6, t * 8:(t + 1) * 8], XNT[:, t * P:(t + 1) * P], WA[:], start=True, stop=True)
            last.then_inc(S("g0.ab_ps"), 1)
            for t in range(T):
                last = mm(PS[:, t // TPC, (t % TPC) * P:(t % TPC + 1) * P], XNT[:, t * P:(t + 1) * P], w0cat[:], start=True, stop=True)
                if t % TPC == TPC - 1:
                    last.then_inc(S("g0.hx_ps"), 1)
            for h in range(HEADS):
                for c in range(NC):
                    n = h * NC + c
                    if n < 4:
                        pe.wait_ge(*at("g0.hx", n + 1))
                    else:
                        pe.wait_ge(*at("g0.abc", n - 3))
                    mm(PS[:, n % 4, :], WA1B[:, h, :], XNT[:, c * CH:(c + 1) * CH], start=True, stop=True).then_inc(S("g0.abc_ps"), 1)

            pe.wait_ge(*at("g0.vh", 3))
            pe.wait_ge(*at("g0.abc", HEADS * NC))
            for r in range(2):
                for j in range(T):
                    if r == 0:
                        pe.wait_ge(*at("mask0", j + 1))
                    for i in range(TH):
                        if r and j == 0:
                            pe.wait_ge(*at("g0.mask_copied", i + 1))
                        t = r * TH + i
                        last = mm(PS[:, i, 0:396].rearrange("p (h s w) -> p h s w", h=HEADS, s=PARTS), MASK[:, j, t * P:(t + 1) * P],
                                  VH[:, j, :, :, FH + 1:], start=(j == 0), stop=(j == T - 1))
                        if j == T - 1:
                            last.then_inc(S("g0.mask_ps"), 1)

            def head_sums(h, first):
                for ib in range(2):
                    for j in range(T):
                        n = (2 * h + ib) * T + j
                        pe.wait_ge(*at("g0.m1", n + 1))
                        if j == 0:
                            if first:
                                pe.wait_ge(*at("g0.mask_copied", T))
                            else:
                                pe.wait_ge(*at("g0.copied", 2 * h + ib - 1))
                        for i in range(TH):
                            last = mm(PS[:, 4 * ib + i // 2, (i % 2) * 198:(i % 2 + 1) * 198], M1[:, n % M1R if isinstance(n, int) else (ib * T + j) % M1R, i * P:(i + 1) * P],
                                      VH[:, j, h, :, :] if isinstance(h, int) else VH[:, j, bass.ds(h, 1), :, :],
                                      start=(j == 0 and i % 2 == 0), stop=(j == T - 1), skip_group_check=True)
                        last.then_inc(S("g0.m1_used"), 1)
            head_sums(0, True)
            with pe.Fori(1, HEADS) as h:
                head_sums(h, False)

            transpose_x("f0")
            pe.wait_ge(*at("f0.xnt", NC))
            pe.wait_ge(*at("w_f0", 16 * 9))
            for c in range(NC):
                for o in range(KH):
                    n = c * KH + o
                    wait(pe, "f0.h", n - 3)
                    mm(PS[:, 4 + n % 4, :], WI[:, o * P:(o + 1) * P], XNT[:, c * CH:(c + 1) * CH], start=True, stop=True).then_inc(S("f0.h_ps"), 1)

            for l in range(LAYERS):
                pe.wait_ge(*at("f0.onehot", 1))
                for c in range(NC):
                    n = l * NC + c
                    pe.wait_ge(*at("f0.h", l * NC * KH + (c + 1) * KH))
                    wait(pe, "f0.sum", KH * (n - 1))
                    cols = slice(c * CH, (c + 1) * CH)
                    bank = 2 * (n % 2)
                    for o in range(KH):
                        for k in range(KH):
                            mm(PS[:, bank + o, :], WS[:, l, k, o * P:(o + 1) * P], HT0[:, k, cols], start=(k == 0), stop=False, skip_group_check=True)
                        mm(PS[:, bank + o, :], BRS[0:E0 + 1, l, o * P:(o + 1) * P], ONEH[0:E0 + 1, cols], start=False, stop=False, skip_group_check=True)
                    for g in range(GPC):
                        gi = n * GPC + g
                        pe.wait_ge(*at("f0.staged", gi + 1))
                        toks = slice(c * CH + g * GT, c * CH + (g + 1) * GT)
                        for o in range(KH):
                            for k in range(KH):
                                last = mm(PS[:, bank + o, g * GT:(g + 1) * GT], WST[:, g % 4, k, o * P:(o + 1) * P], HT0[:, k, toks],
                                          start=False, stop=(k == KH - 1), skip_group_check=True)
                        last.then_inc(S("f0.stage_used"), 1)
            pe.wait_ge(*at("f0.h", (LAYERS + 1) * NC * KH))
            for t in range(T):
                if t % TPC == 0:
                    pe.wait_ge(*at("f0.sum", LAYERS * NC * KH))
                for k in range(KH):
                    last = mm(PS[:, 4 + t // TPC, (t % TPC) * P:(t % TPC + 1) * P], HT0[:, k, t * P:(t + 1) * P], WO[:, k, :],
                              start=(k == 0), stop=(k == KH - 1), skip_group_check=True)
                last.then_inc(S("f0.out_ps"), 1)

            def attention(g):
                ph = f"g{g}"
                W = gw[g]
                pe.wait_ge(*at("x_done", 2 * g))
                pe.wait_ge(*at(f"w_{ph}", 16 * (7 if g == 3 else 4)))
                last = mm(PS[:, 7, 0:2], W["oi"][:], W["a"][:], start=True, stop=True)
                if g == 3:
                    pe.wait_ge(*at("g3.bias_b", 1))
                    last = mm(PS[:, 7, 2:4], b3cb[:], W["a"][:], start=True, stop=True)
                last.then_inc(S(f"{ph}.wa_ps"), 1)
                transpose_x(ph)
                pe.wait_ge(*at(f"{ph}.xnt", NC))
                pe.wait_ge(*at(f"{ph}.wa", 2))
                for t in range(T):
                    last = mm(PS[:, 6, 2 * t:2 * t + 2], XNT[:, t * P:(t + 1) * P], WA[:, 0:2], start=True, stop=True)
                last.then_inc(S(f"{ph}.ab_ps"), 1)
                if g != 2:
                    for c in range(NC):
                        mm(PS[:, c, :], WA1B[:, 0, :], XNT[:, c * CH:(c + 1) * CH], start=True, stop=True).then_inc(S(f"{ph}.abc_ps"), 1)
                    pe.wait_ge(*at(f"{ph}.gbc", NC))
                    pe.wait_ge(*at(f"{ph}.xv", 2))
                    for j in range(T):
                        pe.wait_ge(*at(f"{ph}.q", j + 1))
                        for c in range(NC):
                            last = mm(PS[:, c, :], XV[:, j, :], QT[:, j % 2, c * CH:(c + 1) * CH], start=(j == 0), stop=(j == T - 1))
                        last.then_inc(S(f"{ph}.q_used"), 1)
                else:
                    pe.wait_ge(*at(f"{ph}.xs", PARTS))
                    for j in range(T):
                        for s in range(PARTS):
                            for c in range(NC):
                                last = mm(PS[:, c, :], XS[:, j, s, :], MASK[:, j, c * CH:(c + 1) * CH],
                                          start=(j == 0 and s == 0), stop=(j == T - 1 and s == PARTS - 1))
                    last.then_inc(S(f"{ph}.q_used"), T)
                pe.wait_ge(*at(f"{ph}.wx", 2))
                pe.wait_ge(*at(f"{ph}.acct", NC))
                for t in range(T):
                    mm(PS[:, (4 + t // 3) % 8, (t % 3) * 129:(t % 3 + 1) * 129], ACCT[:, t * P:(t + 1) * P], W["wx"][:], start=True, stop=True).then_inc(S(f"{ph}.out_ps"), 1)

            def sparse():
                for t in range(T):
                    pe.wait_ge(*at("f2.onehot", t + 1))
                    if t == 0:
                        pe.wait_ge(*at("f2.cmbt", NC))
                    for k in range(TOPK):
                        last = mm(PS[:, 0, 0:TILES], OHLO[:, t, k, :], OHHI[:, t, k, :], start=(t == 0 and k == 0), stop=(t == T - 1 and k == TOPK - 1))
                last.then_inc(S("f2.perm_ps"), 1)
                pe.wait_ge(*at("f2.perm", 1))
                pe.wait_ge(*at("f2.acc", 1))

                def turn(r, b):
                    s = r * RING + b
                    pe.wait_ge(*at(f"f2.xg{b}", 16 * r + 16))
                    wait(pe, "f2.xgt", s - 1)
                    nc.tensor.transpose(PS[:, b % 2, 0:P], XG[:, b, :], IDENT[:]).then_inc(S("f2.xg_ps"), 1)

                def hidden(r, b):
                    s = r * RING + b
                    pe.wait_ge(*at("f2.xgt", s + 1))
                    pe.wait_ge(*at(f"f2.w{b}", 16 * r + 16))
                    wait(pe, "f2.hts", s - 1)
                    for k in range(KH):
                        last = mm(PS[:, 2 + b % 2, k * P:(k + 1) * P], WRING[:, b, k * P:(k + 1) * P], XGT[:, b % 2, :], start=True, stop=True)
                    last.then_inc(S("f2.hid_ps"), 1)

                def outputs(r, b):
                    s = r * RING + b
                    pe.wait_ge(*at("f2.hts", s + 1))
                    wait(pe, "f2.y", s - 1)
                    for k in range(KH):
                        last = mm(PS[:, 4 + b % 2, 0:D], HTS[:, b % 2, k, :], WRING[:, b, W2AT + k * D:W2AT + (k + 1) * D], start=(k == 0), stop=(k == KH - 1))
                    last.then_inc(S("f2.out_ps"), 1)

                def round_(r, end=False):
                    for b in range(RING):
                        if b + 2 < RING or not end:
                            turn(r + (b + 2) // RING, (b + 2) % RING)
                        if b + 1 < RING or not end:
                            hidden(r + (b + 1) // RING, (b + 1) % RING)
                        outputs(r, b)
                turn(0, 0)
                turn(0, 1)
                hidden(0, 0)
                round_(0)
                with pe.Fori(1, ROUNDS - 1) as r:
                    round_(r)
                round_(ROUNDS - 1, end=True)

            def moe(m):
                M = MOE[m]
                ph, E, k_, H = f"f{m}", M["E"], M["k"], M["H"]
                pe.wait_ge(*at("x_done", 2 * m + 1))
                transpose_x(ph)
                pe.wait_ge(*at(f"{ph}.xnt", NC))
                pe.wait_ge(*at(f"w_{ph}", 16 * (3 if M["has_bg"] else 2)))
                for t in range(T):
                    bank, col = 4 + t * E // CH, t * E % CH
                    last = mm(PS[:, bank, col:col + E], XNT[:, t * P:(t + 1) * P], M["wg"], start=True, stop=True)
                last.then_inc(S(f"{ph}.lg_ps"), 1)
                pe.wait_ge(*at(f"{ph}.cmb", 1))
                if m == 2:
                    pe.wait_ge(*at("f2.tok", 3))
                    for lhs, bank in ((EARLIER, 4), (ONESB, 6)):
                        for c in range(2):
                            last = mm(PS[:, bank + c, :], lhs, OHB[:, 8 * c:8 * c + 8, :].rearrange("p t e -> p (t e)"), start=True, stop=True)
                    last.then_inc(S("f2.rank_ps"), 1)
                for t in range(T):
                    nc.tensor.transpose(PS[0:E, t // TPC, (t % TPC) * P:(t % TPC + 1) * P], M["cmb"][:, t, :], IDENT[:]).then_inc(S(f"{ph}.cmbt_ps"), 1)
                pe.wait_ge(*at(f"{ph}.cmbt", NC))
                if m == 2:
                    pe.wait_ge(*at("f2.ranked", 2))
                for t in range(T):
                    last = mm(PS[:, 4 + t // TPC, (t % TPC) * P:(t % TPC + 1) * P], M["cmbt"][0:E, t * P:(t + 1) * P], M["b2"][0:E, :], start=True, stop=True)
                    last.then_inc(S(f"{ph}.bias_ps"), 1)
                if m == 2:
                    sparse()
                    return
                pe.wait_ge(*at(f"{ph}.acc", 1))

                def hidden(q, s):
                    b, c = s // NC, s % NC
                    n = q * 2 * NC + s
                    if c == 0:
                        pe.wait_ge(*at(f"{ph}.w{b}", 48 * q + 48))
                    wait(pe, f"{ph}.ht", k_ * (n - 1))
                    for k in range(k_):
                        mm(PS[:, 2 * (s % 2) + k, :], M["w1"][:, b, k * P:(k + 1) * P], XNT[:, c * CH:(c + 1) * CH], start=True, stop=True).then_inc(S(f"{ph}.h_ps"), 1)

                def outputs(q, s):
                    b, c = s // NC, s % NC
                    n = q * 2 * NC + s
                    pe.wait_ge(*at(f"{ph}.ht", k_ * (n + 1)))
                    wait(pe, f"{ph}.y", n - 1)
                    for t in range(TPC):
                        for k in range(k_):
                            last = mm(PS[:, 4 + s % 2, t * P:(t + 1) * P], M["ht"][:, s % 2, k, t * P:(t + 1) * P], M["w2"][:, b, k, :],
                                      start=(k == 0), stop=(k == k_ - 1), skip_group_check=True)
                    last.then_inc(S(f"{ph}.y_ps"), 1)

                def pair(q, end=False):
                    for s in range(2 * NC):
                        if s < 2 * NC - 1:
                            hidden(q, s + 1)
                        elif not end:
                            hidden(q + 1, 0)
                        outputs(q, s)
                hidden(0, 0)
                pair(0)
                if E // 2 > 2:
                    with pe.Fori(1, E // 2 - 1) as q:
                        pair(q)
                pair(E // 2 - 1, end=True)

            for g in (1, 2, 3):
                attention(g)
                moe(g)

        @block.scalar
        def _(act):
            A = nc.scalar.activation

            def copy_xnt(ph):
                for c in range(NC):
                    act.wait_ge(*at(f"{ph}.xnt_ps", TPC * (c + 1)))
                    nc.scalar.copy(XNT[:, c * CH:(c + 1) * CH], PS[:, c, :]).then_inc(S(f"{ph}.xnt"), 1)

            act.wait_ge(*at("g0.wa_ps", 1))
            nc.scalar.copy(WA[:].rearrange("p (s h) -> p s h", s=2), PS[:, 7, 0:8].rearrange("p (h s) -> p s h", s=2)).then_inc(S("g0.wa"), 1)
            nc.scalar.copy(SMALL[:, 0:8].rearrange("p (s h) -> p s h", s=2), PS[:, 7, 8:16].rearrange("p (h s) -> p s h", s=2)).then_inc(S("g0.consts"), 1)
            copy_xnt("g0")
            act.wait_ge(*at("g0.consts", 1))
            for h in range(HEADS):
                for c in range(NC):
                    n = h * NC + c
                    act.wait_ge(*at("g0.abc_ps", n + 1))
                    A(ABC[:, h, c * CH:(c + 1) * CH], PS[:, n % 4, :], ACT.Identity, bias=SMALL[:, h:h + 1]).then_inc(S("g0.abc"), 1)
            act.wait_ge(*at("g0.uv_in", 2))
            A(AV[:, :, 0:4], AV[:, :, 0:4], ACT.Exp).then_inc(S("g0.uv"), 1)
            A(AV[:, :, 4:8], AV[:, :, 4:8], ACT.Exp, scale=SLOPE).then_inc(S("g0.uv"), 1)
            A(AU[:, :, 0:4], AU[:, :, 0:4], ACT.Exp, scale=REST).then_inc(S("g0.uv"), 1)
            A(AU[:, :, 4:8], AU[:, :, 4:8], ACT.Exp, scale=-REST).then_inc(S("g0.uv"), 1)
            for t in range(T):
                act.wait_ge(*at("g0.mask_ps", t + 1))
                if t >= TH:
                    act.wait_ge(*at("g0.rm", t - TH + 1))
                if t == 0:
                    act.wait_ge(*at("mask0", T))
                dst = T1.rearrange("p b t s w -> p (b t s w)")[:, (t % TH) * 396:(t % TH + 1) * 396]
                nc.scalar.copy(dst, PS[:, t % TH, 0:396]).then_inc(S("g0.mask_copied"), 1)
            act.wait_ge(*at("g0.rm", T))
            for n in range(2 * HEADS):
                ib = n % 2
                act.wait_ge(*at("g0.m1_used", (n + 1) * T))
                wait(act, "g0.x_added", n - 1)
                for b in range(4):
                    last = nc.scalar.copy(T1[:, ib, 2 * b:2 * b + 2, :, :].rearrange("p t s w -> p (t s w)"), PS[:, 4 * ib + b, 0:396])
                last.then_inc(S("g0.copied"), 1)

            copy_xnt("f0")
            for c in range(NC):
                for o in range(KH):
                    n = c * KH + o
                    act.wait_ge(*at("f0.h_ps", n + 1))
                    A(HT0[:, o, c * CH:(c + 1) * CH], PS[:, 4 + n % 4, :], ACT.Relu, bias=BI[:, o:o + 1]).then_inc(S("f0.h"), 1)
            for n in range(LAYERS * NC):
                c = n % NC
                for o in range(KH):
                    act.wait_ge(*at("f0.sum", n * KH + o + 1))
                    A(HT0[:, o, c * CH:(c + 1) * CH], HSUM[:, o, :], ACT.Relu).then_inc(S("f0.h"), 1)

            def attention(g):
                ph = f"g{g}"
                act.wait_ge(*at(f"{ph}.wa_ps", 1))
                wn = 4 if g == 3 else 2
                nc.scalar.copy(WA[:, 0:wn], PS[:, 7, 0:wn]).then_inc(S(f"{ph}.wa"), 1)
                copy_xnt(ph)
                if g != 2:
                    act.wait_ge(*at(f"{ph}.shift", 1))
                    for c in range(NC):
                        act.wait_ge(*at(f"{ph}.abc_ps", c + 1))
                        A(GBC[:, c * CH:(c + 1) * CH], PS[:, c, :], ACT.Exp, bias=SMALL[:, 0:1], scale=REST).then_inc(S(f"{ph}.gbc"), 1)
                    A(AU[:, :, 0], AB[:, :, 1], ACT.Exp, bias=SMALL[:, 1:2], scale=REST).then_inc(S(f"{ph}.uv"), 1)
                    A(SMALL[:, 5:6], SMALL[:, 3:4], ACT.Exp).then_inc(S(f"{ph}.uv"), 1)
                    A(AV[:, :, 0], AB[:, :, 1], ACT.Exp, bias=SMALL[:, 2:3], scale=SLOPE).then_inc(S(f"{ph}.uv"), 1)
                    act.wait_ge(*at(f"{ph}.negc", 1))
                    act.wait_ge(*at(f"{ph}.gbc", NC))
                    for j in range(T):
                        wait(act, f"{ph}.q", j - 1)
                        A(REL[:, j % 2, :], GBC, ACT.Relu, bias=SMALL[:, 6:7], scale=AU[:, j, 0:1]).then_inc(S(f"{ph}.rel"), 1)
                else:
                    act.wait_ge(*at(f"{ph}.shift", 1))
                    A(AV[:, :, 0], AB[:, :, 1], ACT.Exp, bias=SMALL[:, 2:3], scale=1.0).then_inc(S(f"{ph}.uv"), 3)
                for c in range(NC):
                    act.wait_ge(*at(f"{ph}.q_used", T))
                    nc.scalar.copy(ACCT[:, c * CH:(c + 1) * CH], PS[:, c, :]).then_inc(S(f"{ph}.acct"), 1)

            def moe(m):
                M = MOE[m]
                ph, E, k_ = f"f{m}", M["E"], M["k"]
                copy_xnt(ph)
                if M["gated"]:
                    act.wait_ge(*at(f"{ph}.gap", 1))
                    A(M["gt"][:, :, 1], M["gt"][:, :, 1], ACT.Exp).then_inc(S(f"{ph}.gap_exp"), 1)
                for c in range(NC):
                    act.wait_ge(*at(f"{ph}.cmbt_ps", TPC * (c + 1)))
                    nc.scalar.copy(M["cmbt"][0:E, c * CH:(c + 1) * CH], PS[0:E, c, :]).then_inc(S(f"{ph}.cmbt"), 1)
                if m == 2:
                    def round_(r):
                        for b in range(RING):
                            s = r * RING + b
                            act.wait_ge(*at("f2.hid_ps", s + 1))
                            wait(act, "f2.out_ps", s - 1)
                            for k in range(KH):
                                last = A(HTS[:, b % 2, k, :], PS[:, 2 + b % 2, k * P:(k + 1) * P], ACT.Relu, bias=WRING[:, b, HID + k:HID + k + 1])
                            last.then_inc(S("f2.hts"), 1)
                    round_(0)
                    with act.Fori(1, ROUNDS) as r:
                        round_(r)
                    return

                def pair(q):
                    for s in range(2 * NC):
                        b, n = s // NC, q * 2 * NC + s
                        wait(act, f"{ph}.y_ps", n - 1)
                        for k in range(k_):
                            act.wait_ge(*at(f"{ph}.h_ps", k_ * n + k + 1))
                            A(M["ht"][:, s % 2, k, :], PS[:, 2 * (s % 2) + k, :], M["act"], bias=M["b1"][:, b, k:k + 1]).then_inc(S(f"{ph}.ht"), 1)
                pair(0)
                with act.Fori(1, E // 2) as q:
                    pair(q)

            for g in (1, 2, 3):
                attention(g)
                moe(g)

        @block.vector
        def _(dve):
            V = nc.vector
            chain = [0]

            def mark(ins):
                chain[0] += 1
                ins.then_inc(S("dve_chain"), 1)
                return chain[0]

            def link(ins):
                dve.wait_ge(*at("dve_chain", mark(ins)))

            def norm(ph):
                for t in range(T):
                    last = V.bn_stats(STATS[:, t, :], X[:, t, :])
                    last.then_inc(S(f"{ph}.stats"), 1)
                for t in range(T):
                    dve.wait_ge(*at(f"{ph}.stats", t + 1))
                    last = V.bn_aggr(MV[:, t, :], STATS[:, t, :])
                link(last)
                V.tensor_scalar(VEPS[:], MV[:, :, 1], EPS, None, ALU.add).then_inc(S(f"{ph}.veps"), 1)
                dve.wait_ge(*at(f"{ph}.rstd", 1))
                for t in range(T):
                    V.tensor_scalar(XN[:, t, :], X[:, t, :], MV[:, t, 0:1], RSTD[:, t:t + 1], ALU.subtract, ALU.mult).then_inc(S(f"{ph}.xn"), 1)

            dve.wait_ge(*at("w_g0", 16 * 5))
            V.tensor_copy(bias0tb[:], bias0t[:].rearrange("p (h a) -> p h a", a=1).to_broadcast([FH, HEADS, P])).then_inc(S("g0.bias_t"), 1)
            dve.wait_ge(*at("x_in", 16))
            norm("g0")
            dve.wait_ge(*at("g0.wa", 1))
            V.tensor_copy(WA1B[:], WA[:, 0:4].rearrange("p (h a) -> p h a", a=1).to_broadcast([P, 4, P])).then_inc(S("g0.wa"), 1)
            dve.wait_ge(*at("g0.ab_ps", 1))
            dve.wait_ge(*at("g0.consts", 1))
            link(V.tensor_tensor(AB[:], PS[:, 6, 0:T * 8].rearrange("p (t c) -> p t c", t=T),
                                 SMALL[:, 0:8].rearrange("p (a c) -> p a c", a=1).to_broadcast([P, T, 8]), ALU.add))
            V.tensor_reduce(MAXES[:, 0:8], AB[:].rearrange("p t c -> p c t"), AX_X, ALU.max).then_inc(S("g0.max"), 1)
            for c in range(NC):
                dve.wait_ge(*at("g0.hx_ps", c + 1))
                V.tensor_tensor(HX[:, c * TPC:(c + 1) * TPC, :], PS[:, c, :].rearrange("p (t d) -> p t d", t=TPC),
                                bias0[:].rearrange("p (a d) -> p a d", a=1).to_broadcast([P, TPC, D]), ALU.add).then_inc(S("g0.hx"), 1)
            dve.wait_ge(*at("g0.gmax", 1))
            bmax = GMAX[:, 4:8].rearrange("p (a c) -> p a c", a=1).to_broadcast([P, T, 4])
            V.tensor_tensor(AV[:, :, 0:4], AB[:, :, 4:8], bmax, ALU.subtract)
            V.tensor_tensor(AV[:, :, 4:8], AB[:, :, 4:8], bmax, ALU.subtract)
            link(V.tensor_tensor(AU[:, :, 0:4], AB[:, :, 0:4], bmax, ALU.add))
            V.tensor_scalar(AU[:, :, 4:8], AU[:, :, 0:4], 0.0, None, ALU.max).then_inc(S("g0.uv_in"), 1)
            dve.wait_ge(*at("g0.uv_in", 1))
            V.tensor_scalar(AU[:, :, 0:4], AU[:, :, 0:4], 0.0, None, ALU.min).then_inc(S("g0.uv_in"), 1)
            link(V.tensor_scalar(AB[:, :, 4:8], AB[:, :, 4:8], -1.0, None, ALU.mult))
            dve.wait_ge(*at("g0.hx", NC))
            dve.wait_ge(*at("g0.uv", 4))
            hx4 = HX.rearrange("p t (h f) -> p t h f", h=HEADS)
            for br in range(2):
                vcol = AV[:, :, 4 * br:4 * br + 4].rearrange("p t (h a) -> p t h a", a=1)
                for t in range(T):
                    V.tensor_tensor(VF[:, t, :, br * (FH + 1):br * (FH + 1) + FH], hx4[:, t], vcol[:, t].to_broadcast([P, HEADS, FH]), ALU.mult)
                last = V.tensor_copy(VF[:, :, :, br * (FH + 1) + FH], AV[:, :, 4 * br:4 * br + 4])
            link(last)
            for s in range(PARTS):
                last = V.tensor_copy(VH[:, :, :, s, :].rearrange("p t h w -> p (t h) w"), VF.rearrange("p t h w -> p (t h) w"))
                last.then_inc(S("g0.vh"), 1)
                if s < PARTS - 1:
                    dve.wait_ge(*at("g0.vh", s + 1))
                    link(V.tensor_tensor(VF.rearrange("p t h w -> p (t h) w"), VF.rearrange("p t h w -> p (t h) w"), VH[:, :, :, s, :].rearrange("p t h w -> p (t h) w"), ALU.subtract))

            dve.wait_ge(*at("ident", 2))
            for j in range(T):
                dve.wait_ge(*at(f"adj{j % 2}", 16 * (j // 2 + 1)))
                V.tensor_scalar(MASK[:, j, :], ADJ[:, j % 2, :], 0, None, ALU.is_gt).then_inc(S("mask"), 1)
                dve.wait_ge(*at("mask", j + 1))
                own = MASK[:, j, j * P:(j + 1) * P]
                link(V.tensor_copy(DIAG[:, j, :], own))
                V.tensor_tensor(own, own, IDB[:], ALU.max).then_inc(S("mask0"), 1)
            dve.wait_ge(*at("mask0", T))
            dve.wait_ge(*at("g0.abc", HEADS * NC))
            dve.wait_ge(*at("g0.vh", PARTS))

            def recip(n):
                dve.wait_ge(*at("g0.weighed", n + 1))
                V.reciprocal(RDEN[:, 0:TH], RE[:, :, FH]).then_inc(S("g0.rec"), 1)

            for h in range(HEADS):
                for ib in range(2):
                    for j in range(T):
                        n = (2 * h + ib) * T + j
                        wait(dve, "g0.m1_used", n - M1R + 1)
                        V.scalar_tensor_tensor(M1[:, n % M1R, :], ABC[:, h, ib * HB:(ib + 1) * HB], AB[:, j, 4 + h:5 + h],
                                               MASK[:, j, ib * HB:(ib + 1) * HB], ALU.is_gt, ALU.mult).then_inc(S("g0.m1"), 1)
                    if 2 * h + ib:
                        recip(2 * h + ib - 1)
            recip(2 * HEADS - 1)
            for j in range(T):
                last = V.tensor_copy(MASK[:, j, j * P:(j + 1) * P], DIAG[:, j, :])
            link(last)
            dve.wait_ge(*at("g0.x_added", 2 * HEADS))
            V.tensor_copy(SMALL[:, 32:33], SMALL[:, 0:1]).then_inc(S("x_done"), 1)

            norm("f0")
            dve.wait_ge(*at("f0.xn", T))
            dve.wait_ge(*at("w_f0", 16 * 9))
            dve.wait_ge(*at("f0.iota", 1))
            link(V.tensor_tensor(X[:], X[:], BO.rearrange("p (a d) -> p a d", a=1).to_broadcast([P, T, D]), ALU.add))
            V.tensor_copy(IOTAF[0:E0, :], IOTAI[0:E0, :])
            link(V.tensor_copy(ROUTEF[0:E0, :], ROUTEF[0:E0, :].bitcast(I32)))
            link(V.memset(ONEH[0:32, :], 1.0))
            V.tensor_scalar(ONEH[0:E0, :].rearrange("p (g t) -> p g t", t=GT), ROUTEF[0:E0, :].rearrange("p (g a) -> p g a", a=1).to_broadcast([E0, GROUPS, GT]),
                            IOTAF[0:E0, 0:1], None, ALU.is_equal).then_inc(S("f0.onehot"), 1)
            for n in range(LAYERS * NC):
                l, c = n // NC, n % NC
                dve.wait_ge(*at("w_f0r", 16 * (l + 1)))
                for g in range(GPC):
                    gi = n * GPC + g
                    wait(dve, "f0.stage_used", gi - 3)
                    with nc.vector.register(f"r{gi}") as _r:
                        e = dve.value_load(ROUTE[0:1, c * GPC + g:c * GPC + g + 1], min_val=0, max_val=E0 - 1)
                        V.tensor_copy(WST[:, g % 4, :, :].rearrange("p k o -> p (k o)"), WR[:, bass.ds(e, 1), :, :].rearrange("p e k o -> p (e k o)")).then_inc(S("f0.staged"), 1)
                for o in range(KH):
                    dve.wait_ge(*at("f0.stage_used", (n + 1) * GPC))
                    wait(dve, "f0.h", NC * KH + (n - 1) * KH + o + 1 if n else 0)
                    V.tensor_tensor(HSUM[:, o, :], PS[:, 2 * (n % 2) + o, :], HT0[:, o, c * CH:(c + 1) * CH], ALU.add).then_inc(S("f0.sum"), 1)
            for t in range(T):
                dve.wait_ge(*at("f0.out_ps", (t // TPC + 1) * TPC))
                last = V.tensor_tensor(X[:, t, :], X[:, t, :], PS[:, 4 + t // TPC, (t % TPC) * P:(t % TPC + 1) * P], ALU.add)
            last.then_inc(S("x_done"), 1)
            dve.wait_ge(*at("x_done", 2))

            def attention(g):
                ph = f"g{g}"
                W = gw[g]
                dve.wait_ge(*at(f"w_{ph}", 16 * (7 if g == 3 else 4)))
                if g == 3:
                    V.tensor_copy(b3cb[:], b3col[:].to_broadcast([P, P])).then_inc(S("g3.bias_b"), 1)
                V.tensor_tensor(W["wx"][:, 0:D], W["io"][:], W["last"][:], ALU.subtract).then_inc(S(f"{ph}.wx"), 1)
                V.tensor_copy(W["wx"][:, D:D + 1], IDENT[:, D - 1:D]).then_inc(S(f"{ph}.wx"), 1)
                norm(ph)
                dve.wait_ge(*at(f"{ph}.wa", 1))
                V.tensor_copy(WA1B[:, 0, :], WA[:, 0:1].to_broadcast([P, P])).then_inc(S(f"{ph}.wa"), 1)
                dve.wait_ge(*at(f"{ph}.ab_ps", 1))
                link(V.tensor_copy(AB[:, :, 0:2], PS[:, 6, 0:2 * T].rearrange("p (t c) -> p t c", t=T)))
                V.tensor_reduce(MAXES[:, 0:2], AB[:, :, 0:2].rearrange("p t c -> p c t"), AX_X, ALU.max).then_inc(S(f"{ph}.max"), 1)
                dve.wait_ge(*at(f"{ph}.gmax", 1))
                if g == 2:
                    V.tensor_scalar(SMALL[:, 2:3], GMAX[:, 1:2], -1.0, None, ALU.mult).then_inc(S(f"{ph}.shift"), 1)
                else:
                    link(V.tensor_tensor(SMALL[:, 4:5], GMAX[:, 0:1], GMAX[:, 1:2], ALU.add))
                    if g == 3:
                        link(V.tensor_tensor(SMALL[:, 4:5], SMALL[:, 4:5], WA[:, 2:3], ALU.add))
                        link(V.tensor_tensor(SMALL[:, 4:5], SMALL[:, 4:5], WA[:, 3:4], ALU.add))
                        link(V.tensor_tensor(SMALL[:, 4:5], SMALL[:, 4:5], ba3[:], ALU.add))
                    V.tensor_scalar(SMALL[:, 0:1], GMAX[:, 0:1], -REST, None, ALU.mult)
                    V.tensor_scalar(SMALL[:, 2:3], GMAX[:, 1:2], -SLOPE, None, ALU.mult)
                    link(V.tensor_scalar(SMALL[:, 3:4], SMALL[:, 4:5], 0.0, -REST, ALU.max, ALU.mult))
                    link(V.tensor_scalar(SMALL[:, 3:4], SMALL[:, 3:4], HEADROOM, None, ALU.add))
                    link(V.tensor_scalar(SMALL[:, 1:2], SMALL[:, 4:5], 0.0, None, ALU.min))
                    link(V.tensor_tensor(SMALL[:, 1:2], SMALL[:, 1:2], GMAX[:, 1:2], ALU.subtract))
                    V.tensor_scalar(SMALL[:, 1:2], SMALL[:, 1:2], REST, HEADROOM, ALU.mult, ALU.add).then_inc(S(f"{ph}.shift"), 1)
                    dve.wait_ge(*at(f"{ph}.uv", 2))
                    V.tensor_scalar(SMALL[:, 6:7], SMALL[:, 5:6], -1.0, None, ALU.mult).then_inc(S(f"{ph}.negc"), 1)
                dve.wait_ge(*at(f"{ph}.uv", 3))
                v = AV[:, :, 0:1]
                V.tensor_tensor(XV[:, :, 0:D - 1], XN[:, :, 0:D - 1], v.to_broadcast([P, T, D - 1]), ALU.mult).then_inc(S(f"{ph}.xv"), 1)
                V.tensor_copy(XV[:, :, D - 1:D], v).then_inc(S(f"{ph}.xv"), 1)
                if g == 2:
                    dve.wait_ge(*at(f"{ph}.xv", 2))
                    for s in range(PARTS):
                        V.tensor_copy(XS[:, :, s, :], XV).then_inc(S(f"{ph}.xs"), 1)
                        if s < PARTS - 1:
                            dve.wait_ge(*at(f"{ph}.xs", s + 1))
                            link(V.tensor_tensor(XV, XV, XS[:, :, s, :], ALU.subtract))
                else:
                    for j in range(T):
                        dve.wait_ge(*at(f"{ph}.rel", j + 1))
                        wait(dve, f"{ph}.q_used", j - 1)
                        V.scalar_tensor_tensor(QT[:, j % 2, :], REL[:, j % 2, :], SMALL[:, 5:6], MASK[:, j, :], ALU.add, ALU.mult).then_inc(S(f"{ph}.q"), 1)
                if g == 3:
                    link(V.tensor_tensor(X[:], X[:], b3row[:].rearrange("p (a d) -> p a d", a=1).to_broadcast([P, T, D]), ALU.add))
                dve.wait_ge(*at(f"{ph}.out_ps", T))
                V.reciprocal(RDEN[:, 0:12].rearrange("p (b t) -> p b t", b=4), PS[:, 4:8, 0:387].rearrange("p b (t c) -> p b t c", c=D + 1)[:, :, :, D])
                V.reciprocal(RDEN[:, 12:15], PS[:, 0, 0:387].rearrange("p (t c) -> p t c", c=D + 1)[:, :, D])
                link(V.reciprocal(RDEN[:, 15:16], PS[:, 1, D:D + 1]))
                for t in range(T):
                    last = V.scalar_tensor_tensor(X[:, t, :], PS[:, (4 + t // 3) % 8, (t % 3) * 129:(t % 3) * 129 + D], RDEN[:, t:t + 1], X[:, t, :], ALU.mult, ALU.add)
                last.then_inc(S("x_done"), 1)
                dve.wait_ge(*at("x_done", 2 * g + 1))

            def route(M, iot):
                link(V.tensor_tensor(RANK, iot, M["idxf"][:, :, 0:1].to_broadcast([P, T, E2]), ALU.is_equal))
                link(V.tensor_tensor(SLOT, iot, M["idxf"][:, :, 1:2].to_broadcast([P, T, E2]), ALU.is_equal))
                link(V.tensor_tensor(OHB, RANK, SLOT, ALU.add))

            def ranks(M):
                dve.wait_ge(*at("f2.rank_ps", 1))
                counts = PS[:, 6:8, :].rearrange("p b (t e) -> p (b t) e", e=E2)
                V.tensor_copy(CNT, counts).then_inc(S("f2.ranked"), 1)
                link(V.memset(BEFORE[:, 0, :], 0.0))
                dve.wait_ge(*at("f2.ranked", 1))
                for t in range(T):
                    link(V.tensor_tensor(BEFORE[:, t + 1, :], BEFORE[:, t, :], CNT[:, t, :], ALU.add))
                V.tensor_tensor(RANK, PS[:, 4:6, :].rearrange("p b (t e) -> p (b t) e", e=E2), BEFORE[:, 0:T, :], ALU.add).then_inc(S("f2.ranked"), 1)
                link(V.tensor_scalar(MORE, BEFORE[:, T, :], float(P - 1), None, ALU.add))
                link(V.tensor_copy(MOREI, MORE))
                link(V.tensor_scalar(MOREI, MOREI, 7, None, ALU.arith_shift_right))
                link(V.tensor_copy(MORE, MOREI))
                link(V.tensor_scalar(MORE, MORE, -1.0, 0.0, ALU.add, ALU.max))
                link(V.memset(ONESF, 1.0))
                link(V.tensor_tensor_scan(MORECUM, ONESF, MORE, 0.0, ALU.mult, ALU.add))
                link(V.tensor_tensor(SHIFT, MORECUM, MORE, ALU.subtract))
                link(V.tensor_tensor(SHIFT, SHIFT, M["iota"], ALU.subtract))
                link(V.tensor_scalar(SHIFT, SHIFT, float(E2 - 1), float(P), ALU.add, ALU.mult))
                link(V.tensor_scalar(EXPERT128, M["iota"], float(P), None, ALU.mult))
                dve.wait_ge(*at("f2.ranked", 2))
                row = lambda a: a.rearrange("p (a e) -> p a e", a=1).to_broadcast([P, T, E2])
                link(V.scalar_tensor_tensor(SLOT, RANK, float(P), row(SHIFT), ALU.is_ge, ALU.mult))
                link(V.tensor_tensor(SLOT, SLOT, RANK, ALU.add))
                link(V.tensor_tensor(SLOT, SLOT, row(EXPERT128), ALU.add))
                iot = row(M["iota"])
                for k in range(TOPK):
                    link(V.tensor_tensor(RANK, iot, M["idxf"][:, :, k:k + 1].to_broadcast([P, T, E2]), ALU.is_equal))
                    link(V.tensor_tensor(RANK, RANK, SLOT, ALU.mult))
                    link(V.tensor_reduce(SLOTF[:, :, k], RANK, AX_X, ALU.add))
                link(V.tensor_copy(SLOTI, SLOTF))
                V.tensor_scalar(LOI, SLOTI, P - 1, None, ALU.bitwise_and)
                link(V.tensor_scalar(HII, SLOTI, 7, None, ALU.arith_shift_right))
                V.tensor_copy(LOF, LOI)
                V.tensor_copy(HIF, HII)
                dve.wait_ge(*at("f2.tok", 3))
                V.tensor_copy(TOKF, TOKI)
                link(V.tensor_copy(COLF, COLI))
                for t in range(T):
                    for k in range(TOPK):
                        V.tensor_scalar(OHLO[:, t, k, :], COLF, LOF[:, t, k:k + 1], None, ALU.is_equal)
                        last = V.tensor_scalar(OHHI[:, t, k, :], COLF[:, 0:TILES], HIF[:, t, k:k + 1], TOKF[:, t:t + 1], ALU.is_equal, ALU.mult)
                    last.then_inc(S("f2.onehot"), 1)
                cum = MORECUM.rearrange("p (a e) -> p a e", a=1).to_broadcast([P, EXTRA, E2])
                num = COLF[:, 0:EXTRA].rearrange("p (o a) -> p o a", a=1).to_broadcast([P, EXTRA, E2])
                tmp = TMP.rearrange("p (o e) -> p o e", o=EXTRA)
                link(V.tensor_tensor(tmp, cum, num, ALU.is_le))
                link(V.tensor_reduce(EXTRAF, tmp, AX_X, ALU.add))
                link(V.tensor_scalar(EXTRAF, EXTRAF, float(E2 - 1), None, ALU.min))
                V.tensor_copy(EXTRAI, EXTRAF).then_inc(S("f2.extra"), 1)

            def sparse(M):
                dve.wait_ge(*at("f2.perm_ps", 1))
                V.tensor_copy(PERM, PS[:, 0, 0:TILES]).then_inc(S("f2.perm"), 1)

                def turned(r, b):
                    s = r * RING + b
                    dve.wait_ge(*at("f2.xg_ps", s + 1))
                    wait(dve, "f2.hid_ps", s - 1)
                    V.tensor_copy(XGT[:, b % 2, :], PS[:, b % 2, 0:P]).then_inc(S("f2.xgt"), 1)

                def round_(r, end=False):
                    for b in range(RING):
                        s = r * RING + b
                        if b + 2 < RING or not end:
                            turned(r + (b + 2) // RING, (b + 2) % RING)
                        dve.wait_ge(*at("f2.out_ps", s + 1))
                        if not (isinstance(r, int) and s < 4):
                            dve.wait_ge(*at(f"f2.y_out{b % 4}", 32 * r + 16 * (b // 4)))
                        V.tensor_copy(YS[:, b % 4, :], PS[:, 4 + b % 2, 0:D]).then_inc(S("f2.y"), 1)
                turned(0, 0)
                turned(0, 1)
                round_(0)
                with dve.Fori(1, ROUNDS - 1) as r:
                    round_(r)
                round_(ROUNDS - 1, end=True)

                dve.wait_ge(*at("f2.acc", 1))

                def add(r):
                    for b in range(RING):
                        n = r * RING + b
                        t, k = r * (RING // TOPK) + b // TOPK, b % TOPK
                        dve.wait_ge(*at(f"f2.xg{b}", 16 * ROUNDS + 16 * r + 16))
                        if k:
                            dve.wait_ge(*at("f2.added", n))
                        x = X[:, bass.ds(t, 1), :].rearrange("p a d -> p (a d)")
                        V.scalar_tensor_tensor(x, XG[:, b, :], M["gt"][:, bass.ds(t, 1), k], x, ALU.mult, ALU.add).then_inc(S("f2.added"), 1)
                with dve.Fori(0, T * TOPK // RING) as r:
                    add(r)
                dve.wait_ge(*at("f2.added", T * TOPK))
                V.tensor_copy(SMALL[:, 32:33], IDENT[:, 0:1]).then_inc(S("x_done"), 1)

            def moe(m):
                M = MOE[m]
                ph, E = f"f{m}", M["E"]
                norm(ph)
                dve.wait_ge(*at(f"{ph}.iota", 1))
                link(V.tensor_copy(M["iota"], M["iotai"]))
                dve.wait_ge(*at(f"{ph}.lg_ps", 1))
                nb = (T * E + CH - 1) // CH
                lgps = PS[:, 4:4 + nb, :].rearrange("p b n -> p (b n)")[:, 0:T * E].rearrange("p (t e) -> p t e", t=T)
                if M["has_bg"]:
                    link(V.tensor_tensor(M["lg"], lgps, M["bg"].rearrange("p (a e) -> p a e", a=1).to_broadcast([P, T, E]), ALU.add))
                else:
                    link(V.tensor_copy(M["lg"], lgps))
                for t in range(T):
                    V.max(M["top8"][:, t, :], M["lg"][:, t, :]).then_inc(S(f"{ph}.top"), 1)
                for t in range(T):
                    dve.wait_ge(*at(f"{ph}.top", t + 1))
                    last = V.max_index(M["idx"][:, t, :], M["top8"][:, t, :], M["lg"][:, t, :])
                link(last)
                link(V.tensor_copy(M["idxf"], M["idx"]))
                if M["gated"]:
                    V.tensor_tensor(M["gt"][:, :, 1], M["top8"][:, :, 1], M["top8"][:, :, 0], ALU.subtract).then_inc(S(f"{ph}.gap"), 1)
                    dve.wait_ge(*at(f"{ph}.gap_exp", 1))
                    link(V.tensor_scalar(M["gd"], M["gt"][:, :, 1], 1.0, None, ALU.add))
                    link(V.reciprocal(M["gt"][:, :, 0], M["gd"]))
                    link(V.tensor_tensor(M["gt"][:, :, 1], M["gt"][:, :, 1], M["gt"][:, :, 0], ALU.mult))
                iot = M["iota"].rearrange("p (a e) -> p a e", a=1).to_broadcast([P, T, E])
                for k, dst in ((0, M["cmb"]), (1, M["oh"])):
                    link(V.tensor_tensor(dst, iot, M["idxf"][:, :, k:k + 1].to_broadcast([P, T, E]), ALU.is_equal))
                    if M["gated"]:
                        link(V.tensor_tensor(dst, dst, M["gt"][:, :, k:k + 1].to_broadcast([P, T, E]), ALU.mult))
                if m == 2:
                    route(M, iot)
                V.tensor_tensor(M["cmb"], M["cmb"], M["oh"], ALU.add).then_inc(S(f"{ph}.cmb"), 1)
                if m == 2:
                    ranks(M)
                if m == 3:
                    link(V.tensor_tensor(X[:], X[:], XN[:], ALU.add))
                for c in range(NC):
                    dve.wait_ge(*at(f"{ph}.bias_ps", TPC * (c + 1)))
                    xs = X[:, c * TPC:(c + 1) * TPC, :]
                    last = V.tensor_tensor(xs, xs, PS[:, 4 + c, :].rearrange("p (t d) -> p t d", t=TPC), ALU.add)
                last.then_inc(S(f"{ph}.acc"), 1)
                if m == 2:
                    sparse(M)
                    return

                def pair(q):
                    for s in range(2 * NC):
                        b, c, n = s // NC, s % NC, q * 2 * NC + s
                        dve.wait_ge(*at(f"{ph}.y_ps", n + 1))
                        if isinstance(n, int) and n < NC:
                            dve.wait_ge(*at(f"{ph}.acc", 1))
                            dve.wait_ge(*at(f"{ph}.cmb", 1))
                        else:
                            dve.wait_ge(*at(f"{ph}.y", n - NC + 1))
                        for t in range(TPC):
                            tt = c * TPC + t
                            last = V.scalar_tensor_tensor(X[:, tt, :], PS[:, 4 + s % 2, t * P:(t + 1) * P], M["cmb"][:, tt, bass.ds(2 * q + b, 1)], X[:, tt, :], ALU.mult, ALU.add)
                        last.then_inc(S(f"{ph}.y"), 1)
                pair(0)
                with dve.Fori(1, E // 2) as q:
                    pair(q)
                dve.wait_ge(*at(f"{ph}.y", E * NC))
                V.tensor_copy(SMALL[:, 32:33], IDENT[:, 0:1]).then_inc(S("x_done"), 1)

            for g in (1, 2, 3):
                attention(g)
                moe(g)


def kernel(**inputs):
    import numpy as np
    import concourse.bacc as bacc
    from concourse.bass_utils import run_bass_kernel_spmd as run

    a = {k: np.asarray(v) for k, v in inputs.items()}
    lay = {
        "x": a["x"],
        "adjt": a["adj"].T,
        "w0cat": a["L0_gnn_weights"].transpose(1, 0, 2).reshape(D, D),
        "w0t": a["L0_gnn_weights"].transpose(2, 0, 1),
        "phi0": a["L0_gnn_phis"][:, :, 0].reshape(HEADS, 2, FH).transpose(2, 0, 1),
        "bias0": a["L0_gnn_biases"].reshape(D),
        "bias0t": a["L0_gnn_biases"].T,
        "g1_io": a["L1_gnn_W"], "g1_oi": a["L1_gnn_W"].T, "g1_a": a["L1_gnn_a"].reshape(2, D).T,
        "g2_io": a["L2_gnn_W"].T, "g2_oi": a["L2_gnn_W"], "g2_a": a["L2_gnn_a"].reshape(2, D).T,
        "g3_io": a["L3_gnn_W"].T, "g3_oi": a["L3_gnn_W"], "g3_a": a["L3_gnn_a_vec"].reshape(2, D).T,
        "g3_b": a["L3_gnn_b_W"], "g3_bc": a["L3_gnn_b_W"].reshape(D, 1), "g3_ba": a["L3_gnn_b_a"],
        "f0_wi": a["L0_ffn_Wi"].T, "f0_bi": a["L0_ffn_bi"].reshape(KH, P).T,
        "f0_route": a["L0_ffn_route_id"],
        "f0_ws": a["L0_ffn_Ws"][:, 0].transpose(0, 2, 1).reshape(LAYERS, KH, P, HID),
        "f0_br": a["L0_ffn_br"], "f0_bs": a["L0_ffn_bs"],
        "f0_wr": a["L0_ffn_Wr"].transpose(0, 1, 3, 2).reshape(LAYERS, E0, KH, P, HID),
        "f0_wo": a["L0_ffn_Wo"].T.reshape(KH, P, D), "f0_bo": a["L0_ffn_bo"],
    }
    for m, (wg, bg, w1, b1, w2, b2) in ((1, ("Wg", "bg", "W1", "b1", "W2", "b2")), (2, ("Wr", "br", "W1", "b1", "W2", "b2")),
                                        (3, ("router_w", None, "w1", "b1", "w2", "b2"))):
        f = lambda name: a[f"L{m}_ffn_{name}"]
        E, _, H = f(w1).shape
        lay[f"f{m}_wg"] = f(wg).T if m == 3 else f(wg)
        if bg:
            lay[f"f{m}_bg"] = f(bg)
        b1t = f(b1).reshape(E, H // P, P).transpose(0, 2, 1)
        w2k = f(w2).reshape(E, H // P, P, D)
        if m == 2:
            lay["f2_w"] = np.concatenate([f(w1), b1t, w2k.transpose(0, 2, 1, 3).reshape(E, P, H // P * D)], axis=2)
        else:
            lay[f"f{m}_w1"], lay[f"f{m}_b1"], lay[f"f{m}_w2"] = f(w1), b1t, w2k
        lay[f"f{m}_b2"] = f(b2)

    nc = bacc.Bacc("TRN2", target_bir_lowering=False, num_devices=1)
    arrays, dram = {}, {}
    for name, v in lay.items():
        v = np.ascontiguousarray(v)
        arrays[f"in_{name}"] = v
        dram[name] = nc.dram_tensor(f"in_{name}", v.shape, mybir.dt.from_np(v.dtype), kind="ExternalInput").ap()
    out = nc.dram_tensor("out_0", (N, D), F32, kind="ExternalOutput").ap()
    build(nc, dram, out)
    r = run(nc, [arrays], core_ids=[0])
    return r.results[0]["out_0"]
```

```python
from contextlib import ExitStack

import concourse.bass as bass
from concourse import mybir

ALU = mybir.AluOpType
ACT = mybir.ActivationFunctionType
F32 = mybir.dt.float32
BF16 = mybir.dt.bfloat16
I32 = mybir.dt.int32
U32 = mybir.dt.uint32
AX_X = mybir.AxisListType.X
RMAX = bass.bass_isa.ReduceOp.max

P = 128
N = 2048
D = 128
T = N // P
CH = 512
NC = N // CH
TPC = CH // P
EPS = 1e-5
SLOPE = 0.2
REST = 1.0 - SLOPE
HEADROOM = 40.0
BIG = 2.0 ** 100

HEADS = 4
FH = D // HEADS
VW = 2 * (FH + 1)
PARTS = 3
HB = N // 2
TH = HB // P

HID = 256
KH = HID // P
LAYERS = 2
E0 = 16
GROUPS = 64
GT = N // GROUPS
GPC = CH // GT


HI_BY_POOL = 10
BY_SCALAR = [j for j in range(T) if j % 8 not in (0, 3, 6)]

PHASES = ["g0", "f0", "g1", "f1", "g2", "f2", "g3", "f3"]
EXPERTS = {"f1": (8, 2), "f3": (8, 1)}


def stage_counts():
    counts = {}
    for stage, n in dict(stats=T, veps=1, rstd=1, xn=T, xnt_ps=T, xnt=NC).items():
        counts[stage] = {p: n for p in PHASES}
    for stage, n in dict(max=1, gmax=1).items():
        counts[stage] = {p: n for p in ("g0", "g1", "g2", "g3")}
    for stage, n in dict(wa_ps=1, wa=2, ab_ps=1, wx=2, shift=1, uv=3, xv=2, q_used=T, acct=NC, out_ps=T).items():
        counts[stage] = {p: n for p in ("g1", "g2", "g3")}
    for stage, n in dict(abc_ps=NC, gbc=NC, negc=1, rel=T, q=T).items():
        counts[stage] = {p: n for p in ("g1", "g3")}
    for stage, n in dict(lg_ps=1, top=T, cmb=1, cmbt_ps=T, cmbt=NC, bias_ps=T, acc=1, iota=1).items():
        counts[stage] = {p: n for p in ("f1", "f2", "f3")}
    for stage, n in dict(gap=1, gap_exp=1).items():
        counts[stage] = {p: n for p in ("f2", "f3")}
    for stage, n in dict(w0=24, w1=24, y_ps=NC, y=NC).items():
        counts[stage] = {p: n * e for p, (e, _) in EXPERTS.items()}
    for stage in ("h_ps", "ht"):
        counts[stage] = {p: NC * e * k for p, (e, k) in EXPERTS.items()}
    return counts


COUNTS = stage_counts()

E2 = 64
TOPK = 2
EXTRA = TOPK * N // P
TILES = E2 + EXTRA
RING = 8
ROUNDS = TILES // RING
W2AT = HID + KH
WROW = W2AT + KH * D
F16 = mybir.dt.float16


def build(nc, dram, out):
    ctx = ExitStack()
    with ctx:
        sems = {}

        def S(name):
            stage = name.split(".")[-1]
            if "." in name and name.split(".")[0] in COUNTS.get(stage, {}):
                name = stage
            if name not in sems:
                sems[name] = ctx.enter_context(nc.semaphore(name.replace(".", "_")))
            return sems[name]

        def sb(name, shape, dt=F32):
            return ctx.enter_context(nc.sbuf_tensor(name, shape, dt))

        def at(name, value):
            phase, stage = name.split(".") if "." in name else (name, "")
            counts = COUNTS.get(stage, {})
            base = sum(n for p, n in counts.items() if phase in counts and PHASES.index(p) < PHASES.index(phase))
            return S(name), base + value

        def wait(eng, sem, value):
            if not isinstance(value, int) or value > 0:
                eng.wait_ge(*at(sem, value))

        X = sb("x_residual", [P, T, D])
        XN = sb("x_normed", [P, T, D])
        XNT = sb("x_normed_t", [P, N])
        MASK = sb("mask_t", [P, T, N], BF16)
        DIAG = sb("mask_diagonal", [P, T, P], BF16)
        IDENT = sb("identity", [P, P])
        IDB = sb("identity_bf16", [P, P], BF16)
        STATS = sb("ln_stats", [P, T, 6])
        MV = sb("ln_mean_var", [P, T, 2])
        RSTD = sb("ln_rstd", [P, T])
        VEPS = sb("ln_var_eps", [P, T])
        MHALF = sb("minus_half", [P, T])
        SMALL = sb("small", [P, 64])
        MAXES = sb("maxes", [P, 8])
        GMAX = sb("global_maxes", [P, 8])
        AB = sb("scores_ab", [P, T, 8])
        AU = sb("scores_u", [P, T, 8])
        AV = sb("scores_v", [P, T, 8])
        WA = sb("wa", [P, 8])
        WA1B = sb("wa1_broadcast", [P, 4, P])
        RDEN = sb("rden", [P, T])

        w0cat = sb("w0_cat", [P, D])
        w0t = sb("w0_t", [FH, HEADS, P])
        phi0 = sb("phi0", [FH, HEADS, 2])
        bias0 = sb("bias0", [P, D])
        bias0t = sb("bias0_t", [FH, HEADS])
        bias0tb = sb("bias0_t_broadcast", [FH, HEADS, P])
        gw, gwall = {}, {}
        for g in (1, 2, 3):
            gwall[g] = sb(f"g{g}_weights", [P, 4 * D + 3])
            gw[g] = dict(io=gwall[g][:, 0:D], oi=gwall[g][:, D:2 * D], last=gwall[g][:, 2 * D:3 * D],
                         wx=gwall[g][:, 3 * D:4 * D + 1], a=gwall[g][:, 4 * D + 1:4 * D + 3])
        b3row = sb("g3_b_row", [P, D])
        b3col = sb("g3_b_col", [P, 1])
        b3cb = sb("g3_b_col_broadcast", [P, P])
        ba3 = sb("g3_b_a", [P, 1])

        ARENA_WORDS = 25088
        arena = sb("arena", [P, ARENA_WORDS])
        top = [0]

        def region(words, at=None):
            a = top[0] if at is None else at
            assert a + words <= ARENA_WORDS, (a, words)
            if at is None:
                top[0] = a + words
            return arena[:, a:a + words]

        PS = ctx.enter_context(nc.psum_tensor("ps", [P, 8, CH], F32))

        ABC = region(HEADS * N).rearrange("p (h n) -> p h n", h=HEADS)
        VH = region(T * HEADS * PARTS * VW // 2).bitcast(BF16).rearrange(
            "p (t h s w) -> p t h s w", t=T, h=HEADS, s=PARTS)
        vf_at = top[0]
        VF = region(T * HEADS * VW).rearrange("p (t h w) -> p t h w", t=T, h=HEADS)
        M1R = 4
        M1 = region(M1R * HB // 2, at=vf_at).bitcast(BF16).rearrange("p (r n) -> p r n", r=M1R)
        REACH = region(4 * HB // 2, at=vf_at + M1R * HB // 2).bitcast(BF16).rearrange("p (r n) -> p r n", r=4)
        NB = region(T * HEADS, at=vf_at + M1R * HB // 2 + 2 * HB).rearrange("p (t h) -> p t h", t=T)
        hx_at = top[0]
        RM = region(T * HEADS * (FH + 1)).rearrange("p (t h w) -> p t h w", t=T, h=HEADS)
        HX = region(T * D, at=hx_at).rearrange("p (t d) -> p t d", t=T)
        t1_at = top[0]
        T1 = region(2 * TH * PARTS * VW).rearrange("p (b t s w) -> p b t s w", b=2, t=TH, s=PARTS)
        RS = region(TH * VW).rearrange("p (t w) -> p t w", t=TH)
        RD = region(TH * (FH + 1)).rearrange("p (t w) -> p t w", t=TH)
        RE = region(TH * (FH + 1)).rearrange("p (t w) -> p t w", t=TH)
        ADJ = region(2 * N, at=t1_at).bitcast(I32).rearrange("p (b n) -> p b n", b=2)

        top[0] = 0
        GBC = region(N)
        REL = region(2 * N).rearrange("p (b n) -> p b n", b=2)
        QT = region(2 * N).rearrange("p (b n) -> p b n", b=2)
        XV = region(T * D).rearrange("p (t d) -> p t d", t=T)
        XS = region(T * PARTS * D // 2).bitcast(BF16).rearrange("p (t s d) -> p t s d", t=T, s=PARTS)
        ACCT = region(N)

        top[0] = 0
        WR = region(LAYERS * E0 * KH * HID).rearrange("p (l e k o) -> p l e k o", l=LAYERS, e=E0, k=KH)
        WST01 = region(2 * KH * HID).rearrange("p (b k o) -> p b k o", b=2, k=KH)
        WST = [WST01[:, 0], WST01[:, 1]] + [gwall[g][:, 0:KH * HID].rearrange("p (k o) -> p k o", k=KH) for g in (2, 3)]
        HT0 = region(KH * N).rearrange("p (k n) -> p k n", k=KH)
        HIGH = region(T // 2 * HID).rearrange("p (t o) -> p t o", t=T // 2)
        WI = region(HID)
        WO = region(KH * D).rearrange("p (k o) -> p k o", k=KH)
        BRS = region(LAYERS * HID).rearrange("p (l o) -> p l o", l=LAYERS)
        BI = region(HID)
        ROUTE = region(GROUPS).bitcast(I32)
        ROUTEF = region(GROUPS)
        IOTAF = region(1)
        IOTAI = region(1).bitcast(I32)
        LOW = XN[:].rearrange("p t d -> p (t d)").rearrange("p (t o) -> p t o", t=T // 2)
        ONEH = XNT[:, :]
        WS = DIAG[:].rearrange("p t n -> p (t n)").bitcast(F32).rearrange("p (l k o) -> p l k o", l=LAYERS, k=KH)
        HSUM = WA1B[:].rearrange("p a b -> p (a b)").rearrange("p (b o) -> p b o", b=2)
        BO = bias0[:]

        def HTOK(t):
            return LOW[:, t, :] if t < T // 2 else HIGH[:, t - T // 2, :]

        def moe_arena(E, H):
            top[0] = 0
            k = H // P
            dense = dict(
                w1=region(2 * H).rearrange("p (b h) -> p b h", b=2),
                w2=region(2 * k * D).rearrange("p (b k d) -> p b k d", b=2, k=k),
                b1=region(2 * k).rearrange("p (b k) -> p b k", b=2),
                ht=region(2 * k * CH).rearrange("p (b k n) -> p b k n", b=2, k=k)) if E == 8 else {}
            return dict(
                dense, k=k,
                wg=region(E), bg=region(E), b2=region(D),
                lg=region(T * E).rearrange("p (t e) -> p t e", t=T),
                cmb=region(T * E).rearrange("p (t e) -> p t e", t=T),
                oh=region(T * E).rearrange("p (t e) -> p t e", t=T),
                iota=region(E), iotai=region(E).bitcast(I32),
                top8=region(T * 8).rearrange("p (t e) -> p t e", t=T),
                idx=region(T * 8).bitcast(U32).rearrange("p (t e) -> p t e", t=T),
                idxf=region(T * 8).rearrange("p (t e) -> p t e", t=T),
                gt=region(T * 2).rearrange("p (t e) -> p t e", t=T),
                gd=region(T),
                cmbt=region(N))

        MOE = {1: dict(E=8, H=256, act=ACT.Gelu, gated=False, has_bg=True),
               2: dict(E=64, H=256, act=ACT.Relu, gated=True, has_bg=True),
               3: dict(E=8, H=128, act=ACT.Gelu, gated=True, has_bg=False)}
        for m in (1, 3, 2):
            MOE[m].update(moe_arena(MOE[m]["E"], MOE[m]["H"]))

        M2 = MOE[2]
        WRING = region(RING * WROW).rearrange("p (b w) -> p b w", b=RING)
        XG = region(RING * D).rearrange("p (b d) -> p b d", b=RING)
        XGT = region(2 * P).rearrange("p (b n) -> p b n", b=2)
        HTS = region(2 * KH * P).rearrange("p (b k n) -> p b k n", b=2, k=KH)
        YS = region(4 * D).rearrange("p (b d) -> p b d", b=4)
        OHB = region(T * E2 // 2).bitcast(BF16).rearrange("p (t e) -> p t e", t=T)
        CNT = region(T * E2).rearrange("p (t e) -> p t e", t=T)
        BEFORE = region((T + 1) * E2).rearrange("p (t e) -> p t e", t=T + 1)
        RANK = region(T * E2).rearrange("p (t e) -> p t e", t=T)
        SLOT = region(T * E2).rearrange("p (t e) -> p t e", t=T)
        TMP = region(EXTRA * E2)
        MORE = region(E2)
        MOREI = region(E2).bitcast(I32)
        MORECUM = region(E2)
        SHIFT = region(E2)
        EXPERT128 = region(E2)
        ONESF = region(E2)
        SLOTF = region(T * TOPK).rearrange("p (t k) -> p t k", t=T)
        SLOTI = region(T * TOPK).bitcast(I32).rearrange("p (t k) -> p t k", t=T)
        LOI = region(T * TOPK).bitcast(I32).rearrange("p (t k) -> p t k", t=T)
        HII = region(T * TOPK).bitcast(I32).rearrange("p (t k) -> p t k", t=T)
        LOF = region(T * TOPK).rearrange("p (t k) -> p t k", t=T)
        HIF = region(T * TOPK).rearrange("p (t k) -> p t k", t=T)
        EXTRAF = region(EXTRA)
        EXTRAI = region(EXTRA).bitcast(I32)
        TOKI = region(T).bitcast(I32)
        TOKF = region(T)
        COLI = region(P).bitcast(I32)
        COLF = region(P)
        OHLO = region(T * TOPK * P // 2).bitcast(F16).rearrange("p (t k n) -> p t k n", t=T, k=TOPK)
        OHHI = region(T * TOPK * TILES // 2).bitcast(F16).rearrange("p (t k n) -> p t k n", t=T, k=TOPK)
        PERM = region(TILES).bitcast(U32)
        EARLIER = region(P // 2).bitcast(BF16)
        ONESB = region(P // 2).bitcast(BF16)
        xn_rows = nc.dram_tensor("x_normed_rows", (N, D), F32).ap()
        y_rows = nc.dram_tensor("y_rows", (TILES * P, D), F32).ap()

        block = ctx.enter_context(nc.Block())

        @block.sync
        def _(sp):
            def load(dst, src, sem):
                sp.dma_start(dst, src).then_inc(S(sem), 16)

            load(X[:], dram["x"].rearrange("(t p) d -> p t d", p=P), "x_in")
            load(w0cat[:], dram["w0cat"], "w_g0")
            load(w0t[:], dram["w0t"], "w_g0")
            load(phi0[:], dram["phi0"], "w_g0")
            load(bias0[:], dram["bias0"].partition_broadcast(P), "w_g0")
            load(bias0t[:], dram["bias0t"], "w_g0")

            def attention_weights(g):
                load(gw[g]["io"], dram[f"g{g}_io"], f"w_g{g}")
                load(gw[g]["oi"], dram[f"g{g}_oi"], f"w_g{g}")
                load(gw[g]["last"], dram[f"g{g}_io"][D - 1, :].partition_broadcast(P), f"w_g{g}")
                load(gw[g]["a"], dram[f"g{g}_a"], f"w_g{g}")
            attention_weights(1)
            load(b3row[:], dram["g3_b"].partition_broadcast(P), "w_g3")
            load(b3col[:], dram["g3_bc"], "w_g3")
            load(ba3[:], dram["g3_ba"].partition_broadcast(P), "w_g3")
            for j in range(T):
                wait(sp, "mask", j - 1)
                load(ADJ[:, j % 2, :], dram["adjt"][j * P:(j + 1) * P, :], f"adj{j % 2}")

            sp.wait_ge(*at("x_done", 1))
            load(WI, dram["f0_wi"], "w_f0")
            load(BI, dram["f0_bi"].partition_broadcast(P), "w_f0")
            load(ROUTE[0:1, :], dram["f0_route"].rearrange("(a g) -> a g", a=1), "w_f0")
            load(ROUTEF[0:E0, :].bitcast(I32), dram["f0_route"].partition_broadcast(E0), "w_f0")
            load(WS, dram["f0_ws"].rearrange("l k p o -> p l k o"), "w_f0")
            load(BRS[0:E0, :, :], dram["f0_br"].rearrange("l e o -> e l o"), "w_f0")
            load(BRS[E0:E0 + 1, :, :], dram["f0_bs"].rearrange("l e o -> e l o"), "w_f0")
            load(WO, dram["f0_wo"].rearrange("k p o -> p k o"), "w_f0")
            load(BO, dram["f0_bo"].partition_broadcast(P), "w_f0")
            for l in range(LAYERS):
                load(WR[:, l], dram["f0_wr"][l].rearrange("e k p o -> p e k o"), f"w_f0r{l}")

            def sparse():
                def weights(r, extra=False):
                    for b in range(RING):
                        if extra:
                            e = sp.value_load(EXTRAI[0:1, bass.ds(r * RING + b - E2, 1)], min_val=0, max_val=E2 - 1)
                        else:
                            e = r * RING + b
                        sp.dma_start(WRING[:, b, :], dram["f2_w"][bass.ds(e, 1)].rearrange("e p w -> p (e w)")).then_inc(S(f"f2.w{b}"), 16)
                        yield

                def round_(r, extra, last=False):
                    nxt = iter(()) if last else weights(r + 1, extra)
                    for b in range(RING):
                        s = r * RING + b
                        sp.wait_ge(*at("f2.y", s + 1))
                        sp.dma_start(y_rows[bass.ds(s * P, P), :], YS[:, b % 4, :]).then_inc(S(f"f2.y_out{b % 4}"), 16)
                        next(nxt, None)

                for _ in weights(0):
                    pass
                sp.wait_ge(*at("f2.xn", T))
                load(xn_rows.rearrange("(t p) d -> p t d", p=P), XN[:], "f2.rows")
                with sp.Fori(0, E2 // RING - 1) as r:
                    round_(r, False)
                sp.wait_ge(*at("f2.extra", 1))
                with sp.Fori(E2 // RING - 1, ROUNDS - 1) as r:
                    round_(r, True)
                round_(ROUNDS - 1, True, last=True)

            for m, M in MOE.items():
                ph = f"f{m}"
                if m == 1:
                    sp.wait_ge(*at("x_done", 2))
                    attention_weights(2)
                    attention_weights(3)
                sp.wait_ge(*at("x_done", 2 * m + 1))
                load(M["wg"], dram[f"{ph}_wg"], f"w_{ph}")
                if M["has_bg"]:
                    load(M["bg"], dram[f"{ph}_bg"].partition_broadcast(P), f"w_{ph}")
                load(M["b2"][0:M["E"], :], dram[f"{ph}_b2"], f"w_{ph}")
                if m == 2:
                    sparse()
                    continue

                def experts(q):
                    for b in range(2):
                        if not (isinstance(q, int) and q == 0):
                            sp.wait_ge(*at(f"{ph}.y_ps", NC * (2 * q + b - 1)))
                        e = 2 * q + b
                        load(M["w1"][:, b, :], dram[f"{ph}_w1"][bass.ds(e, 1)].rearrange("e p h -> p (e h)"), f"{ph}.w{b}")
                        load(M["w2"][:, b, :, :], dram[f"{ph}_w2"][bass.ds(e, 1)].rearrange("e k p d -> p (e k) d"), f"{ph}.w{b}")
                        load(M["b1"][:, b, :], dram[f"{ph}_b1"][bass.ds(e, 1)].rearrange("e p k -> p (e k)"), f"{ph}.w{b}")
                experts(0)
                with sp.Fori(1, M["E"] // 2) as q:
                    experts(q)

            sp.wait_ge(*at("x_done", len(PHASES)))
            sp.dma_start(out.rearrange("(t p) d -> p t d", p=P), X[:]).then_inc(S("stored"), 16)
            sp.wait_ge(*at("stored", 16))

        @block.gpsimd
        def _(pool):
            chain = [0]

            def link(ins):
                chain[0] += 1
                ins.then_inc(S("pool_chain"), 1)
                pool.wait_ge(*at("pool_chain", chain[0]))

            link(nc.gpsimd.memset(IDENT[:], 0.0))
            link(nc.gpsimd.affine_select(out=IDENT[:], in_=IDENT[:], compare_op=ALU.not_equal, fill=1.0,
                                         base=0, pattern=[[-1, P]], channel_multiplier=1))
            nc.gpsimd.memset(MHALF[:], -0.5).then_inc(S("ident"), 1)
            nc.gpsimd.tensor_copy(IDB[:], IDENT[:]).then_inc(S("ident"), 1)

            def rstd(ph):
                pool.wait_ge(*at(f"{ph}.veps", 1))
                if ph == "g0":
                    pool.wait_ge(*at("ident", 1))
                nc.gpsimd.tensor_tensor(RSTD[:], VEPS[:], MHALF[:], ALU.pow).then_inc(S(f"{ph}.rstd"), 1)

            def all_max(ph, n):
                pool.wait_ge(*at(f"{ph}.max", 1))
                nc.gpsimd.partition_all_reduce(GMAX[:, 0:n], MAXES[:, 0:n], P, RMAX).then_inc(S(f"{ph}.gmax"), 1)

            rstd("g0")
            all_max("g0", 8)

            pool.wait_ge(*at("g0.vh", 2 * PARTS))
            for t in range(T):
                pool.wait_ge(*at("g0.mask_copied", t + 1))
                src = T1.rearrange("p b t s w -> p (b t s w)")[:, (t % TH) * 396:(t % TH + 1) * 396].rearrange(
                    "p (h s w) -> p h s w", h=HEADS, s=PARTS)
                dst = RM[:, t, :, :]
                link(nc.gpsimd.tensor_tensor(dst, src[:, :, 0, :], src[:, :, 1, :], ALU.add))
                nc.gpsimd.tensor_tensor(dst, dst, src[:, :, 2, :], ALU.add).then_inc(S("g0.rm"), 1)

            def head_out(h, ib):
                n = 2 * h + ib
                pool.wait_ge(*at("g0.copied", n + 1))
                tiles = slice(ib * TH, (ib + 1) * TH)
                pool_ops = [
                    (RS, T1[:, ib, :, 0, :], T1[:, ib, :, 1, :], ALU.add),
                    (RS, RS, T1[:, ib, :, 2, :], ALU.add),
                    (RD, RM[:, tiles, h, :], RS[:, :, FH + 1:], ALU.subtract),
                    (RD, RD, AU[:, tiles, 4 + h:5 + h].to_broadcast([P, TH, FH + 1]), ALU.mult),
                    (RE, RS[:, :, 0:FH + 1], AU[:, tiles, h:h + 1].to_broadcast([P, TH, FH + 1]), ALU.mult),
                ]
                if n:
                    pool.wait_ge(*at("g0.rec", n))
                for o, a, b, op in pool_ops:
                    link(nc.gpsimd.tensor_tensor(o, a, b, op))
                link(nc.gpsimd.tensor_tensor(RE, RE, RD, ALU.add))
                nc.gpsimd.nop().then_inc(S("g0.weighed"), 1)
                pool.wait_ge(*at("g0.rec", n + 1))
                link(nc.gpsimd.tensor_tensor(RE[:, :, 0:FH], RE[:, :, 0:FH], RDEN[:, 0:TH].rearrange("p (t a) -> p t a", a=1).to_broadcast([P, TH, FH]), ALU.mult))
                xs = X[:, tiles, h * FH:(h + 1) * FH]
                link(nc.gpsimd.tensor_tensor(xs, xs, RE[:, :, 0:FH], ALU.add))
                nc.gpsimd.nop().then_inc(S("g0.x_added"), 1)

            for h in range(HEADS):
                for ib in range(2):
                    head_out(h, ib)

            def sparse():
                nc.gpsimd.iota(TOKI, pattern=[[P, T]], base=0, channel_multiplier=1).then_inc(S("f2.tok"), 1)
                nc.gpsimd.iota(COLI, pattern=[[1, P]], base=0, channel_multiplier=0).then_inc(S("f2.tok"), 1)
                link(nc.gpsimd.memset(ONESB, 1.0))
                nc.gpsimd.affine_select(out=EARLIER, in_=ONESB, compare_op=ALU.is_gt, fill=0.0, base=0,
                                        pattern=[[1, P]], channel_multiplier=-1).then_inc(S("f2.tok"), 1)
                pool.wait_ge(*at("f2.slots", 3))
                for t in range(HI_BY_POOL, T):
                    for k in range(TOPK):
                        last = nc.gpsimd.tensor_scalar(OHHI[:, t, k, :], COLF[:, 0:TILES], HIF[:, t, k:k + 1], TOKF[:, t:t + 1], ALU.is_equal, ALU.mult)
                    last.then_inc(S("f2.onehot_hi"), 1)
                pool.wait_ge(*at("f2.perm", 1))
                pool.wait_ge(*at("f2.rows", 16))

                for n in range(TILES):
                    b = n % RING
                    wait(pool, "f2.xg_ps", n - RING + 1)
                    nc.gpsimd.indirect_dma_start(out=XG[:, b, :], out_offset=None, in_=xn_rows,
                                                 in_offset=bass.IndirectOffsetOnAxis(ap=PERM[:, n:n + 1], axis=0)).then_inc(S(f"f2.xg{b}"), 16)
                for b in range(4):
                    pool.wait_ge(*at(f"f2.y_out{b}", 16 * TILES // 4))
                pool.wait_ge(*at("f2.xg_ps", TILES))
                slots = SLOTI.rearrange("p t k -> p (t k)").bitcast(U32)
                for n in range(T * TOPK):
                    b = n % RING
                    wait(pool, "f2.added", n - RING + 1)
                    nc.gpsimd.indirect_dma_start(out=XG[:, b, :], out_offset=None, in_=y_rows,
                                                 in_offset=bass.IndirectOffsetOnAxis(ap=slots[:, n:n + 1], axis=0)).then_inc(S(f"f2.xg{b}"), 16)

            nc.gpsimd.iota(IOTAI[0:E0, :], pattern=[[0, 1]], base=0, channel_multiplier=1).then_inc(S("f0.iota"), 1)
            rstd("f0")
            for m, M in MOE.items():
                rstd(f"g{m}")
                all_max(f"g{m}", 2)
                pool.wait_ge(*at("x_done", 2 * m + 1))
                nc.gpsimd.iota(M["iotai"], pattern=[[1, M["E"]]], base=0, channel_multiplier=0).then_inc(S(f"f{m}.iota"), 1)
                rstd(f"f{m}")
                if m == 2:
                    sparse()

        @block.tensor
        def _(pe):
            mm = nc.tensor.matmul

            def transpose_x(ph):
                if ph == "g0":
                    pe.wait_ge(*at("ident", 1))
                for t in range(T):
                    pe.wait_ge(*at(f"{ph}.xn", t + 1))
                    nc.tensor.transpose(PS[:, t // TPC, (t % TPC) * P:(t % TPC + 1) * P], XN[:, t, :], IDENT[:]).then_inc(S(f"{ph}.xnt_ps"), 1)

            pe.wait_ge(*at("w_g0", 16 * 5))
            pe.wait_ge(*at("g0.bias_t", 1))
            for h in range(HEADS):
                mm(PS[:, 7, 2 * h:2 * h + 2], w0t[:, h, :], phi0[:, h, :], start=True, stop=True)
                last = mm(PS[:, 7, 8 + 2 * h:10 + 2 * h], bias0tb[:, h, :], phi0[:, h, :], start=True, stop=True)
            last.then_inc(S("g0.wa_ps"), 1)
            transpose_x("g0")
            pe.wait_ge(*at("g0.xnt", NC))
            pe.wait_ge(*at("g0.wa", 2))
            for t in range(T):
                last = mm(PS[:, 6, t * 8:(t + 1) * 8], XNT[:, t * P:(t + 1) * P], WA[:], start=True, stop=True)
            last.then_inc(S("g0.ab_ps"), 1)
            for t in range(T):
                last = mm(PS[:, t // TPC, (t % TPC) * P:(t % TPC + 1) * P], XNT[:, t * P:(t + 1) * P], w0cat[:], start=True, stop=True)
                if t % TPC == TPC - 1:
                    last.then_inc(S("g0.hx_ps"), 1)
            for h in range(HEADS):
                for c in range(NC):
                    n = h * NC + c
                    if n < 4:
                        pe.wait_ge(*at("g0.hx", n + 1))
                    else:
                        pe.wait_ge(*at("g0.abc", n - 3))
                    mm(PS[:, n % 4, :], WA1B[:, h, :], XNT[:, c * CH:(c + 1) * CH], start=True, stop=True).then_inc(S("g0.abc_ps"), 1)

            pe.wait_ge(*at("g0.vh", 3))
            pe.wait_ge(*at("g0.abc", HEADS * NC))
            for r in range(2):
                for j in range(T):
                    if r == 0:
                        pe.wait_ge(*at("mask0", j + 1))
                    for i in range(TH):
                        if r and j == 0:
                            pe.wait_ge(*at("g0.mask_copied", i + 1))
                        t = r * TH + i
                        last = mm(PS[:, i, 0:396].rearrange("p (h s w) -> p h s w", h=HEADS, s=PARTS), MASK[:, j, t * P:(t + 1) * P],
                                  VH[:, j, :, :, FH + 1:], start=(j == 0), stop=(j == T - 1))
                        if j == T - 1:
                            last.then_inc(S("g0.mask_ps"), 1)

            def head_sums(h, first):
                for ib in range(2):
                    for j in range(T):
                        n = (2 * h + ib) * T + j
                        pe.wait_ge(*at("g0.m1", n + 1))
                        if j == 0:
                            if first:
                                pe.wait_ge(*at("g0.mask_copied", TH + 4 * (ib + 1)))
                            else:
                                pe.wait_ge(*at("g0.copied", 2 * h + ib - 1))
                        for i in range(TH):
                            last = mm(PS[:, 4 * ib + i // 2, (i % 2) * 198:(i % 2 + 1) * 198], M1[:, n % M1R if isinstance(n, int) else (ib * T + j) % M1R, i * P:(i + 1) * P],
                                      VH[:, j, h, :, :] if isinstance(h, int) else VH[:, j, bass.ds(h, 1), :, :],
                                      start=(j == 0 and i % 2 == 0), stop=(j == T - 1), skip_group_check=True)
                        last.then_inc(S("g0.m1_used"), 1)
            head_sums(0, True)
            with pe.Fori(1, HEADS) as h:
                head_sums(h, False)

            transpose_x("f0")
            pe.wait_ge(*at("f0.xnt", NC))
            pe.wait_ge(*at("w_f0", 16 * 9))

            def hidden_t(i):
                pe.wait_ge(*at("f0.h", i + 1))
                wait(pe, "f0.ht", i - 1)
                for k in range(KH):
                    last = nc.tensor.transpose(PS[:, 6 + i % 2, k * P:(k + 1) * P], HTOK(i % T)[:, k * P:(k + 1) * P], IDENT[:])
                last.then_inc(S("f0.ht_ps"), 1)

            for i in range((LAYERS + 1) * T):
                l, t = i // T - 1, i % T
                toks = slice(t * P, (t + 1) * P)
                wait(pe, "f0.sum", i - 1)
                if l < 0:
                    last = mm(PS[:, 4 + i % 2, 0:HID], XNT[:, toks], WI, start=True, stop=True)
                else:
                    pe.wait_ge(*at("f0.ht", i - T + 1))
                    for k in range(KH):
                        mm(PS[:, 4 + i % 2, 0:HID], HT0[:, k, toks], WS[:, l, k, :], start=(k == 0), stop=False, skip_group_check=True)
                    for g in range(P // GT):
                        gi = (i - T) * (P // GT) + g
                        pe.wait_ge(*at("f0.staged", gi + 1))
                        for k in range(KH):
                            last = mm(PS[g * GT:(g + 1) * GT, 4 + i % 2, 0:HID], HT0[:, k, t * P + g * GT:t * P + (g + 1) * GT], WST[gi % len(WST)][:, k, :],
                                      start=False, stop=False, skip_group_check=True)
                        last.then_inc(S("f0.stage_used"), 1)
                    pe.wait_ge(*at("f0.onehot", 1))
                    last = mm(PS[:, 4 + i % 2, 0:HID], ONEH[0:E0 + 1, toks], BRS[0:E0 + 1, l, :], start=False, stop=True, skip_group_check=True)
                last.then_inc(S("f0.main_ps"), 1)
                if i >= 2:
                    hidden_t(i - 2)
            hidden_t((LAYERS + 1) * T - 2)
            hidden_t((LAYERS + 1) * T - 1)
            pe.wait_ge(*at("f0.ht", (LAYERS + 1) * T))
            for t in range(T):
                for k in range(KH):
                    last = mm(PS[:, t // TPC, (t % TPC) * P:(t % TPC + 1) * P], HT0[:, k, t * P:(t + 1) * P], WO[:, k, :],
                              start=(k == 0), stop=(k == KH - 1), skip_group_check=True)
                last.then_inc(S("f0.out_ps"), 1)

            def attention(g):
                ph = f"g{g}"
                W = gw[g]
                pe.wait_ge(*at("x_done", 2 * g))
                pe.wait_ge(*at(f"w_{ph}", 16 * (7 if g == 3 else 4)))
                last = mm(PS[:, 7, 0:2], W["oi"], W["a"], start=True, stop=True)
                if g == 3:
                    pe.wait_ge(*at("g3.bias_b", 1))
                    last = mm(PS[:, 7, 2:4], b3cb[:], W["a"], start=True, stop=True)
                last.then_inc(S(f"{ph}.wa_ps"), 1)
                transpose_x(ph)
                pe.wait_ge(*at(f"{ph}.xnt", NC))
                pe.wait_ge(*at(f"{ph}.wa", 2))
                for t in range(T):
                    last = mm(PS[:, 6, 2 * t:2 * t + 2], XNT[:, t * P:(t + 1) * P], WA[:, 0:2], start=True, stop=True)
                last.then_inc(S(f"{ph}.ab_ps"), 1)
                if g != 2:
                    for c in range(NC):
                        mm(PS[:, c, :], WA1B[:, 0, :], XNT[:, c * CH:(c + 1) * CH], start=True, stop=True).then_inc(S(f"{ph}.abc_ps"), 1)
                    pe.wait_ge(*at(f"{ph}.gbc", NC))
                    pe.wait_ge(*at(f"{ph}.xv", 2))
                    for j in range(T):
                        pe.wait_ge(*at(f"{ph}.q", j + 1))
                        for c in range(NC):
                            last = mm(PS[:, c, :], XV[:, j, :], QT[:, j % 2, c * CH:(c + 1) * CH], start=(j == 0), stop=(j == T - 1))
                        last.then_inc(S(f"{ph}.q_used"), 1)
                else:
                    pe.wait_ge(*at(f"{ph}.xs", PARTS))
                    for j in range(T):
                        for s in range(PARTS):
                            for c in range(NC):
                                last = mm(PS[:, c, :], XS[:, j, s, :], MASK[:, j, c * CH:(c + 1) * CH],
                                          start=(j == 0 and s == 0), stop=(j == T - 1 and s == PARTS - 1))
                    last.then_inc(S(f"{ph}.q_used"), T)
                pe.wait_ge(*at(f"{ph}.wx", 2))
                pe.wait_ge(*at(f"{ph}.acct", NC))
                for t in range(T):
                    mm(PS[:, (4 + t // 3) % 8, (t % 3) * 129:(t % 3 + 1) * 129], ACCT[:, t * P:(t + 1) * P], W["wx"], start=True, stop=True).then_inc(S(f"{ph}.out_ps"), 1)

            def sparse():
                for t in range(T):
                    pe.wait_ge(*at("f2.onehot", t + 1))
                    wait(pe, "f2.onehot_hi", t - HI_BY_POOL + 1)
                    for k in range(TOPK):
                        last = mm(PS[:, 0, 0:TILES], OHLO[:, t, k, :], OHHI[:, t, k, :], start=(t == 0 and k == 0), stop=(t == T - 1 and k == TOPK - 1))
                last.then_inc(S("f2.perm_ps"), 1)
                pe.wait_ge(*at("f2.perm", 1))

                def turn(r, b):
                    s = r * RING + b
                    pe.wait_ge(*at(f"f2.xg{b}", 16 * r + 16))
                    wait(pe, "f2.xgt", s - 1)
                    nc.tensor.transpose(PS[:, b % 2, 0:P], XG[:, b, :], IDENT[:]).then_inc(S("f2.xg_ps"), 1)

                def hidden(r, b):
                    s = r * RING + b
                    pe.wait_ge(*at("f2.xgt", s + 1))
                    pe.wait_ge(*at(f"f2.w{b}", 16 * r + 16))
                    wait(pe, "f2.hts", s - 1)
                    for k in range(KH):
                        last = mm(PS[:, 2 + b % 2, k * P:(k + 1) * P], WRING[:, b, k * P:(k + 1) * P], XGT[:, b % 2, :], start=True, stop=True)
                    last.then_inc(S("f2.hid_ps"), 1)

                def outputs(r, b):
                    s = r * RING + b
                    pe.wait_ge(*at("f2.hts", s + 1))
                    wait(pe, "f2.y", s - 1)
                    for k in range(KH):
                        last = mm(PS[:, 4 + b % 2, 0:D], HTS[:, b % 2, k, :], WRING[:, b, W2AT + k * D:W2AT + (k + 1) * D], start=(k == 0), stop=(k == KH - 1))
                    last.then_inc(S("f2.out_ps"), 1)

                def round_(r, end=False):
                    for b in range(RING):
                        if b + 2 < RING or not end:
                            turn(r + (b + 2) // RING, (b + 2) % RING)
                        if b + 1 < RING or not end:
                            hidden(r + (b + 1) // RING, (b + 1) % RING)
                        outputs(r, b)
                turn(0, 0)
                turn(0, 1)
                hidden(0, 0)
                round_(0)
                with pe.Fori(1, ROUNDS - 1) as r:
                    round_(r)
                round_(ROUNDS - 1, end=True)

            def moe(m):
                M = MOE[m]
                ph, E, k_, H = f"f{m}", M["E"], M["k"], M["H"]
                pe.wait_ge(*at("x_done", 2 * m + 1))
                transpose_x(ph)
                pe.wait_ge(*at(f"{ph}.xnt", NC))
                pe.wait_ge(*at(f"w_{ph}", 16 * (3 if M["has_bg"] else 2)))
                for t in range(T):
                    bank, col = 4 + t * E // CH, t * E % CH
                    last = mm(PS[:, bank, col:col + E], XNT[:, t * P:(t + 1) * P], M["wg"], start=True, stop=True)
                last.then_inc(S(f"{ph}.lg_ps"), 1)
                if m == 2:
                    pe.wait_ge(*at("f2.routed", 1))
                    pe.wait_ge(*at("f2.tok", 3))
                    for lhs, bank in ((EARLIER, 4), (ONESB, 6)):
                        for c in range(2):
                            last = mm(PS[:, bank + c, :], lhs, OHB[:, 8 * c:8 * c + 8, :].rearrange("p t e -> p (t e)"), start=True, stop=True)
                    last.then_inc(S("f2.rank_ps"), 1)
                    sparse()
                    pe.wait_ge(*at("f2.y", TILES))
                pe.wait_ge(*at(f"{ph}.cmb", 1))
                for t in range(T):
                    nc.tensor.transpose(PS[0:E, t // TPC, (t % TPC) * P:(t % TPC + 1) * P], M["cmb"][:, t, :], IDENT[:]).then_inc(S(f"{ph}.cmbt_ps"), 1)
                pe.wait_ge(*at(f"{ph}.cmbt", NC))
                for t in range(T):
                    last = mm(PS[:, 4 + t // TPC, (t % TPC) * P:(t % TPC + 1) * P], M["cmbt"][0:E, t * P:(t + 1) * P], M["b2"][0:E, :], start=True, stop=True)
                    last.then_inc(S(f"{ph}.bias_ps"), 1)
                if m == 2:
                    return
                pe.wait_ge(*at(f"{ph}.acc", 1))

                def hidden(q, s):
                    b, c = s // NC, s % NC
                    n = q * 2 * NC + s
                    if c == 0:
                        pe.wait_ge(*at(f"{ph}.w{b}", 48 * q + 48))
                    wait(pe, f"{ph}.ht", k_ * (n - 1))
                    for k in range(k_):
                        mm(PS[:, 2 * (s % 2) + k, :], M["w1"][:, b, k * P:(k + 1) * P], XNT[:, c * CH:(c + 1) * CH], start=True, stop=True).then_inc(S(f"{ph}.h_ps"), 1)

                def outputs(q, s):
                    b, c = s // NC, s % NC
                    n = q * 2 * NC + s
                    pe.wait_ge(*at(f"{ph}.ht", k_ * (n + 1)))
                    wait(pe, f"{ph}.y", n - 1)
                    for t in range(TPC):
                        for k in range(k_):
                            last = mm(PS[:, 4 + s % 2, t * P:(t + 1) * P], M["ht"][:, s % 2, k, t * P:(t + 1) * P], M["w2"][:, b, k, :],
                                      start=(k == 0), stop=(k == k_ - 1), skip_group_check=True)
                    last.then_inc(S(f"{ph}.y_ps"), 1)

                def pair(q, end=False):
                    for s in range(2 * NC):
                        if s < 2 * NC - 1:
                            hidden(q, s + 1)
                        elif not end:
                            hidden(q + 1, 0)
                        outputs(q, s)
                hidden(0, 0)
                pair(0)
                if E // 2 > 2:
                    with pe.Fori(1, E // 2 - 1) as q:
                        pair(q)
                pair(E // 2 - 1, end=True)

            for g in (1, 2, 3):
                attention(g)
                moe(g)

        @block.scalar
        def _(act):
            A = nc.scalar.activation

            def copy_xnt(ph):
                for c in range(NC):
                    act.wait_ge(*at(f"{ph}.xnt_ps", TPC * (c + 1)))
                    nc.scalar.copy(XNT[:, c * CH:(c + 1) * CH], PS[:, c, :]).then_inc(S(f"{ph}.xnt"), 1)

            act.wait_ge(*at("g0.wa_ps", 1))
            nc.scalar.copy(WA[:].rearrange("p (s h) -> p s h", s=2), PS[:, 7, 0:8].rearrange("p (h s) -> p s h", s=2)).then_inc(S("g0.wa"), 1)
            nc.scalar.copy(SMALL[:, 0:8].rearrange("p (s h) -> p s h", s=2), PS[:, 7, 8:16].rearrange("p (h s) -> p s h", s=2)).then_inc(S("g0.consts"), 1)
            copy_xnt("g0")
            act.wait_ge(*at("g0.consts", 1))
            for h in range(HEADS):
                for c in range(NC):
                    n = h * NC + c
                    act.wait_ge(*at("g0.abc_ps", n + 1))
                    A(ABC[:, h, c * CH:(c + 1) * CH], PS[:, n % 4, :], ACT.Identity, bias=SMALL[:, h:h + 1]).then_inc(S("g0.abc"), 1)
            act.wait_ge(*at("g0.uv_in", 2))
            A(AV[:, :, 0:4], AV[:, :, 0:4], ACT.Exp).then_inc(S("g0.uv"), 1)
            A(AV[:, :, 4:8], AV[:, :, 4:8], ACT.Exp, scale=SLOPE).then_inc(S("g0.uv"), 1)
            A(AU[:, :, 0:4], AU[:, :, 0:4], ACT.Exp, scale=REST).then_inc(S("g0.uv"), 1)
            A(AU[:, :, 4:8], AU[:, :, 4:8], ACT.Exp, scale=-REST).then_inc(S("g0.uv"), 1)
            far = [0]

            def reach(upto):
                for f in range(far[0], upto):
                    h, ib, j = f // len(BY_SCALAR) // 2, f // len(BY_SCALAR) % 2, BY_SCALAR[f % len(BY_SCALAR)]
                    if f >= 4:
                        act.wait_ge(*at("g0.m1", (f - 4) // len(BY_SCALAR) * T + BY_SCALAR[(f - 4) % len(BY_SCALAR)] + 1))
                    A(REACH[:, f % 4, :], ABC[:, h, ib * HB:(ib + 1) * HB], ACT.Relu, bias=NB[:, j, h:h + 1], scale=-BIG).then_inc(S("g0.reach"), 1)
                far[0] = upto

            for t in range(T):
                act.wait_ge(*at("g0.mask_ps", t + 1))
                if t == TH:
                    act.wait_ge(*at("g0.nb", 1))
                    act.wait_ge(*at("g0.vh", 2 * PARTS))
                    reach(4)
                if t >= TH:
                    act.wait_ge(*at("g0.rm", t - TH + 1))
                if t == 0:
                    act.wait_ge(*at("mask0", T))
                dst = T1.rearrange("p b t s w -> p (b t s w)")[:, (t % TH) * 396:(t % TH + 1) * 396]
                nc.scalar.copy(dst, PS[:, t % TH, 0:396]).then_inc(S("g0.mask_copied"), 1)
            act.wait_ge(*at("g0.rm", T))
            reach(len(BY_SCALAR))
            for n in range(2 * HEADS):
                ib = n % 2
                if n + 1 < 2 * HEADS:
                    reach((n + 2) * len(BY_SCALAR))
                act.wait_ge(*at("g0.m1_used", (n + 1) * T))
                wait(act, "g0.x_added", n - 1)
                for b in range(4):
                    last = nc.scalar.copy(T1[:, ib, 2 * b:2 * b + 2, :, :].rearrange("p t s w -> p (t s w)"), PS[:, 4 * ib + b, 0:396])
                last.then_inc(S("g0.copied"), 1)

            copy_xnt("f0")

            def hidden_copy(i):
                act.wait_ge(*at("f0.ht_ps", i + 1))
                t = i % T
                nc.scalar.copy(HT0[:, :, t * P:(t + 1) * P], PS[:, 6 + i % 2, 0:HID].rearrange("p (k n) -> p k n", k=KH)).then_inc(S("f0.ht"), 1)

            for i in range((LAYERS + 1) * T):
                act.wait_ge(*at("f0.sum", i + 1))
                A(HTOK(i % T), HSUM[:, i % 2, :], ACT.Relu).then_inc(S("f0.h"), 1)
                if i >= 2:
                    hidden_copy(i - 2)
            hidden_copy((LAYERS + 1) * T - 2)
            hidden_copy((LAYERS + 1) * T - 1)

            def attention(g):
                ph = f"g{g}"
                act.wait_ge(*at(f"{ph}.wa_ps", 1))
                wn = 4 if g == 3 else 2
                nc.scalar.copy(WA[:, 0:wn], PS[:, 7, 0:wn]).then_inc(S(f"{ph}.wa"), 1)
                copy_xnt(ph)
                if g != 2:
                    act.wait_ge(*at(f"{ph}.shift", 1))
                    for c in range(NC):
                        act.wait_ge(*at(f"{ph}.abc_ps", c + 1))
                        A(GBC[:, c * CH:(c + 1) * CH], PS[:, c, :], ACT.Exp, bias=SMALL[:, 0:1], scale=REST).then_inc(S(f"{ph}.gbc"), 1)
                    A(AU[:, :, 0], AB[:, :, 1], ACT.Exp, bias=SMALL[:, 1:2], scale=REST).then_inc(S(f"{ph}.uv"), 1)
                    A(SMALL[:, 5:6], SMALL[:, 3:4], ACT.Exp).then_inc(S(f"{ph}.uv"), 1)
                    A(AV[:, :, 0], AB[:, :, 1], ACT.Exp, bias=SMALL[:, 2:3], scale=SLOPE).then_inc(S(f"{ph}.uv"), 1)
                    act.wait_ge(*at(f"{ph}.negc", 1))
                    act.wait_ge(*at(f"{ph}.gbc", NC))
                    for j in range(T):
                        wait(act, f"{ph}.q", j - 1)
                        A(REL[:, j % 2, :], GBC, ACT.Relu, bias=SMALL[:, 6:7], scale=AU[:, j, 0:1]).then_inc(S(f"{ph}.rel"), 1)
                else:
                    act.wait_ge(*at(f"{ph}.shift", 1))
                    A(AV[:, :, 0], AB[:, :, 1], ACT.Exp, bias=SMALL[:, 2:3], scale=1.0).then_inc(S(f"{ph}.uv"), 3)
                for c in range(NC):
                    act.wait_ge(*at(f"{ph}.q_used", T))
                    nc.scalar.copy(ACCT[:, c * CH:(c + 1) * CH], PS[:, c, :]).then_inc(S(f"{ph}.acct"), 1)

            def moe(m):
                M = MOE[m]
                ph, E, k_ = f"f{m}", M["E"], M["k"]
                copy_xnt(ph)
                if M["gated"]:
                    act.wait_ge(*at(f"{ph}.gap", 1))
                    A(M["gt"][:, :, 1], M["gt"][:, :, 1], ACT.Exp).then_inc(S(f"{ph}.gap_exp"), 1)
                if m == 2:
                    def round_(r):
                        for b in range(RING):
                            s = r * RING + b
                            act.wait_ge(*at("f2.hid_ps", s + 1))
                            wait(act, "f2.out_ps", s - 1)
                            for k in range(KH):
                                last = A(HTS[:, b % 2, k, :], PS[:, 2 + b % 2, k * P:(k + 1) * P], ACT.Relu, bias=WRING[:, b, HID + k:HID + k + 1])
                            last.then_inc(S("f2.hts"), 1)
                    round_(0)
                    with act.Fori(1, ROUNDS) as r:
                        round_(r)
                for c in range(NC):
                    act.wait_ge(*at(f"{ph}.cmbt_ps", TPC * (c + 1)))
                    nc.scalar.copy(M["cmbt"][0:E, c * CH:(c + 1) * CH], PS[0:E, c, :]).then_inc(S(f"{ph}.cmbt"), 1)
                if m == 2:
                    return

                def pair(q):
                    for s in range(2 * NC):
                        b, n = s // NC, q * 2 * NC + s
                        wait(act, f"{ph}.y_ps", n - 1)
                        for k in range(k_):
                            act.wait_ge(*at(f"{ph}.h_ps", k_ * n + k + 1))
                            A(M["ht"][:, s % 2, k, :], PS[:, 2 * (s % 2) + k, :], M["act"], bias=M["b1"][:, b, k:k + 1]).then_inc(S(f"{ph}.ht"), 1)
                pair(0)
                with act.Fori(1, E // 2) as q:
                    pair(q)

            for g in (1, 2, 3):
                attention(g)
                moe(g)

        @block.vector
        def _(dve):
            V = nc.vector
            chain = [0]

            def mark(ins):
                chain[0] += 1
                ins.then_inc(S("dve_chain"), 1)
                return chain[0]

            def link(ins):
                dve.wait_ge(*at("dve_chain", mark(ins)))

            def norm(ph):
                for t in range(T):
                    last = V.bn_stats(STATS[:, t, :], X[:, t, :])
                    last.then_inc(S(f"{ph}.stats"), 1)
                for t in range(T):
                    dve.wait_ge(*at(f"{ph}.stats", t + 1))
                    last = V.bn_aggr(MV[:, t, :], STATS[:, t, :])
                link(last)
                V.tensor_scalar(VEPS[:], MV[:, :, 1], EPS, None, ALU.add).then_inc(S(f"{ph}.veps"), 1)
                dve.wait_ge(*at(f"{ph}.rstd", 1))
                for t in range(T):
                    V.tensor_scalar(XN[:, t, :], X[:, t, :], MV[:, t, 0:1], RSTD[:, t:t + 1], ALU.subtract, ALU.mult).then_inc(S(f"{ph}.xn"), 1)

            masked = [0]

            def masks(upto):
                for j in range(masked[0], upto):
                    if j == 0:
                        dve.wait_ge(*at("ident", 2))
                    dve.wait_ge(*at(f"adj{j % 2}", 16 * (j // 2 + 1)))
                    V.tensor_scalar(MASK[:, j, :], ADJ[:, j % 2, :], 0.0, None, ALU.is_gt).then_inc(S("mask"), 1)
                    dve.wait_ge(*at("mask", j + 1))
                    own = MASK[:, j, j * P:(j + 1) * P]
                    link(V.tensor_copy(DIAG[:, j, :], own))
                    V.tensor_tensor(own, own, IDB[:], ALU.max).then_inc(S("mask0"), 1)
                masked[0] = upto

            dve.wait_ge(*at("w_g0", 16 * 5))
            V.tensor_copy(bias0tb[:], bias0t[:].rearrange("p (h a) -> p h a", a=1).to_broadcast([FH, HEADS, P])).then_inc(S("g0.bias_t"), 1)
            dve.wait_ge(*at("x_in", 16))
            norm("g0")
            dve.wait_ge(*at("g0.wa", 1))
            V.tensor_copy(WA1B[:], WA[:, 0:4].rearrange("p (h a) -> p h a", a=1).to_broadcast([P, 4, P])).then_inc(S("g0.wa"), 1)
            masks(1)
            dve.wait_ge(*at("g0.ab_ps", 1))
            dve.wait_ge(*at("g0.consts", 1))
            link(V.tensor_tensor(AB[:], PS[:, 6, 0:T * 8].rearrange("p (t c) -> p t c", t=T),
                                 SMALL[:, 0:8].rearrange("p (a c) -> p a c", a=1).to_broadcast([P, T, 8]), ALU.add))
            V.tensor_reduce(MAXES[:, 0:8], AB[:].rearrange("p t c -> p c t"), AX_X, ALU.max).then_inc(S("g0.max"), 1)
            masks(2)
            for c in range(NC):
                dve.wait_ge(*at("g0.hx_ps", c + 1))
                V.tensor_tensor(HX[:, c * TPC:(c + 1) * TPC, :], PS[:, c, :].rearrange("p (t d) -> p t d", t=TPC),
                                bias0[:].rearrange("p (a d) -> p a d", a=1).to_broadcast([P, TPC, D]), ALU.add).then_inc(S("g0.hx"), 1)
            masks(3)
            dve.wait_ge(*at("g0.gmax", 1))
            bmax = GMAX[:, 4:8].rearrange("p (a c) -> p a c", a=1).to_broadcast([P, T, 4])
            V.tensor_tensor(AV[:, :, 0:4], AB[:, :, 4:8], bmax, ALU.subtract)
            V.tensor_tensor(AV[:, :, 4:8], AB[:, :, 4:8], bmax, ALU.subtract)
            link(V.tensor_tensor(AU[:, :, 0:4], AB[:, :, 0:4], bmax, ALU.add))
            V.tensor_scalar(AU[:, :, 4:8], AU[:, :, 0:4], 0.0, None, ALU.max).then_inc(S("g0.uv_in"), 1)
            dve.wait_ge(*at("g0.uv_in", 1))
            V.tensor_scalar(AU[:, :, 0:4], AU[:, :, 0:4], 0.0, None, ALU.min).then_inc(S("g0.uv_in"), 1)
            link(V.tensor_scalar(AB[:, :, 4:8], AB[:, :, 4:8], -1.0, None, ALU.mult))
            dve.wait_ge(*at("g0.hx", NC))
            masks(7)
            dve.wait_ge(*at("g0.uv", 4))
            hx4 = HX.rearrange("p t (h f) -> p t h f", h=HEADS)
            vhs = 0
            for br in (1, 0):
                own = slice(br * (FH + 1), (br + 1) * (FH + 1))
                vcol = AV[:, :, 4 * br:4 * br + 4].rearrange("p t (h a) -> p t h a", a=1)
                for t in range(T):
                    V.tensor_tensor(VF[:, t, :, br * (FH + 1):br * (FH + 1) + FH], hx4[:, t], vcol[:, t].to_broadcast([P, HEADS, FH]), ALU.mult)
                last = V.tensor_copy(VF[:, :, :, br * (FH + 1) + FH], AV[:, :, 4 * br:4 * br + 4])
                if br == 1:
                    masks(9)
                link(last)
                vf = VF.rearrange("p t h w -> p (t h) w")[:, :, own]
                for s in range(PARTS):
                    vh = VH[:, :, :, s, own].rearrange("p t h w -> p (t h) w")
                    V.tensor_copy(vh, vf).then_inc(S("g0.vh"), 1)
                    vhs += 1
                    if br == 1:
                        masks(11 + s)
                    if s < PARTS - 1:
                        dve.wait_ge(*at("g0.vh", vhs))
                        link(V.tensor_tensor(vf, vf, vh, ALU.subtract))
                if br == 1:
                    masks(T)

            dve.wait_ge(*at("g0.vh", 2 * PARTS))
            V.tensor_scalar(NB, AB[:, :, 4:8], BIG, None, ALU.mult).then_inc(S("g0.nb"), 1)

            dve.wait_ge(*at("mask0", T))
            dve.wait_ge(*at("g0.abc", HEADS * NC))

            def recip(n):
                dve.wait_ge(*at("g0.weighed", n + 1))
                V.reciprocal(RDEN[:, 0:TH], RE[:, :, FH]).then_inc(S("g0.rec"), 1)

            for h in range(HEADS):
                for ib in range(2):
                    for j in range(T):
                        n = (2 * h + ib) * T + j
                        wait(dve, "g0.m1_used", n - M1R + 1)
                        if j in BY_SCALAR:
                            at_far = (2 * h + ib) * len(BY_SCALAR) + BY_SCALAR.index(j)
                            dve.wait_ge(*at("g0.reach", at_far + 1))
                            V.tensor_tensor(M1[:, n % M1R, :], MASK[:, j, ib * HB:(ib + 1) * HB], REACH[:, at_far % 4, :], ALU.is_gt).then_inc(S("g0.m1"), 1)
                            continue
                        V.scalar_tensor_tensor(M1[:, n % M1R, :], ABC[:, h, ib * HB:(ib + 1) * HB], AB[:, j, 4 + h:5 + h],
                                               MASK[:, j, ib * HB:(ib + 1) * HB], ALU.is_gt, ALU.mult).then_inc(S("g0.m1"), 1)
                    if 2 * h + ib:
                        recip(2 * h + ib - 1)
            recip(2 * HEADS - 1)
            for j in range(T):
                last = V.tensor_copy(MASK[:, j, j * P:(j + 1) * P], DIAG[:, j, :])
            link(last)
            dve.wait_ge(*at("g0.x_added", 2 * HEADS))
            V.tensor_copy(SMALL[:, 32:33], SMALL[:, 0:1]).then_inc(S("x_done"), 1)

            norm("f0")
            dve.wait_ge(*at("f0.xn", T))
            dve.wait_ge(*at("w_f0", 16 * 9))
            dve.wait_ge(*at("f0.iota", 1))
            link(V.tensor_tensor(X[:], X[:], BO.rearrange("p (a d) -> p a d", a=1).to_broadcast([P, T, D]), ALU.add))
            V.tensor_copy(IOTAF[0:E0, :], IOTAI[0:E0, :])
            link(V.tensor_copy(ROUTEF[0:E0, :], ROUTEF[0:E0, :].bitcast(I32)))
            GPT = P // GT
            routes = {}

            def stage(gi):
                l, g = gi // GROUPS, gi % GROUPS
                if gi % GROUPS == 0:
                    dve.wait_ge(*at(f"w_f0r{l}", 16))
                if gi % GPT == 0:
                    for n in range(GPT):
                        routes[n] = dve.value_load(ROUTE[0:1, g + n:g + n + 1], min_val=0, max_val=E0 - 1)
                wait(dve, "f0.stage_used", gi - len(WST) + 1)
                V.tensor_copy(WST[gi % len(WST)].rearrange("p k o -> p (k o)"), WR[:, l, bass.ds(routes[gi % GPT], 1), :, :].rearrange("p e k o -> p (e k o)")).then_inc(S("f0.staged"), 1)

            for i in range((LAYERS + 1) * T):
                t = i % T
                if i >= T:
                    for g in range(1, GPT):
                        stage((i - T) * GPT + g)
                if T - 1 <= i < (LAYERS + 1) * T - 1:
                    stage((i + 1 - T) * GPT)
                dve.wait_ge(*at("f0.main_ps", i + 1))
                wait(dve, "f0.h", i - 1)
                if i >= T:
                    dve.wait_ge(*at("f0.h", i - T + 1))
                V.tensor_tensor(HSUM[:, i % 2, :], PS[:, 4 + i % 2, 0:HID], BI if i < T else HTOK(t), ALU.add).then_inc(S("f0.sum"), 1)
                if i == T - 1:
                    link(V.memset(ONEH[0:32, :], 1.0))
                    V.tensor_scalar(ONEH[0:E0, :].rearrange("p (g t) -> p g t", t=GT), ROUTEF[0:E0, :].rearrange("p (g a) -> p g a", a=1).to_broadcast([E0, GROUPS, GT]),
                                    IOTAF[0:E0, 0:1], None, ALU.is_equal).then_inc(S("f0.onehot"), 1)
            for t in range(T):
                dve.wait_ge(*at("f0.out_ps", (t // TPC + 1) * TPC))
                last = V.tensor_tensor(X[:, t, :], X[:, t, :], PS[:, t // TPC, (t % TPC) * P:(t % TPC + 1) * P], ALU.add)
            last.then_inc(S("x_done"), 1)
            dve.wait_ge(*at("x_done", 2))

            def attention(g):
                ph = f"g{g}"
                W = gw[g]
                dve.wait_ge(*at(f"w_{ph}", 16 * (7 if g == 3 else 4)))
                if g == 3:
                    V.tensor_copy(b3cb[:], b3col[:].to_broadcast([P, P])).then_inc(S("g3.bias_b"), 1)
                V.tensor_tensor(W["wx"][:, 0:D], W["io"], W["last"], ALU.subtract).then_inc(S(f"{ph}.wx"), 1)
                V.tensor_copy(W["wx"][:, D:D + 1], IDENT[:, D - 1:D]).then_inc(S(f"{ph}.wx"), 1)
                norm(ph)
                dve.wait_ge(*at(f"{ph}.wa", 1))
                V.tensor_copy(WA1B[:, 0, :], WA[:, 0:1].to_broadcast([P, P])).then_inc(S(f"{ph}.wa"), 1)
                dve.wait_ge(*at(f"{ph}.ab_ps", 1))
                link(V.tensor_copy(AB[:, :, 0:2], PS[:, 6, 0:2 * T].rearrange("p (t c) -> p t c", t=T)))
                V.tensor_reduce(MAXES[:, 0:2], AB[:, :, 0:2].rearrange("p t c -> p c t"), AX_X, ALU.max).then_inc(S(f"{ph}.max"), 1)
                dve.wait_ge(*at(f"{ph}.gmax", 1))
                if g == 2:
                    V.tensor_scalar(SMALL[:, 2:3], GMAX[:, 1:2], -1.0, None, ALU.mult).then_inc(S(f"{ph}.shift"), 1)
                else:
                    link(V.tensor_tensor(SMALL[:, 4:5], GMAX[:, 0:1], GMAX[:, 1:2], ALU.add))
                    if g == 3:
                        link(V.tensor_tensor(SMALL[:, 4:5], SMALL[:, 4:5], WA[:, 2:3], ALU.add))
                        link(V.tensor_tensor(SMALL[:, 4:5], SMALL[:, 4:5], WA[:, 3:4], ALU.add))
                        link(V.tensor_tensor(SMALL[:, 4:5], SMALL[:, 4:5], ba3[:], ALU.add))
                    V.tensor_scalar(SMALL[:, 0:1], GMAX[:, 0:1], -REST, None, ALU.mult)
                    V.tensor_scalar(SMALL[:, 2:3], GMAX[:, 1:2], -SLOPE, None, ALU.mult)
                    link(V.tensor_scalar(SMALL[:, 3:4], SMALL[:, 4:5], 0.0, -REST, ALU.max, ALU.mult))
                    link(V.tensor_scalar(SMALL[:, 3:4], SMALL[:, 3:4], HEADROOM, None, ALU.add))
                    link(V.tensor_scalar(SMALL[:, 1:2], SMALL[:, 4:5], 0.0, None, ALU.min))
                    link(V.tensor_tensor(SMALL[:, 1:2], SMALL[:, 1:2], GMAX[:, 1:2], ALU.subtract))
                    V.tensor_scalar(SMALL[:, 1:2], SMALL[:, 1:2], REST, HEADROOM, ALU.mult, ALU.add).then_inc(S(f"{ph}.shift"), 1)
                    dve.wait_ge(*at(f"{ph}.uv", 2))
                    V.tensor_scalar(SMALL[:, 6:7], SMALL[:, 5:6], -1.0, None, ALU.mult).then_inc(S(f"{ph}.negc"), 1)
                dve.wait_ge(*at(f"{ph}.uv", 3))
                v = AV[:, :, 0:1]
                V.tensor_tensor(XV[:, :, 0:D - 1], XN[:, :, 0:D - 1], v.to_broadcast([P, T, D - 1]), ALU.mult).then_inc(S(f"{ph}.xv"), 1)
                V.tensor_copy(XV[:, :, D - 1:D], v).then_inc(S(f"{ph}.xv"), 1)
                if g == 2:
                    dve.wait_ge(*at(f"{ph}.xv", 2))
                    for s in range(PARTS):
                        V.tensor_copy(XS[:, :, s, :], XV).then_inc(S(f"{ph}.xs"), 1)
                        if s < PARTS - 1:
                            dve.wait_ge(*at(f"{ph}.xs", s + 1))
                            link(V.tensor_tensor(XV, XV, XS[:, :, s, :], ALU.subtract))
                else:
                    for j in range(T):
                        dve.wait_ge(*at(f"{ph}.rel", j + 1))
                        wait(dve, f"{ph}.q_used", j - 1)
                        V.scalar_tensor_tensor(QT[:, j % 2, :], REL[:, j % 2, :], SMALL[:, 5:6], MASK[:, j, :], ALU.add, ALU.mult).then_inc(S(f"{ph}.q"), 1)
                if g == 3:
                    link(V.tensor_tensor(X[:], X[:], b3row[:].rearrange("p (a d) -> p a d", a=1).to_broadcast([P, T, D]), ALU.add))
                dve.wait_ge(*at(f"{ph}.out_ps", T))
                V.reciprocal(RDEN[:, 0:12].rearrange("p (b t) -> p b t", b=4), PS[:, 4:8, 0:387].rearrange("p b (t c) -> p b t c", c=D + 1)[:, :, :, D])
                V.reciprocal(RDEN[:, 12:15], PS[:, 0, 0:387].rearrange("p (t c) -> p t c", c=D + 1)[:, :, D])
                link(V.reciprocal(RDEN[:, 15:16], PS[:, 1, D:D + 1]))
                for t in range(T):
                    last = V.scalar_tensor_tensor(X[:, t, :], PS[:, (4 + t // 3) % 8, (t % 3) * 129:(t % 3) * 129 + D], RDEN[:, t:t + 1], X[:, t, :], ALU.mult, ALU.add)
                last.then_inc(S("x_done"), 1)
                dve.wait_ge(*at("x_done", 2 * g + 1))

            def ranks(M):
                dve.wait_ge(*at("f2.rank_ps", 1))
                counts = PS[:, 6:8, :].rearrange("p b (t e) -> p (b t) e", e=E2)
                V.tensor_copy(CNT, counts).then_inc(S("f2.ranked"), 1)
                link(V.memset(BEFORE[:, 0, :], 0.0))
                dve.wait_ge(*at("f2.ranked", 1))
                for t in range(T):
                    link(V.tensor_tensor(BEFORE[:, t + 1, :], BEFORE[:, t, :], CNT[:, t, :], ALU.add))
                V.tensor_tensor(RANK, PS[:, 4:6, :].rearrange("p b (t e) -> p (b t) e", e=E2), BEFORE[:, 0:T, :], ALU.add).then_inc(S("f2.ranked"), 1)
                link(V.tensor_scalar(MORE, BEFORE[:, T, :], float(P - 1), None, ALU.add))
                link(V.tensor_copy(MOREI, MORE))
                link(V.tensor_scalar(MOREI, MOREI, 7, None, ALU.arith_shift_right))
                link(V.tensor_copy(MORE, MOREI))
                link(V.tensor_scalar(MORE, MORE, -1.0, 0.0, ALU.add, ALU.max))
                link(V.memset(ONESF, 1.0))
                link(V.tensor_tensor_scan(MORECUM, ONESF, MORE, 0.0, ALU.mult, ALU.add))
                link(V.tensor_tensor(SHIFT, MORECUM, MORE, ALU.subtract))
                link(V.tensor_tensor(SHIFT, SHIFT, M["iota"], ALU.subtract))
                link(V.tensor_scalar(SHIFT, SHIFT, float(E2 - 1), float(P), ALU.add, ALU.mult))
                link(V.tensor_scalar(EXPERT128, M["iota"], float(P), None, ALU.mult))
                dve.wait_ge(*at("f2.ranked", 2))
                row = lambda a: a.rearrange("p (a e) -> p a e", a=1).to_broadcast([P, T, E2])
                link(V.scalar_tensor_tensor(SLOT, RANK, float(P), row(SHIFT), ALU.is_ge, ALU.mult))
                link(V.tensor_tensor(SLOT, SLOT, RANK, ALU.add))
                link(V.tensor_tensor(SLOT, SLOT, row(EXPERT128), ALU.add))
                for k in range(TOPK):
                    link(V.tensor_tensor(RANK, (M["cmb"], M["oh"])[k], SLOT, ALU.mult))
                    link(V.tensor_reduce(SLOTF[:, :, k], RANK, AX_X, ALU.add))
                link(V.tensor_copy(SLOTI, SLOTF))
                V.tensor_scalar(LOI, SLOTI, P - 1, None, ALU.bitwise_and)
                link(V.tensor_scalar(HII, SLOTI, 7, None, ALU.arith_shift_right))
                dve.wait_ge(*at("f2.tok", 3))
                V.tensor_copy(HIF, HII).then_inc(S("f2.slots"), 1)
                V.tensor_copy(TOKF, TOKI).then_inc(S("f2.slots"), 1)
                V.tensor_copy(COLF, COLI).then_inc(S("f2.slots"), 1)
                dve.wait_ge(*at("f2.slots", 3))
                link(V.tensor_copy(LOF, LOI))
                for t in range(T):
                    for k in range(TOPK):
                        if t < HI_BY_POOL:
                            V.tensor_scalar(OHHI[:, t, k, :], COLF[:, 0:TILES], HIF[:, t, k:k + 1], TOKF[:, t:t + 1], ALU.is_equal, ALU.mult)
                        last = V.tensor_scalar(OHLO[:, t, k, :], COLF, LOF[:, t, k:k + 1], None, ALU.is_equal)
                    last.then_inc(S("f2.onehot"), 1)
                cum = MORECUM.rearrange("p (a e) -> p a e", a=1).to_broadcast([P, EXTRA, E2])
                num = COLF[:, 0:EXTRA].rearrange("p (o a) -> p o a", a=1).to_broadcast([P, EXTRA, E2])
                tmp = TMP.rearrange("p (o e) -> p o e", o=EXTRA)
                link(V.tensor_tensor(tmp, cum, num, ALU.is_le))
                link(V.tensor_reduce(EXTRAF, tmp, AX_X, ALU.add))
                link(V.tensor_scalar(EXTRAF, EXTRAF, float(E2 - 1), None, ALU.min))
                V.tensor_copy(EXTRAI, EXTRAF).then_inc(S("f2.extra"), 1)

            def sparse(M):
                dve.wait_ge(*at("f2.perm_ps", 1))
                V.tensor_copy(PERM, PS[:, 0, 0:TILES]).then_inc(S("f2.perm"), 1)

                def turned(r, b):
                    s = r * RING + b
                    dve.wait_ge(*at("f2.xg_ps", s + 1))
                    wait(dve, "f2.hid_ps", s - 1)
                    V.tensor_copy(XGT[:, b % 2, :], PS[:, b % 2, 0:P]).then_inc(S("f2.xgt"), 1)

                def round_(r, end=False):
                    for b in range(RING):
                        s = r * RING + b
                        if b + 2 < RING or not end:
                            turned(r + (b + 2) // RING, (b + 2) % RING)
                        dve.wait_ge(*at("f2.out_ps", s + 1))
                        if not (isinstance(r, int) and s < 4):
                            dve.wait_ge(*at(f"f2.y_out{b % 4}", 32 * r + 16 * (b // 4)))
                        V.tensor_copy(YS[:, b % 4, :], PS[:, 4 + b % 2, 0:D]).then_inc(S("f2.y"), 1)
                turned(0, 0)
                turned(0, 1)
                round_(0)
                with dve.Fori(1, ROUNDS - 1) as r:
                    round_(r)
                round_(ROUNDS - 1, end=True)

            def combine(M):
                dve.wait_ge(*at("f2.acc", 1))

                def add(r):
                    for b in range(RING):
                        n = r * RING + b
                        t, k = r * (RING // TOPK) + b // TOPK, b % TOPK
                        dve.wait_ge(*at(f"f2.xg{b}", 16 * ROUNDS + 16 * r + 16))
                        if k:
                            dve.wait_ge(*at("f2.added", n))
                        x = X[:, bass.ds(t, 1), :].rearrange("p a d -> p (a d)")
                        V.scalar_tensor_tensor(x, XG[:, b, :], M["gt"][:, bass.ds(t, 1), k], x, ALU.mult, ALU.add).then_inc(S("f2.added"), 1)
                with dve.Fori(0, T * TOPK // RING) as r:
                    add(r)
                dve.wait_ge(*at("f2.added", T * TOPK))
                V.tensor_copy(SMALL[:, 32:33], IDENT[:, 0:1]).then_inc(S("x_done"), 1)

            def moe(m):
                M = MOE[m]
                ph, E = f"f{m}", M["E"]
                norm(ph)
                dve.wait_ge(*at(f"{ph}.iota", 1))
                link(V.tensor_copy(M["iota"], M["iotai"]))
                dve.wait_ge(*at(f"{ph}.lg_ps", 1))
                nb = (T * E + CH - 1) // CH
                lgps = PS[:, 4:4 + nb, :].rearrange("p b n -> p (b n)")[:, 0:T * E].rearrange("p (t e) -> p t e", t=T)
                if M["has_bg"]:
                    link(V.tensor_tensor(M["lg"], lgps, M["bg"].rearrange("p (a e) -> p a e", a=1).to_broadcast([P, T, E]), ALU.add))
                else:
                    link(V.tensor_copy(M["lg"], lgps))
                for t in range(T):
                    V.max(M["top8"][:, t, :], M["lg"][:, t, :]).then_inc(S(f"{ph}.top"), 1)
                for t in range(T):
                    dve.wait_ge(*at(f"{ph}.top", t + 1))
                    last = V.max_index(M["idx"][:, t, :], M["top8"][:, t, :], M["lg"][:, t, :])
                link(last)
                link(V.tensor_copy(M["idxf"], M["idx"]))
                if M["gated"]:
                    V.tensor_tensor(M["gt"][:, :, 1], M["top8"][:, :, 1], M["top8"][:, :, 0], ALU.subtract).then_inc(S(f"{ph}.gap"), 1)
                    dve.wait_ge(*at(f"{ph}.gap_exp", 1))
                    link(V.tensor_scalar(M["gd"], M["gt"][:, :, 1], 1.0, None, ALU.add))
                    link(V.reciprocal(M["gt"][:, :, 0], M["gd"]))
                    link(V.tensor_tensor(M["gt"][:, :, 1], M["gt"][:, :, 1], M["gt"][:, :, 0], ALU.mult))
                iot = M["iota"].rearrange("p (a e) -> p a e", a=1).to_broadcast([P, T, E])
                for k, dst in ((0, M["cmb"]), (1, M["oh"])):
                    link(V.tensor_tensor(dst, iot, M["idxf"][:, :, k:k + 1].to_broadcast([P, T, E]), ALU.is_equal))
                if m == 2:
                    V.tensor_tensor(OHB, M["cmb"], M["oh"], ALU.add).then_inc(S("f2.routed"), 1)
                    ranks(M)
                    sparse(M)
                for k, dst in ((0, M["cmb"]), (1, M["oh"])):
                    if M["gated"]:
                        link(V.tensor_tensor(dst, dst, M["gt"][:, :, k:k + 1].to_broadcast([P, T, E]), ALU.mult))
                V.tensor_tensor(M["cmb"], M["cmb"], M["oh"], ALU.add).then_inc(S(f"{ph}.cmb"), 1)
                if m == 3:
                    link(V.tensor_tensor(X[:], X[:], XN[:], ALU.add))
                for c in range(NC):
                    dve.wait_ge(*at(f"{ph}.bias_ps", TPC * (c + 1)))
                    xs = X[:, c * TPC:(c + 1) * TPC, :]
                    last = V.tensor_tensor(xs, xs, PS[:, 4 + c, :].rearrange("p (t d) -> p t d", t=TPC), ALU.add)
                last.then_inc(S(f"{ph}.acc"), 1)
                if m == 2:
                    combine(M)
                    return

                def pair(q):
                    for s in range(2 * NC):
                        b, c, n = s // NC, s % NC, q * 2 * NC + s
                        dve.wait_ge(*at(f"{ph}.y_ps", n + 1))
                        if isinstance(n, int) and n < NC:
                            dve.wait_ge(*at(f"{ph}.acc", 1))
                            dve.wait_ge(*at(f"{ph}.cmb", 1))
                        else:
                            dve.wait_ge(*at(f"{ph}.y", n - NC + 1))
                        for t in range(TPC):
                            tt = c * TPC + t
                            last = V.scalar_tensor_tensor(X[:, tt, :], PS[:, 4 + s % 2, t * P:(t + 1) * P], M["cmb"][:, tt, bass.ds(2 * q + b, 1)], X[:, tt, :], ALU.mult, ALU.add)
                        last.then_inc(S(f"{ph}.y"), 1)
                pair(0)
                with dve.Fori(1, E // 2) as q:
                    pair(q)
                dve.wait_ge(*at(f"{ph}.y", E * NC))
                V.tensor_copy(SMALL[:, 32:33], IDENT[:, 0:1]).then_inc(S("x_done"), 1)

            for g in (1, 2, 3):
                attention(g)
                moe(g)


def kernel(**inputs):
    import numpy as np
    import concourse.bacc as bacc
    from concourse.bass_utils import run_bass_kernel_spmd as run

    a = {k: np.asarray(v) for k, v in inputs.items()}
    lay = {
        "x": a["x"],
        "adjt": a["adj"].T,
        "w0cat": a["L0_gnn_weights"].transpose(1, 0, 2).reshape(D, D),
        "w0t": a["L0_gnn_weights"].transpose(2, 0, 1),
        "phi0": a["L0_gnn_phis"][:, :, 0].reshape(HEADS, 2, FH).transpose(2, 0, 1),
        "bias0": a["L0_gnn_biases"].reshape(D),
        "bias0t": a["L0_gnn_biases"].T,
        "g1_io": a["L1_gnn_W"], "g1_oi": a["L1_gnn_W"].T, "g1_a": a["L1_gnn_a"].reshape(2, D).T,
        "g2_io": a["L2_gnn_W"].T, "g2_oi": a["L2_gnn_W"], "g2_a": a["L2_gnn_a"].reshape(2, D).T,
        "g3_io": a["L3_gnn_W"].T, "g3_oi": a["L3_gnn_W"], "g3_a": a["L3_gnn_a_vec"].reshape(2, D).T,
        "g3_b": a["L3_gnn_b_W"], "g3_bc": a["L3_gnn_b_W"].reshape(D, 1), "g3_ba": a["L3_gnn_b_a"],
        "f0_wi": a["L0_ffn_Wi"].T, "f0_bi": a["L0_ffn_bi"],
        "f0_route": a["L0_ffn_route_id"],
        "f0_ws": a["L0_ffn_Ws"][:, 0].transpose(0, 2, 1).reshape(LAYERS, KH, P, HID),
        "f0_br": a["L0_ffn_br"], "f0_bs": a["L0_ffn_bs"],
        "f0_wr": a["L0_ffn_Wr"].transpose(0, 1, 3, 2).reshape(LAYERS, E0, KH, P, HID),
        "f0_wo": a["L0_ffn_Wo"].T.reshape(KH, P, D), "f0_bo": a["L0_ffn_bo"],
    }
    for m, (wg, bg, w1, b1, w2, b2) in ((1, ("Wg", "bg", "W1", "b1", "W2", "b2")), (2, ("Wr", "br", "W1", "b1", "W2", "b2")),
                                        (3, ("router_w", None, "w1", "b1", "w2", "b2"))):
        f = lambda name: a[f"L{m}_ffn_{name}"]
        E, _, H = f(w1).shape
        lay[f"f{m}_wg"] = f(wg).T if m == 3 else f(wg)
        if bg:
            lay[f"f{m}_bg"] = f(bg)
        b1t = f(b1).reshape(E, H // P, P).transpose(0, 2, 1)
        w2k = f(w2).reshape(E, H // P, P, D)
        if m == 2:
            lay["f2_w"] = np.concatenate([f(w1), b1t, w2k.transpose(0, 2, 1, 3).reshape(E, P, H // P * D)], axis=2)
        else:
            lay[f"f{m}_w1"], lay[f"f{m}_b1"], lay[f"f{m}_w2"] = f(w1), b1t, w2k
        lay[f"f{m}_b2"] = f(b2)

    nc = bacc.Bacc("TRN2", target_bir_lowering=False, num_devices=1)
    arrays, dram = {}, {}
    for name, v in lay.items():
        v = np.ascontiguousarray(v)
        arrays[f"in_{name}"] = v
        dram[name] = nc.dram_tensor(f"in_{name}", v.shape, mybir.dt.from_np(v.dtype), kind="ExternalInput").ap()
    out = nc.dram_tensor("out_0", (N, D), F32, kind="ExternalOutput").ap()
    build(nc, dram, out)
    r = run(nc, [arrays], core_ids=[0])
    return r.results[0]["out_0"]
```
